# Optimizing a Trainium2 kernel written in Bass

```python
import numpy as np
import jax
import jax.numpy as jnp

def _softmax(x, axis=-1):
    return jax.nn.softmax(x, axis=axis)

def _gelu(x):
    return jax.nn.gelu(x, approximate=True)

def _silu(x):
    return jax.nn.silu(x)

def _sigmoid(x):
    return jax.nn.sigmoid(x)

def _layernorm(x, axis=-1, eps=1e-05):
    m = jnp.mean(x, axis=axis, keepdims=True)
    v = jnp.var(x, axis=axis, keepdims=True)
    return (x - m) / jnp.sqrt(v + eps)

def _scatter_add(tgt, idx, src, axis=0):
    return tgt.at[idx].add(src)

def _segment_sum(src, seg, n):
    return jax.ops.segment_sum(src, seg, n)
kernel_name = 'mk_gnn_preln_d4_gnn_r64_d8da99'

def setup_inputs(seed: int=0):
    np.random.seed(seed)
    _w = jnp.asarray

    def _rec_inputs():
        import jax
        import jax.numpy as jnp
        _gk = jax.random.key(seed)
        x = -0.000202 + 1 * jax.random.normal(jax.random.fold_in(_gk, 1), (100000, 128), jnp.float32)
        src = jax.random.randint(jax.random.fold_in(_gk, 2), (25000,), 0, 100000, jnp.int32)
        dst = jnp.minimum((100000 * jax.random.uniform(jax.random.fold_in(_gk, 3), (25000,)) ** 2.0).astype(jnp.int32), 99999)
        _o = jnp.argsort(dst, stable=True)
        src = src[_o]
        dst = dst[_o]
        edge_attr_2 = -0.000414295 + 0.999828 * jax.random.normal(jax.random.fold_in(_gk, 11), (25000, 2), jnp.float32)
        edge_weight = jax.random.uniform(jax.random.fold_in(_gk, 13), (25000,), jnp.float32, 0.0, 0.999999)
        return (x, src, dst, edge_attr_2, edge_weight)
    x, src, dst, edge_attr_2, edge_weight = _rec_inputs()

    def _L0_gnn_setup():
        import jax, jax.numpy as jnp
        import numpy as np
        N_NODES = 50000
        N_EDGES = 25000
        D_FEAT = 128
        key = jax.random.key(seed)
        k1, k2, k3 = jax.random.split(key, 3)
        x = jax.random.normal(k1, (N_NODES, D_FEAT), dtype=jnp.float32)
        edge_index = jax.random.randint(k2, (2, N_EDGES), 0, N_NODES, dtype=jnp.int64)
        edge_attr = jax.random.uniform(k3, (N_EDGES,), dtype=jnp.float32)
        return {'x': x, 'edge_index': edge_index, 'edge_attr': edge_attr}
    _L0_gnn_all = _L0_gnn_setup()
    _L0_gnn_in = {k: v for k, v in _L0_gnn_all.items() if k in ()}
    del _L0_gnn_all

    def _L1_gnn_setup():
        import jax, jax.numpy as jnp
        import numpy as np
        N_NODES = 100000
        N_EDGES = 25000
        D_IN = 128
        D_HID = 128

        def _sage_conv(x, src, dst, W_l, W_r, b, num_nodes):
            msgs = x[src]
            agg = jax.ops.segment_sum(msgs, dst, num_segments=num_nodes)
            deg = jax.ops.segment_sum(jnp.ones((src.shape[0],), x.dtype), dst, num_segments=num_nodes)
            agg = agg / jnp.maximum(deg, 1.0)[:, None]
            return agg @ W_l.T + b + x @ W_r.T
        key = jax.random.key(seed)
        ks = jax.random.split(key, 8)
        s = 1.0 / np.sqrt(D_IN)
        return {'x': jax.random.normal(ks[0], (N_NODES, D_IN), dtype=jnp.float32), 'edge_index': jax.random.randint(ks[1], (2, N_EDGES), 0, N_NODES, dtype=jnp.int64), 'W1_l': jax.random.uniform(ks[2], (D_HID, D_IN), jnp.float32, -s, s), 'W1_r': jax.random.uniform(ks[3], (D_HID, D_IN), jnp.float32, -s, s), 'b1': jnp.zeros((D_HID,), jnp.float32), 'W2_l': jax.random.uniform(ks[4], (D_HID, D_HID), jnp.float32, -s, s), 'W2_r': jax.random.uniform(ks[5], (D_HID, D_HID), jnp.float32, -s, s), 'b2': jnp.zeros((D_HID,), jnp.float32)}
    _L1_gnn_all = _L1_gnn_setup()
    _L1_gnn_in = {k: v for k, v in _L1_gnn_all.items() if k in ('W1_l', 'W1_r', 'b1', 'W2_l', 'W2_r', 'b2')}
    del _L1_gnn_all

    def _L2_gnn_setup():
        import jax, jax.numpy as jnp
        import numpy as np
        N_NODES = 50000
        N_EDGES = 12500
        IN_DIM = 128
        OUT_DIM = 128
        EDGE_DIM = 2
        LN_EPS = 1e-05
        key = jax.random.key(seed)
        ks = jax.random.split(key, 8)
        s = lambda fan_in: 1.0 / np.sqrt(fan_in)
        x = jax.random.normal(ks[0], (N_NODES, IN_DIM), dtype=jnp.float32)
        edge_attr = jax.random.normal(ks[1], (N_EDGES, EDGE_DIM), dtype=jnp.float32)
        mW1 = jax.random.normal(ks[2], (2 * IN_DIM + EDGE_DIM, OUT_DIM), dtype=jnp.float32) * s(2 * IN_DIM + EDGE_DIM)
        mb1 = jnp.zeros((OUT_DIM,), jnp.float32)
        mW2 = jax.random.normal(ks[3], (OUT_DIM, OUT_DIM), dtype=jnp.float32) * s(OUT_DIM)
        mb2 = jnp.zeros((OUT_DIM,), jnp.float32)
        uW1 = jax.random.normal(ks[4], (IN_DIM + OUT_DIM, OUT_DIM), dtype=jnp.float32) * s(IN_DIM + OUT_DIM)
        ub1 = jnp.zeros((OUT_DIM,), jnp.float32)
        uW2 = jax.random.normal(ks[5], (OUT_DIM, OUT_DIM), dtype=jnp.float32) * s(OUT_DIM)
        ub2 = jnp.zeros((OUT_DIM,), jnp.float32)
        gamma = jnp.ones((OUT_DIM,), jnp.float32)
        beta = jnp.zeros((OUT_DIM,), jnp.float32)
        edge_index = jax.random.randint(ks[6], (2, N_EDGES), 0, N_NODES, dtype=jnp.int64 if jax.config.jax_enable_x64 else jnp.int32)
        return {'x': x, 'edge_attr': edge_attr, 'mW1': mW1, 'mb1': mb1, 'mW2': mW2, 'mb2': mb2, 'uW1': uW1, 'ub1': ub1, 'uW2': uW2, 'ub2': ub2, 'gamma': gamma, 'beta': beta, 'edge_index': edge_index}
    _L2_gnn_all = _L2_gnn_setup()
    _L2_gnn_in = {k: v for k, v in _L2_gnn_all.items() if k in ('mW1', 'mb1', 'mW2', 'mb2', 'uW1', 'ub1', 'uW2', 'ub2', 'gamma', 'beta')}
    del _L2_gnn_all

    def _L3_gnn_setup():
        import jax, jax.numpy as jnp
        import numpy as np
        N_NODES = 50000
        N_EDGES = 12500
        D = 128
        key = jax.random.key(seed)
        ks = jax.random.split(key, 6)
        x = jax.random.normal(ks[0], (N_NODES, D), dtype=jnp.float32)
        edge_index = jax.random.randint(ks[1], (2, N_EDGES), 0, N_NODES, dtype=jnp.int64)
        s = 1.0 / np.sqrt(D)
        W_self = jax.random.uniform(ks[2], (D, D), jnp.float32, -s, s)
        b_self = jax.random.uniform(ks[3], (D,), jnp.float32, -s, s)
        W_neighbor = jax.random.uniform(ks[4], (D, D), jnp.float32, -s, s)
        b_neighbor = jax.random.uniform(ks[5], (D,), jnp.float32, -s, s)
        return {'x': x, 'edge_index': edge_index, 'W_self': W_self, 'b_self': b_self, 'W_neighbor': W_neighbor, 'b_neighbor': b_neighbor}
    _L3_gnn_all = _L3_gnn_setup()
    _L3_gnn_in = {k: v for k, v in _L3_gnn_all.items() if k in ('W_self', 'b_self', 'W_neighbor', 'b_neighbor')}
    del _L3_gnn_all
    return {'x': x, 'src': src, 'dst': dst, 'edge_attr_2': edge_attr_2, 'edge_weight': edge_weight, 'L1_gnn_W1_l': _L1_gnn_in['W1_l'], 'L1_gnn_W1_r': _L1_gnn_in['W1_r'], 'L1_gnn_b1': _L1_gnn_in['b1'], 'L1_gnn_W2_l': _L1_gnn_in['W2_l'], 'L1_gnn_W2_r': _L1_gnn_in['W2_r'], 'L1_gnn_b2': _L1_gnn_in['b2'], 'L2_gnn_mW1': _L2_gnn_in['mW1'], 'L2_gnn_mb1': _L2_gnn_in['mb1'], 'L2_gnn_mW2': _L2_gnn_in['mW2'], 'L2_gnn_mb2': _L2_gnn_in['mb2'], 'L2_gnn_uW1': _L2_gnn_in['uW1'], 'L2_gnn_ub1': _L2_gnn_in['ub1'], 'L2_gnn_uW2': _L2_gnn_in['uW2'], 'L2_gnn_ub2': _L2_gnn_in['ub2'], 'L2_gnn_gamma': _L2_gnn_in['gamma'], 'L2_gnn_beta': _L2_gnn_in['beta'], 'L3_gnn_W_self': _L3_gnn_in['W_self'], 'L3_gnn_b_self': _L3_gnn_in['b_self'], 'L3_gnn_W_neighbor': _L3_gnn_in['W_neighbor'], 'L3_gnn_b_neighbor': _L3_gnn_in['b_neighbor']}

def reference(x, src, dst, edge_attr_2, edge_weight, L1_gnn_W1_l, L1_gnn_W1_r, L1_gnn_b1, L1_gnn_W2_l, L1_gnn_W2_r, L1_gnn_b2, L2_gnn_mW1, L2_gnn_mb1, L2_gnn_mW2, L2_gnn_mb2, L2_gnn_uW1, L2_gnn_ub1, L2_gnn_uW2, L2_gnn_ub2, L2_gnn_gamma, L2_gnn_beta, L3_gnn_W_self, L3_gnn_b_self, L3_gnn_W_neighbor, L3_gnn_b_neighbor):
    import jax
    import jax.numpy as jnp

    def _L0_gnn_ref(x, edge_index, edge_attr):
        import jax, jax.numpy as jnp
        import numpy as np
        N_NODES = 50000
        N_EDGES = 25000
        D_FEAT = 128
        row, col = (edge_index[0], edge_index[1])
        num_nodes = x.shape[0]
        deg = jax.ops.segment_sum(jnp.ones_like(edge_attr), row, num_segments=num_nodes)
        deg_inv_sqrt = jnp.where(deg > 0, deg ** (-0.5), 0.0)
        w = deg_inv_sqrt[row] * edge_attr * deg_inv_sqrt[col]
        w = jnp.where(row == col, 0.0, w)
        agg = jax.ops.segment_sum(w[:, None] * x[col], row, num_segments=num_nodes)
        out = agg + (deg_inv_sqrt * deg_inv_sqrt)[:, None] * x
        return out

    def _L1_gnn_ref(x, edge_index, W1_l, W1_r, b1, W2_l, W2_r, b2):
        import jax, jax.numpy as jnp
        import numpy as np
        N_NODES = 100000
        N_EDGES = 25000
        D_IN = 128
        D_HID = 128

        def _sage_conv(x, src, dst, W_l, W_r, b, num_nodes):
            msgs = x[src]
            agg = jax.ops.segment_sum(msgs, dst, num_segments=num_nodes)
            deg = jax.ops.segment_sum(jnp.ones((src.shape[0],), x.dtype), dst, num_segments=num_nodes)
            agg = agg / jnp.maximum(deg, 1.0)[:, None]
            return agg @ W_l.T + b + x @ W_r.T
        src, dst = (edge_index[0], edge_index[1])
        n = x.shape[0]
        h = jax.nn.relu(_sage_conv(x, src, dst, W1_l, W1_r, b1, n))
        h = jax.nn.relu(_sage_conv(h, src, dst, W2_l, W2_r, b2, n))
        return h

    def _L2_gnn_ref(x, edge_attr, mW1, mb1, mW2, mb2, uW1, ub1, uW2, ub2, gamma, beta, edge_index):
        import jax, jax.numpy as jnp
        import numpy as np
        N_NODES = 50000
        N_EDGES = 12500
        IN_DIM = 128
        OUT_DIM = 128
        EDGE_DIM = 2
        LN_EPS = 1e-05
        num_nodes = x.shape[0]
        src, dst = (edge_index[0], edge_index[1])
        msg_in = jnp.concatenate([x[src], x[dst], edge_attr], axis=-1)
        msgs = jnp.maximum(msg_in @ mW1 + mb1, 0.0) @ mW2 + mb2
        agg = jax.ops.segment_sum(msgs, dst, num_segments=num_nodes)
        cnt = jax.ops.segment_sum(jnp.ones((dst.shape[0],), x.dtype), dst, num_segments=num_nodes)
        agg = agg / jnp.clip(cnt, 1.0)[:, None]
        upd_in = jnp.concatenate([x, agg], axis=-1)
        upd = jnp.maximum(upd_in @ uW1 + ub1, 0.0) @ uW2 + ub2
        upd = upd + x
        mu = jnp.mean(upd, axis=-1, keepdims=True)
        var = jnp.mean(jnp.square(upd - mu), axis=-1, keepdims=True)
        return (upd - mu) * jax.lax.rsqrt(var + LN_EPS) * gamma + beta

    def _L3_gnn_ref(x, edge_index, W_self, b_self, W_neighbor, b_neighbor):
        import jax, jax.numpy as jnp
        import numpy as np
        N_NODES = 50000
        N_EDGES = 12500
        D = 128
        num_nodes = x.shape[0]
        src = edge_index[0]
        dst = edge_index[1]
        gathered = x[dst]
        seg_sum = jax.ops.segment_sum(gathered, src, num_segments=num_nodes)
        counts = jax.ops.segment_sum(jnp.ones_like(src, dtype=x.dtype), src, num_segments=num_nodes)
        mean = seg_sum / jnp.maximum(counts, 1.0)[:, None]
        x_self = x @ W_self.T + b_self
        neigh = mean @ W_neighbor.T + b_neighbor
        neigh = jnp.where((counts > 0)[:, None], neigh, 0.0)
        return jax.nn.relu(x_self + neigh)
    edge_index = jnp.stack([src, dst])
    h = jnp.maximum(_layernorm(x, axis=-1), 0.0)
    x = x + _L0_gnn_ref(h, edge_index, edge_weight)
    h = jnp.maximum(_layernorm(x, axis=-1), 0.0)
    x = x + _L1_gnn_ref(h, edge_index, L1_gnn_W1_l, L1_gnn_W1_r, L1_gnn_b1, L1_gnn_W2_l, L1_gnn_W2_r, L1_gnn_b2)
    h = jnp.maximum(_layernorm(x, axis=-1), 0.0)
    x = x + _L2_gnn_ref(h, edge_attr_2, L2_gnn_mW1, L2_gnn_mb1, L2_gnn_mW2, L2_gnn_mb2, L2_gnn_uW1, L2_gnn_ub1, L2_gnn_uW2, L2_gnn_ub2, L2_gnn_gamma, L2_gnn_beta, edge_index)
    h = jnp.maximum(_layernorm(x, axis=-1), 0.0)
    x = x + _L3_gnn_ref(h, edge_index, L3_gnn_W_self, L3_gnn_b_self, L3_gnn_W_neighbor, L3_gnn_b_neighbor)
    return x

_drawn_inputs = setup_inputs


def setup_inputs(seed=0):
    import zlib

    import numpy as np

    out = dict(_drawn_inputs(seed))
    spreads = {'L1_gnn_b1': (0.0, 0.295),
     'L1_gnn_b2': (0.0, 0.1),
     'L2_gnn_mb1': (0.0, 0.8),
     'L2_gnn_mb2': (0.0, 0.552),
     'L2_gnn_ub1': (0.0, 0.1),
     'L2_gnn_ub2': (0.0, 0.1),
     'L2_gnn_gamma': (1.0, 0.2),
     'L2_gnn_beta': (0.0, 0.1)}
    factors = {'edge_attr_2': 7.258, 'L3_gnn_b_self': 3.343, 'L3_gnn_b_neighbor': 6.151}
    for name, (base, spread) in spreads.items():
        noise = np.random.default_rng([zlib.crc32(name.encode()), seed]).standard_normal(out[name].shape)
        drawn = base * np.exp(spread * noise) if base else spread * noise
        out[name] = jnp.asarray(drawn.astype(out[name].dtype))
    for name, factor in factors.items():
        out[name] = (out[name] * factor).astype(out[name].dtype)
    return out
```

```python
import concourse.bass as bass
from concourse import mybir
from concourse.bass import DynSlice
from contextlib import ExitStack

F32, I32 = mybir.dt.float32, mybir.dt.int32
BF16, F16 = mybir.dt.bfloat16, mybir.dt.float16
ALU = mybir.AluOpType
ACT = mybir.ActivationFunctionType

N, E, D = 100000, 25000, 128
P = 128
T = 4
CH = P * T
NCH = -(-E // (2 * CH)) * 2
EP = NCH * CH
PAD = EP - E
HIQ = -(-(N + PAD) // (P * P))
NT = HIQ * P * P
DUMP = -(-(N + PAD) // P) * P
ZR = 9
R = -(-(DUMP + CH) // (P * ZR)) * P * ZR
G = 2
GD = 4
NBLK = -(-N // (CH * GD))
EPS = 1e-5

C_DIS, C_INVS, C_INVD, C_IND = range(4)
G_SRC, G_DST, G_SRC3, G_DSTC = range(4)
A_SRC3, A_DST3, A_DST, A_SRC = range(4)
F_KEYS, F_KEYD, F_W, F_INVD, F_INVS = range(5)


def stream_base(c):
    return c * (N - NBLK * CH) // (GD - 1)


def tiles(f):
    for t in range(T):
        last = f(t)
    return last


def counter(order):
    return lambda i, step, n=len(order): i * n + (order + ["end"]).index(step) + 1


def start(eng, *sems):
    for s in sems:
        eng.sem_inc(s, 1)


LN = ["stats", "mean_var", "std", "rstd", "shift", "norm"]


def ln(prefix):
    return [prefix + s for s in LN]


def wait_alone(eng, ticks, sem, value):
    eng.wait_ge(sem, value)
    eng.sem_inc(ticks, 1)


class Norm:

    def __init__(self, sb, name, ticks):
        self.ticks = ticks
        self.st = sb(name + "_stats", [P, T, 6], F32)
        self.mv = sb(name + "_mean_var", [P, T, 2], F32)
        self.sd = sb(name + "_std", [P, T], F32)
        self.rs = sb(name + "_rstd", [P, T], F32)
        self.sh = sb(name + "_shift", [P, T], F32)


def norm_vector_1(nc, dve, done, at, i, pre, b, x):
    dve.wait_ge(done, at(i, pre + "stats"))
    tiles(lambda t: nc.vector.bn_stats(b.st[:, t, :], x[:, t, :])).then_inc(done, 1)


def norm_vector_2(nc, dve, done, at, i, pre, b):
    wait_alone(dve, b.ticks, done, at(i, pre + "mean_var"))
    tiles(lambda t: nc.vector.bn_aggr(b.mv[:, t, :], b.st[:, t, :])).then_inc(done, 1)


def norm_vector_3(nc, dve, done, at, i, pre, b):
    dve.wait_ge(done, at(i, pre + "rstd"))
    nc.vector.reciprocal(b.rs[:, :], b.sd[:, :]).then_inc(done, 1)


def norm_vector_4(nc, dve, done, at, i, pre, b):
    dve.wait_ge(done, at(i, pre + "shift"))
    nc.vector.scalar_tensor_tensor(out=b.sh[:, :], in0=b.mv[:, :, 0], scalar=-1.0, in1=b.rs[:, :],
                                   op0=ALU.mult, op1=ALU.mult).then_inc(done, 1)


def norm_scalar_1(nc, act, done, at, i, pre, b, eps):
    act.wait_ge(done, at(i, pre + "std"))
    nc.scalar.activation(b.sd[:, :], b.mv[:, :, 1], ACT.Sqrt, bias=eps).then_inc(done, 1)


def norm_scalar_2(nc, act, done, at, i, pre, b, out, x, func):
    act.wait_ge(done, at(i, pre + "norm"))
    tiles(lambda t: nc.scalar.activation(out[:, t, :], x[:, t, :], func,
                                         bias=b.sh[:, t:t + 1], scale=b.rs[:, t:t + 1])).then_inc(done, 1)


def transpose4(nc, ps, x, ident):
    return tiles(lambda t: nc.tensor.transpose(ps[:, t * P:(t + 1) * P], x[:, t, :], ident))


def rows_matmul(nc, ps, pairs, bias=None):
    for t in range(T):
        o = ps[:, t * P:(t + 1) * P]
        for n, (xT, w) in enumerate(pairs):
            last = nc.tensor.matmul(o, xT[:, t * P:(t + 1) * P], w, start=(n == 0),
                                    stop=(bias is None and n == len(pairs) - 1))
        if bias is not None:
            last = nc.tensor.matmul(o, bias[0](t), bias[1], start=False, stop=True)
    return last


def combine_messages(nc, ps, same, msg):
    for a in range(T):
        for b in range(T):
            last = nc.tensor.matmul(ps[:, a * P:(a + 1) * P], same[:, b, a:CH:T], msg[:, b, :],
                                    start=(b == 0), stop=(b == T - 1))
    return last


class Tables:

    def __init__(self, nc):
        def dram(name, shape, dt):
            return nc.dram_tensor(name, shape, dt, kind="Internal").ap()
        self.node3 = dram("node3", (R, 3, D), F32)
        self.sum3 = dram("sum3", (R, D), F32)
        self.sum4 = dram("sum4", (R, D), F32)
        self.small = dram("small", (NT, 4), F32)
        self.ind = dram("ind", (NT,), BF16)
        self.src = dram("src_padded", (EP,), I32)
        self.dst = dram("dst_padded", (EP,), I32)
        self.ew = dram("ew_padded", (EP,), F32)
        self.ea = dram("ea_padded", (EP, 2), F32)
        self.rec_g = dram("rec_gather", (NCH, P, 16), I32)
        self.rec_a = dram("rec_add", (NCH, P, 16), I32)
        self.rec_f = dram("rec_float", (NCH, P, 20), F32)
        self.x1s = dram("x1_src", (NCH, P, T * D), F32)
        self.h1s = dram("h1_src", (NCH, P, T * D), F32)
        self.g1s = dram("g1_src", (NCH, P, T * D), F32)
        self.x2d = dram("x2_dst", (NCH, P, T * D), F32)
        self.h2d = dram("h2_dst", (NCH, P, T * D), F32)
        self.split = dram("bias_split", (6, 3, D), BF16)


class Consts:

    def __init__(self, sb, ticks):
        self.ticks = ticks
        self.ident = sb("ident", [P, P], F32)
        self.eps = sb("eps", [P, 1], F32)
        self.wT = sb("wT", [P, 6, D], F32)
        self.wD = sb("wD", [P, 6, D], F32)
        self.wC = sb("wC", [P, T, D], F32)
        self.bcol = sb("bcol", [P, 3], F32)
        self.brow = sb("brow", [P, 5, D], BF16)
        self.ones = sb("ones", [P, P], BF16)
        self.gamma = sb("gamma", [P, D], F32)
        self.beta = sb("beta", [P, D], F32)


def setup_phase(nc, k, tb, inp, hist):
    with ExitStack() as ctx:
        def sb(name, shape, dt):
            return ctx.enter_context(nc.sbuf_tensor(name, shape, dt))

        def sem(name):
            return ctx.enter_context(nc.semaphore(name))

        zero = sb("zero", [P, ZR * 2 * D], F32)
        padkey = sb("padkey", [1, PAD], I32)
        wraw = sb("wraw", [P, 6, D], F32)
        brows = sb("brows", [6, D], F32)
        bres = sb("bres", [6, 2, D], F32)
        bsplit = sb("bsplit", [6, 3, D], BF16)
        srcI = sb("srcI", [P, NCH, T], I32)
        dstI = sb("dstI", [P, NCH, T], I32)
        digit = sb("digit", [P, NCH, T], I32)
        parts = sb("parts", [P, NCH, 6 * T], F32)
        counts = sb("counts", [P, NCH, 2 * T], F32)
        spare = sb("spare", [P, NCH, T], F32)
        dup = sb("dup", [P, NCH, T], F32)
        lead = sb("lead", [P, NCH, T], F32)
        recg = sb("recg", [P, NCH, 16], I32)
        reca = sb("reca", [P, NCH, 16], I32)
        iota = sb("iota", [P, HIQ * P], F16)
        earlier = sb("earlier", [P, T, CH], BF16)
        zh = sb("zh", [P, 512], F16)
        part = [sb(f"part{c}", [P, 6 * T], F32) for c in range(G)]
        krow = [sb(f"krow{c}", [P, 2, CH], I32) for c in range(G)]
        hi = [sb(f"hi{c}", [P, 2, T, HIQ * P], F16) for c in range(G)]
        lo = [sb(f"lo{c}", [P, 2, T, P], F16) for c in range(G)]
        junk = [sb(f"junk{c}", [P, 2 * T, CH], BF16) for c in range(G)]
        prev = [sb(f"prev{c}", [P, 2 * T], F32) for c in range(G)]
        tps = ctx.enter_context(nc.psum_tensor("tps", [P, 2, 512], F32))

        zero_set, const_set, cleared, padded = sem("zero_set"), sem("const_set"), sem("cleared"), sem("padded")
        edges_in, weights_in, bias_in, split_out = sem("edges_in"), sem("weights_in"), sem("bias_in"), sem("split_out")
        split_in, recs_out = sem("split_in"), sem("recs_out")
        transposed, linked, weights_ready, memzero = sem("transposed"), sem("linked"), sem("weights_ready"), sem("memzero")
        keys_in = [sem(f"keys_in{c}") for c in range(G)]
        led = [sem(f"led{c}") for c in range(G)]
        counted = [sem(f"counted{c}") for c in range(G)]
        block = ctx.enter_context(nc.Block())
        order = ["pick", "onehots", "earlier", "keep"]
        at = counter(order)

        @block.gpsimd
        def _(pool):
            nc.gpsimd.memset(zero[:, :], 0.0).then_inc(zero_set, 1)
            nc.gpsimd.iota(padkey[:, :], pattern=[[1, PAD]], base=N, channel_multiplier=0).then_inc(zero_set, 1)
            nc.gpsimd.memset(k.ident[:, :], 0.0).then_inc(memzero, 1)
            nc.gpsimd.memset(earlier[:, :, :], 1.0).then_inc(memzero, 1)
            nc.gpsimd.memset(k.wC[:, :, :], 0.0).then_inc(memzero, 1)
            nc.gpsimd.memset(k.brow[:, :, :], 0.0).then_inc(memzero, 1)
            nc.gpsimd.memset(k.ones[:, :], 1.0)
            nc.gpsimd.memset(k.eps[:, :], EPS)
            nc.gpsimd.memset(zh[:, :], 0.0)
            nc.gpsimd.iota(iota[:, :], pattern=[[1, HIQ * P]], base=0, channel_multiplier=0,
                           allow_small_or_imprecise_dtypes=True)
            nc.gpsimd.iota(spare[:, :, :], pattern=[[0, NCH], [1, T]], base=DUMP, channel_multiplier=T,
                           allow_small_or_imprecise_dtypes=True)
            pool.wait_ge(memzero, 2)
            nc.gpsimd.affine_select(out=k.ident[:, :], in_=k.ident[:, :], compare_op=ALU.not_equal, fill=1.0,
                                    base=0, pattern=[[-1, P]], channel_multiplier=1)
            for t in range(T):
                last = nc.gpsimd.affine_select(out=earlier[:, t, :], in_=earlier[:, t, :], compare_op=ALU.is_gt,
                                               fill=0.0, base=t, pattern=[[-1, CH]], channel_multiplier=T)
            last.then_inc(const_set, 1)

        @block.sync
        def _(sp):
            sp.wait_ge(padded, 128)
            with sp.Fori(0, NCH // G) as i:
                for c in range(G):
                    sp.wait_ge(led[c], at(i, "pick"))
                    for n, key in enumerate((tb.src, tb.dst)):
                        row = key.rearrange("(c e) -> c e", e=CH)[DynSlice(i * G + c, 1), :]
                        sp.dma_start(krow[c][:, n, :], row.partition_broadcast(P)).then_inc(keys_in[c], 16)
            sp.wait_ge(linked, 9 + 10)
            sp.dma_start(tb.rec_g.rearrange("c p k -> p c k"), recg[:, :, :]).then_inc(recs_out, 16)
            sp.dma_start(tb.rec_a.rearrange("c p k -> p c k"), reca[:, :, :]).then_inc(recs_out, 16)
            sp.wait_ge(recs_out, 32)

        @block.scalar
        def _(act):
            act.wait_ge(zero_set, 2)
            z = zero[0:1, :]
            act.dma_start(tb.src[0:E], inp["src"]).then_inc(padded, 16)
            act.dma_start(tb.dst[0:E], inp["dst"]).then_inc(padded, 16)
            act.dma_start(tb.ew[0:E], inp["edge_weight"]).then_inc(padded, 16)
            act.dma_start(tb.ea[0:E, :], inp["edge_attr_2"]).then_inc(padded, 16)
            act.dma_start(tb.src[E:EP].unsqueeze(0), padkey[:, :]).then_inc(padded, 16)
            act.dma_start(tb.dst[E:EP].unsqueeze(0), padkey[:, :]).then_inc(padded, 16)
            act.dma_start(tb.ew[E:EP].unsqueeze(0), z[:, 0:PAD]).then_inc(padded, 16)
            act.dma_start(tb.ea[E:EP, :].rearrange("e k -> (e k)").unsqueeze(0), z[:, 0:2 * PAD]).then_inc(padded, 16)
            for n, name in enumerate(("L1_gnn_W1_l", "L1_gnn_W1_r", "L1_gnn_W2_l", "L1_gnn_W2_r",
                                      "L3_gnn_W_self", "L3_gnn_W_neighbor")):
                act.dma_start(wraw[:, n, :], inp[name]).then_inc(weights_in, 16)
            for n, name in enumerate(("L1_gnn_b1", "L1_gnn_b2", "L2_gnn_mb2", "L2_gnn_ub2",
                                      "L3_gnn_b_self", "L3_gnn_b_neighbor")):
                act.dma_start(brows[n:n + 1, :], inp[name].unsqueeze(0)).then_inc(bias_in, 16)
            act.wait_ge(padded, 128)
            act.dma_start(srcI[:, :, :], tb.src.rearrange("(c p t) -> p c t", p=P, t=T)).then_inc(edges_in, 16)
            act.dma_start(dstI[:, :, :], tb.dst.rearrange("(c p t) -> p c t", p=P, t=T)).then_inc(edges_in, 16)
            m = inp["L2_gnn_mW1"]
            u = inp["L2_gnn_uW1"]
            for n, w in enumerate((m[0:D, :], m[D:2 * D, :], inp["L2_gnn_mW2"], u[0:D, :], u[D:2 * D, :],
                                   inp["L2_gnn_uW2"])):
                act.dma_start(k.wD[:, n, :], w).then_inc(weights_in, 16)
            for n, name in enumerate(("L1_gnn_b1", "L2_gnn_mb1", "L2_gnn_ub1")):
                act.dma_start(k.bcol[:, n:n + 1], inp[name].unsqueeze(1)).then_inc(weights_in, 16)
            act.dma_start(k.gamma[:, :], inp["L2_gnn_gamma"].partition_broadcast(P)).then_inc(weights_in, 16)
            act.dma_start(k.beta[:, :], inp["L2_gnn_beta"].partition_broadcast(P)).then_inc(weights_in, 16)
            act.wait_ge(memzero, 4)
            for t in range(T):
                act.dma_start(k.wC[2 * t:2 * t + 2, t, :], m[2 * D:2 * D + 2, :]).then_inc(weights_in, 16)
            rows3 = tb.node3.rearrange("(p b) k f -> p b k f", p=P)
            rows1 = [s.rearrange("(p b) f -> p b f", p=P) for s in (tb.sum3, tb.sum4)]
            z2 = zero[:, :].rearrange("p (b k f) -> p b k f", b=ZR, k=2)
            z1 = zero[:, 0:ZR * D].rearrange("p (b f) -> p b f", b=ZR)
            act.dma_start(tb.node3[N:R, 0, :].rearrange("(p b) f -> p b f", p=32),
                          zero[0:32, 0:D].unsqueeze(1).to_broadcast([32, (R - N) // 32, D])).then_inc(cleared, 16)
            with act.Fori(0, R // P // ZR) as i:
                act.dma_start(rows3[:, DynSlice(i * ZR, ZR), 1:3, :], z2).then_inc(cleared, 16)
                for r in rows1:
                    act.dma_start(r[:, DynSlice(i * ZR, ZR), :], z1).then_inc(cleared, 16)
            act.wait_ge(split_out, 1)
            act.dma_start(tb.split, bsplit[:, :, :]).then_inc(split_in, 16)
            act.wait_ge(split_in, 16)
            act.dma_start(k.brow[0:3, :, :], tb.split[0:5].rearrange("b s f -> s b f")).then_inc(split_in, 16)
            act.dma_start(k.brow[3:6, 4, :], tb.split[5]).then_inc(split_in, 16)
            act.wait_ge(split_in, 48)
            act.wait_ge(weights_in, 16 * (6 + 6 + 3 + 2 + T))
            act.wait_ge(cleared, 16 * (3 * (R // P // ZR) + 1))

        @block.vector
        def _(dve):
            start(dve, *led, *counted)
            links = [0]

            def link(ins):
                links[0] += 1
                ins.then_inc(linked, 1)
                dve.wait_ge(linked, links[0])

            dve.wait_ge(edges_in, 32)
            for n, key in enumerate((srcI, dstI)):
                a = 2 * n * T
                link(nc.vector.tensor_scalar(digit[:, :, :], key[:, :, :], 7, None, ALU.arith_shift_right))
                link(nc.vector.tensor_copy(parts[:, :, a:a + T], digit[:, :, :]))
                link(nc.vector.tensor_scalar(digit[:, :, :], key[:, :, :], P - 1, None, ALU.bitwise_and))
                nc.vector.tensor_copy(parts[:, :, a + T:a + 2 * T], digit[:, :, :])
                link(nc.vector.tensor_copy(parts[:, :, (4 + n) * T:(5 + n) * T], key[:, :, :]))
            assert links[0] == 8
            dve.wait_ge(const_set, 1)
            with dve.Fori(0, NCH // G) as i:
                for c in range(G):
                    dve.wait_ge(led[c], at(i, "pick"))
                    dve.wait_ge(counted[c], i + 1)
                    nc.vector.tensor_copy(part[c][:, :].unsqueeze(1), parts[:, DynSlice(i * G + c, 1), :]).then_inc(led[c], 1)
                for c in range(G):
                    dve.wait_ge(led[c], at(i, "onehots"))
                    for n in range(2):
                        for t in range(T):
                            a = 2 * n * T + t
                            nc.vector.tensor_scalar(hi[c][:, n, t, :], iota[:, :], part[c][:, a:a + 1], None, ALU.is_equal)
                            last = nc.vector.tensor_scalar(lo[c][:, n, t, :], iota[:, 0:P], part[c][:, a + T:a + T + 1],
                                                           None, ALU.is_equal)
                    last.then_inc(led[c], 1)
                for c in range(G):
                    dve.wait_ge(keys_in[c], (i + 1) * 32)
                    dve.wait_ge(led[c], at(i, "earlier"))
                    for n in range(2):
                        for t in range(T):
                            last = nc.vector.scalar_tensor_tensor(
                                out=junk[c][:, n * T + t, :], in0=krow[c][:, n, :],
                                scalar=part[c][:, (4 + n) * T + t:(4 + n) * T + t + 1], in1=earlier[:, t, :],
                                op0=ALU.is_equal, op1=ALU.mult, accum_out=prev[c][:, n * T + t:n * T + t + 1])
                    last.then_inc(led[c], 1)
                for c in range(G):
                    dve.wait_ge(led[c], at(i, "keep"))
                    nc.vector.tensor_copy(counts[:, DynSlice(i * G + c, 1), :], prev[c][:, :].unsqueeze(1)).then_inc(led[c], 1)
            for c in range(G):
                dve.wait_ge(led[c], at(NCH // G, "pick"))
            for n, (src, a, b) in enumerate(((srcI, 0.0, 1.0), (dstI, 0.0, 1.0), (srcI, 0.0, 3.0))):
                nc.vector.tensor_scalar(recg[:, :, n * T:(n + 1) * T], src[:, :, :], b, None, ALU.mult)
            link(nc.vector.tensor_scalar(recg[:, :, G_DSTC * T:(G_DSTC + 1) * T], dstI[:, :, :], float(N - 1), None, ALU.min))
            for n, (one, three) in enumerate(((A_SRC, A_SRC3), (A_DST, A_DST3))):
                key = parts[:, :, (4 + n) * T:(5 + n) * T]
                link(nc.vector.tensor_scalar(dup[:, :, :], counts[:, :, n * T:(n + 1) * T], 0.0, None, ALU.is_gt))
                link(nc.vector.tensor_tensor(lead[:, :, :], spare[:, :, :], key, ALU.subtract))
                link(nc.vector.tensor_tensor(dup[:, :, :], dup[:, :, :], lead[:, :, :], ALU.mult))
                link(nc.vector.tensor_tensor(lead[:, :, :], dup[:, :, :], key, ALU.add))
                nc.vector.tensor_copy(reca[:, :, one * T:(one + 1) * T], lead[:, :, :])
                link(nc.vector.tensor_scalar(reca[:, :, three * T:(three + 1) * T], lead[:, :, :], 3.0, None, ALU.mult))
            assert links[0] == 9 + 10
            dve.wait_ge(bias_in, 96)
            link(nc.vector.tensor_copy(bsplit[:, 0, :], brows[:, :]))
            link(nc.vector.tensor_tensor(bres[:, 0, :], brows[:, :], bsplit[:, 0, :], ALU.subtract))
            link(nc.vector.tensor_copy(bsplit[:, 1, :], bres[:, 0, :]))
            link(nc.vector.tensor_tensor(bres[:, 1, :], bres[:, 0, :], bsplit[:, 1, :], ALU.subtract))
            nc.vector.tensor_copy(bsplit[:, 2, :], bres[:, 1, :]).then_inc(split_out, 1)
            dve.wait_ge(transposed, 1)
            nc.vector.tensor_copy(k.wT[:, 0:4, :], tps[:, 0, :].rearrange("p (n f) -> p n f", f=D))
            nc.vector.tensor_copy(k.wT[:, 4:6, :], tps[:, 1, 0:2 * D].rearrange("p (n f) -> p n f", f=D)).then_inc(weights_ready, 1)

        @block.tensor
        def _(pe):
            pe.wait_ge(const_set, 1)
            pe.wait_ge(weights_in, 16 * (6 + 6 + 3 + 2 + T))
            for n in range(6):
                last = nc.tensor.transpose(tps[:, n // 4, n % 4 * D:(n % 4 + 1) * D], wraw[:, n, :], k.ident[:, :])
            last.then_inc(transposed, 1)
            for n in range(2):
                for b in range(2):
                    nc.tensor.matmul(hist[:, n, b * 512:(b + 1) * 512], zh[:, 0:P], zh[:, :], start=True, stop=False,
                                     skip_group_check=True)
            with pe.Fori(0, NCH // G) as i:
                for c in range(G):
                    pe.wait_ge(led[c], at(i, "earlier"))
                    for n in range(2):
                        for t in range(T):
                            for q in range(HIQ):
                                last = nc.tensor.matmul(hist[:, n, q * P:(q + 1) * P], hi[c][:, n, t, q * P:(q + 1) * P],
                                                        lo[c][:, n, t, :], start=False, stop=False, skip_group_check=True)
                    last.then_inc(counted[c], 1)


def small_table_phase(nc, tb, hist):
    with ExitStack() as ctx:
        def sb(name, shape, dt):
            return ctx.enter_context(nc.sbuf_tensor(name, shape, dt))
        W = HIQ * P
        val = sb("val", [P, W, 4], F32)
        atl = sb("atl", [P, 2, W], F32)
        root = sb("root", [P, W], F32)
        rroot = sb("rroot", [P, W], F32)
        indb = sb("indb", [P, W], BF16)
        step = ctx.enter_context(nc.semaphore("table_step"))
        stored = ctx.enter_context(nc.semaphore("table_stored"))
        block = ctx.enter_context(nc.Block())

        @block.vector
        def _(dve):
            nc.vector.tensor_scalar(val[:, :, C_IND], hist[:, 0, 0:W], 0.0, None, ALU.is_gt)
            nc.vector.tensor_scalar(indb[:, :], hist[:, 0, 0:W], 0.0, None, ALU.is_gt)
            nc.vector.tensor_scalar(atl[:, 1, :], hist[:, 1, 0:W], 1.0, None, ALU.max)
            nc.vector.tensor_scalar(atl[:, 0, :], hist[:, 0, 0:W], 1.0, None, ALU.max).then_inc(step, 1)
            dve.wait_ge(step, 2)
            nc.vector.reciprocal(val[:, :, C_INVS], atl[:, 0, :])
            nc.vector.reciprocal(val[:, :, C_INVD], atl[:, 1, :])
            nc.vector.reciprocal(rroot[:, :], root[:, :]).then_inc(step, 1)
            dve.wait_ge(step, 3)
            nc.vector.tensor_tensor(val[:, :, C_DIS], rroot[:, :], val[:, :, C_IND], ALU.mult).then_inc(step, 1)

        @block.scalar
        def _(act):
            act.wait_ge(step, 1)
            nc.scalar.activation(root[:, :], atl[:, 0, :], ACT.Sqrt).then_inc(step, 1)
            act.wait_ge(step, 4)
            act.dma_start(tb.small.rearrange("(q h l) k -> h q (l k)", h=P, l=P),
                          val[:, :, :].rearrange("h (q l) k -> h q (l k)", l=P)).then_inc(stored, 16)
            act.dma_start(tb.ind.rearrange("(q h l) -> h q l", h=P, l=P),
                          indb[:, :].rearrange("h (q l) -> h q l", l=P)).then_inc(stored, 16)
            act.wait_ge(stored, 32)


def gather(pool, out, table, idx, t, signal, offset=0, bound=None):
    pool.indirect_dma_start(out, None, table, bass.IndirectOffsetOnAxis(ap=idx[:, t:t + 1], axis=0),
                            element_offset=offset).then_inc(signal, 16)


def add_rows(pool, table, rows, idx, signal, offset=0):
    for t in range(T):
        pool.indirect_dma_start(table, bass.IndirectOffsetOnAxis(ap=idx[:, t:t + 1], axis=0), rows[:, t, :], None,
                                element_offset=offset, compute_op=ALU.add).then_inc(signal, 16)


def first_rows_phase(nc, k, tb, inp):
    ROUNDS = NBLK
    with ExitStack() as ctx:
        sb, sem, _ = phase_tools(ctx, nc, "first")
        C = range(GD)
        x = [sb(f"x{c}", [P, T, D], F32) for c in C]
        h = [sb(f"h{c}", [P, T, D], F32) for c in C]
        y = [sb(f"y{c}", [P, T, D], F32) for c in C]
        deg = [sb(f"deg{c}", [P, T, 4], F32) for c in C]
        dis2 = [sb(f"dis2{c}", [P, T], F32) for c in C]
        b = [Norm(sb, f"n{c}", k.ticks) for c in C]
        loaded = [sem(f"loaded{c}") for c in C]
        stored = [sem(f"stored{c}") for c in C]
        done = [sem(f"done{c}") for c in C]
        L = range(G)
        idx = [sb(f"idx{c}", [P, 16], I32) for c in L]
        srci = [sb(f"srci{c}", [P, T], I32) for c in L]
        ew = [sb(f"ew{c}", [P, T], F32) for c in L]
        ends = [sb(f"ends{c}", [P, 2, T, 4], F32) for c in L]
        rec = [sb(f"rec{c}", [P, 5, T], F32) for c in L]
        neq = [sb(f"neq{c}", [P, T], F32) for c in L]
        prod = [sb(f"prod{c}", [P, 2, T], F32) for c in L]
        idx_in = [sem(f"idx_in{c}") for c in L]
        ends_in = [sem(f"ends_in{c}") for c in L]
        weighed = [sem(f"weighed{c}") for c in L]
        rec_out = [sem(f"rec_out{c}") for c in L]
        block = ctx.enter_context(nc.Block())
        order = ln("x_") + ["square", "first"]
        at = counter(order)
        worder = ["mask", "mask2", "dis", "final"]
        wat = counter(worder)
        EDGE_ROUNDS = NCH // G

        @block.sync
        def _(sp):
            def node_rows(i):
                for c in C:
                    rows = DynSlice(i * CH + stream_base(c), CH)
                    sp.wait_ge(done[c], at(i, "x_stats"))
                    sp.dma_start(x[c][:, :, :], inp["x"][rows, :].rearrange("(p t) f -> p t f", t=T)).then_inc(loaded[c], 16)
                    sp.dma_start(deg[c][:, :, :], tb.small[rows, :].rearrange("(p t) k -> p t k", t=T)).then_inc(loaded[c], 16)
                for c in C:
                    rows = DynSlice(i * CH + stream_base(c), CH)
                    sp.wait_ge(done[c], at(i + 1, "x_stats"))
                    sp.dma_start(tb.node3[rows, 0, :].rearrange("(p t) f -> p t f", t=T), y[c][:, :, :]).then_inc(stored[c], 16)

            with sp.Fori(0, EDGE_ROUNDS) as i:
                node_rows(i)
                for c in L:
                    sp.wait_ge(weighed[c], wat(i + 1, "mask"))
                    sp.dma_start(tb.rec_f[DynSlice(i * G + c, 1)].rearrange("c p k -> p c k"),
                                 rec[c][:, :, :].rearrange("p a t -> p (a t)").unsqueeze(1)).then_inc(rec_out[c], 16)
            with sp.Fori(EDGE_ROUNDS, ROUNDS) as i:
                node_rows(i)
            for c in C:
                sp.wait_ge(stored[c], ROUNDS * 16 + 1)
            for c in L:
                sp.wait_ge(rec_out[c], EDGE_ROUNDS * 16 + 1)

        @block.gpsimd
        def _(pool):
            with pool.Fori(0, EDGE_ROUNDS) as i:
                for c in L:
                    pool.wait_ge(weighed[c], wat(i, "mask"))
                    pool.dma_start(idx[c][:, :].unsqueeze(1), tb.rec_g[DynSlice(i * G + c, 1)].rearrange("c p k -> p c k")).then_inc(idx_in[c], 16)
                    pool.dma_start(ew[c][:, :].unsqueeze(1), tb.ew.rearrange("(c p t) -> p c t", p=P, t=T)[:, DynSlice(i * G + c, 1), :]).then_inc(idx_in[c], 16)
                for c in L:
                    wait_alone(pool, k.ticks, idx_in[c], (i + 1) * 32)
                    for n in range(2):
                        for t in range(T):
                            gather(pool, ends[c][:, n, t, :], tb.small, idx[c], n * T + t, ends_in[c])

        @block.vector
        def _(dve):
            start(dve, *done, *stored, *weighed, *rec_out)

            def edge_weights(i, c):
                dve.wait_ge(rec_out[c], i * 16 + 1)
                dve.wait_ge(ends_in[c], (i + 1) * 2 * T * 16)
                nc.vector.tensor_copy(rec[c][:, F_KEYS:F_KEYS + 2, :].rearrange("p a t -> p (a t)"), idx[c][:, 0:2 * T])
                nc.vector.tensor_copy(rec[c][:, F_INVD, :], ends[c][:, 1, :, C_INVD])
                nc.vector.tensor_copy(rec[c][:, F_INVS, :], ends[c][:, 0, :, C_INVS])
                nc.vector.tensor_tensor(prod[c][:, 0, :], ends[c][:, 0, :, C_DIS], ew[c][:, :], ALU.mult).then_inc(weighed[c], 1)
                dve.wait_ge(weighed[c], wat(i, "mask2"))
                nc.vector.tensor_tensor(neq[c][:, :], rec[c][:, F_KEYS, :], rec[c][:, F_KEYD, :], ALU.not_equal).then_inc(weighed[c], 1)
                dve.wait_ge(weighed[c], wat(i, "dis"))
                nc.vector.tensor_tensor(prod[c][:, 1, :], prod[c][:, 0, :], ends[c][:, 1, :, C_DIS], ALU.mult).then_inc(weighed[c], 1)
                dve.wait_ge(weighed[c], wat(i, "final"))
                nc.vector.tensor_tensor(rec[c][:, F_W, :], prod[c][:, 1, :], neq[c][:, :], ALU.mult).then_inc(weighed[c], 1)

            def node_rows(i):
                for c in C:
                    dve.wait_ge(loaded[c], (i + 1) * 32)
                    norm_vector_1(nc, dve, done[c], at, i, "x_", b[c], x[c])
                for c in C:
                    norm_vector_2(nc, dve, done[c], at, i, "x_", b[c])
                for c in C:
                    norm_vector_3(nc, dve, done[c], at, i, "x_", b[c])
                for c in C:
                    norm_vector_4(nc, dve, done[c], at, i, "x_", b[c])
                for c in C:
                    dve.wait_ge(done[c], at(i, "square"))
                    nc.vector.tensor_tensor(dis2[c][:, :], deg[c][:, :, C_DIS], deg[c][:, :, C_DIS], ALU.mult).then_inc(done[c], 1)
                for c in C:
                    dve.wait_ge(stored[c], i * 16 + 1)
                    dve.wait_ge(done[c], at(i, "first"))
                    tiles(lambda t: nc.vector.scalar_tensor_tensor(
                        out=y[c][:, t, :], in0=h[c][:, t, :], scalar=dis2[c][:, t:t + 1], in1=x[c][:, t, :],
                        op0=ALU.mult, op1=ALU.add)).then_inc(done[c], 1)

            with dve.Fori(0, EDGE_ROUNDS) as i:
                node_rows(i)
                for c in L:
                    edge_weights(i, c)
            with dve.Fori(EDGE_ROUNDS, ROUNDS) as i:
                node_rows(i)

        @block.scalar
        def _(act):
            with act.Fori(0, ROUNDS) as i:
                for c in C:
                    norm_scalar_1(nc, act, done[c], at, i, "x_", b[c], k.eps[:, :])
                for c in C:
                    norm_scalar_2(nc, act, done[c], at, i, "x_", b[c], h[c], x[c], ACT.Relu)


class EdgeSide:

    def __init__(self, ctx, nc, sb, sem, rows=1):
        L = range(G)
        self.gidx = [sb(f"gidx{c}", [P, 16], I32) for c in L]
        self.aidx = [sb(f"aidx{c}", [P, 16], I32) for c in L]
        self.rec = [sb(f"erec{c}", [P, 5, T], F32) for c in L]
        self.krow = [sb(f"ekrow{c}", [P, CH], I32) for c in L]
        self.same = [sb(f"same{c}", [P, T, CH], F32) for c in L]
        self.comb = [sb(f"comb{c}", [P, T, D], F32) for c in L]
        self.gidx_in = [sem(f"gidx_in{c}") for c in L]
        self.aidx_in = [sem(f"aidx_in{c}") for c in L]
        self.rec_in = [sem(f"rec_in{c}") for c in L]
        self.gathered = [sem(f"gathered{c}") for c in L]
        self.done = [sem(f"edone{c}") for c in L]
        self.summed = sem("summed")
        self.turns = sem("turns")


def load_gather_rows(sp, e, tb, i, c):
    sp.dma_start(e.gidx[c][:, :].unsqueeze(1), tb.rec_g[DynSlice(i * G + c, 1)].rearrange("c p k -> p c k")).then_inc(e.gidx_in[c], 16)


def load_records(sp, e, tb, key, i, c):
    sp.dma_start(e.rec[c][:, :, :].rearrange("p a t -> p (a t)").unsqueeze(1),
                 tb.rec_f[DynSlice(i * G + c, 1)].rearrange("c p k -> p c k")).then_inc(e.rec_in[c], 16)
    sp.dma_start(e.krow[c][:, :], key.rearrange("(c e) -> c e", e=CH)[DynSlice(i * G + c, 1), :].partition_broadcast(P)).then_inc(e.rec_in[c], 16)


def match_keys(nc, dve, e, at, i, c, key, weight):
    dve.wait_ge(e.rec_in[c], (i + 1) * 32)
    dve.wait_ge(e.done[c], at(i, "match"))
    tiles(lambda b: nc.vector.tensor_scalar(e.same[c][:, b, :], e.krow[c][:, :], e.rec[c][:, key, b:b + 1],
                                            e.rec[c][:, weight, b:b + 1], ALU.is_equal, ALU.mult)).then_inc(e.done[c], 1)


def keep_sums(nc, act, e, tb, at, i, c, ps):
    act.wait_ge(e.turns, i * G + c + 1)
    act.dma_start(e.aidx[c][:, :].unsqueeze(1), tb.rec_a[DynSlice(i * G + c, 1)].rearrange("c p k -> p c k")).then_inc(e.aidx_in[c], 16)
    act.wait_ge(e.done[c], at(i, "keep"))
    nc.scalar.activation(e.comb[c][:, :, :].rearrange("p t f -> p (t f)"), ps[:, :], ACT.Copy).then_inc(e.done[c], 1)


def pool_program(pool, ticks, e, at, rounds, gathers, free, table, group, offset):
    def fetch(i, c):
        wait_alone(pool, ticks, e.gidx_in[c], (i + 1) * 16)
        gathers(c)

    def add(i, c):
        pool.wait_ge(e.aidx_in[c], (i + 1) * 16)
        pool.wait_ge(e.done[c], at(i, "end"))
        if not (isinstance(i, int) and i * G + c == 0):
            pool.wait_ge(e.summed, (i * G + c) * T * 16)
        pool.sem_inc(e.turns, 1)
        add_rows(pool, table, e.comb[c], e.aidx[c][:, group * T:(group + 1) * T], e.summed, offset)

    for c in range(G):
        fetch(0, c)

    def both(i):
        for c in range(G):
            free(i, c)
            fetch(i + 1, c)
            add(i, c)
    both(0)
    with pool.Fori(1, rounds - 1) as i:
        both(i)
    for c in range(G):
        add(rounds - 1, c)
    pool.wait_ge(e.summed, rounds * G * T * 16)


def phase_tools(ctx, nc, phase):
    def sb(name, shape, dt):
        return ctx.enter_context(nc.sbuf_tensor(f"{phase}_{name}", shape, dt))

    def sem(name):
        return ctx.enter_context(nc.semaphore(f"{phase}_{name}"))

    def banks(name, n):
        return [ctx.enter_context(nc.psum_tensor(f"{phase}_{name}{c}", [P, 512], F32)) for c in range(n)]
    return sb, sem, banks


def chunk_rows(table, i, c):
    return table[DynSlice(i * G + c, 1)].rearrange("c p f -> p c f")


def flat(x):
    return x.rearrange("p t f -> p (t f)")


def gcn_phase(nc, k, tb, inp, first):
    with ExitStack() as ctx:
        sb, sem, banks = phase_tools(ctx, nc, "gcn" if first else "sage1")
        L = range(G)
        e = EdgeSide(ctx, nc, sb, sem)
        x = [sb(f"x{c}", [P, T, D], F32) for c in L]
        h = [sb(f"h{c}", [P, T, D], F32) for c in L]
        b = [Norm(sb, f"n{c}", k.ticks) for c in L]
        kept = [sem(f"kept{c}") for c in L]
        ps = banks("sums", G)
        block = ctx.enter_context(nc.Block())
        order = ln("x_") + ["match", "combine", "keep"]
        at = counter(order)
        RD = NCH // G
        key, weight, target, offset, krow, group = (F_KEYS, F_W, A_SRC3, 0, tb.src, G_DSTC) if first else \
            (F_KEYD, F_INVD, A_DST3, D, tb.dst, G_SRC3)
        rows3 = tb.node3.rearrange("r k f -> (r k) f")
        source = inp["x"] if first else rows3

        @block.sync
        def _(sp):
            for c in L:
                load_gather_rows(sp, e, tb, 0, c)
                load_records(sp, e, tb, krow, 0, c)

            def keep_rows(i, c):
                sp.wait_ge(e.done[c], at(i, "match"))
                sp.dma_start(chunk_rows(tb.x1s, i, c), flat(x[c][:, :, :]).unsqueeze(1)).then_inc(kept[c], 16)
                sp.dma_start(chunk_rows(tb.h1s, i, c), flat(h[c][:, :, :]).unsqueeze(1)).then_inc(kept[c], 16)

            with sp.Fori(0, RD - 1) as i:
                for c in L:
                    sp.wait_ge(e.gathered[c], (i + 1) * T * 16)
                    load_gather_rows(sp, e, tb, i + 1, c)
                if not first:
                    for c in L:
                        keep_rows(i, c)
                for c in L:
                    sp.wait_ge(e.done[c], at(i, "combine"))
                    load_records(sp, e, tb, krow, i + 1, c)
            if not first:
                for c in L:
                    keep_rows(RD - 1, c)
                for c in L:
                    sp.wait_ge(kept[c], RD * 32 + 1)

        @block.gpsimd
        def _(pool):
            def gathers(c):
                for t in range(T):
                    gather(pool, x[c][:, t, :], source, e.gidx[c], group * T + t, e.gathered[c])

            def free(i, c):
                pool.wait_ge(e.done[c], at(i, "match"))
                if not first:
                    pool.wait_ge(kept[c], (i + 1) * 32 + 1)
            pool_program(pool, k.ticks, e, at, RD, gathers, free, rows3, target, offset)

        @block.vector
        def _(dve):
            start(dve, *e.done, e.turns, *kept)

            with dve.Fori(0, RD) as i:
                for c in L:
                    dve.wait_ge(e.gathered[c], (i + 1) * T * 16)
                    norm_vector_1(nc, dve, e.done[c], at, i, "x_", b[c], x[c])
                for c in L:
                    norm_vector_2(nc, dve, e.done[c], at, i, "x_", b[c])
                for c in L:
                    norm_vector_3(nc, dve, e.done[c], at, i, "x_", b[c])
                for c in L:
                    norm_vector_4(nc, dve, e.done[c], at, i, "x_", b[c])
                for c in L:
                    match_keys(nc, dve, e, at, i, c, key, weight)

        @block.scalar
        def _(act):
            with act.Fori(0, RD) as i:
                for c in L:
                    norm_scalar_1(nc, act, e.done[c], at, i, "x_", b[c], k.eps[:, :])
                for c in L:
                    if not first:
                        act.wait_ge(kept[c], i * 32 + 1)
                    norm_scalar_2(nc, act, e.done[c], at, i, "x_", b[c], h[c], x[c], ACT.Relu)
                for c in L:
                    keep_sums(nc, act, e, tb, at, i, c, ps[c])

        @block.tensor
        def _(pe):
            with pe.Fori(0, RD) as i:
                for c in L:
                    pe.wait_ge(e.done[c], at(i, "combine"))
                    combine_messages(nc, ps[c], e.same[c], h[c]).then_inc(e.done[c], 1)


def sage2_phase(nc, k, tb):
    with ExitStack() as ctx:
        sb, sem, banks = phase_tools(ctx, nc, "sage2")
        L = range(G)
        e = EdgeSide(ctx, nc, sb, sem)
        a = [sb(f"a{c}", [P, T, D], F32) for c in L]
        h = [sb(f"h{c}", [P, T, D], F32) for c in L]
        g = [sb(f"g{c}", [P, T, D], F32) for c in L]
        aT = [sb(f"aT{c}", [P, CH], F32) for c in L]
        hT = [sb(f"hT{c}", [P, CH], F32) for c in L]
        h_in = [sem(f"h_in{c}") for c in L]
        kept = [sem(f"kept{c}") for c in L]
        pa, ph, pm, ps = banks("pa", G), banks("ph", G), banks("pm", G), banks("ps", G)
        block = ctx.enter_context(nc.Block())
        order = ["turn", "aT", "hT", "mix", "relu", "match", "combine", "keep"]
        at = counter(order)
        RD = NCH // G
        rows3 = tb.node3.rearrange("r k f -> (r k) f")

        @block.sync
        def _(sp):
            def load_h(i, c):
                sp.dma_start(flat(h[c][:, :, :]).unsqueeze(1), chunk_rows(tb.h1s, i, c)).then_inc(h_in[c], 16)

            def keep_rows(i, c):
                sp.wait_ge(e.done[c], at(i, "match"))
                sp.dma_start(chunk_rows(tb.g1s, i, c), flat(g[c][:, :, :]).unsqueeze(1)).then_inc(kept[c], 16)

            for c in L:
                load_gather_rows(sp, e, tb, 0, c)
                load_records(sp, e, tb, tb.dst, 0, c)
                load_h(0, c)
            with sp.Fori(0, RD - 1) as i:
                for c in L:
                    sp.wait_ge(e.gathered[c], (i + 1) * T * 16)
                    load_gather_rows(sp, e, tb, i + 1, c)
                for c in L:
                    sp.wait_ge(e.done[c], at(i, "mix"))
                    load_h(i + 1, c)
                for c in L:
                    keep_rows(i, c)
                for c in L:
                    sp.wait_ge(e.done[c], at(i, "combine"))
                    load_records(sp, e, tb, tb.dst, i + 1, c)
            for c in L:
                keep_rows(RD - 1, c)
            for c in L:
                sp.wait_ge(kept[c], RD * 16 + 1)

        @block.gpsimd
        def _(pool):
            def gathers(c):
                for t in range(T):
                    gather(pool, a[c][:, t, :], rows3, e.gidx[c], G_SRC3 * T + t, e.gathered[c], D)

            def free(i, c):
                pool.wait_ge(e.done[c], at(i, "aT"))
            pool_program(pool, k.ticks, e, at, RD, gathers, free, rows3, A_DST3, 2 * D)

        @block.vector
        def _(dve):
            start(dve, *e.done, e.turns, *kept)

            with dve.Fori(0, RD) as i:
                for c in L:
                    dve.wait_ge(e.done[c], at(i, "hT"))
                    nc.vector.tensor_copy(hT[c][:, :], ph[c][:, :]).then_inc(e.done[c], 1)
                for c in L:
                    match_keys(nc, dve, e, at, i, c, F_KEYD, F_INVD)

        @block.scalar
        def _(act):
            with act.Fori(0, RD) as i:
                for c in L:
                    act.wait_ge(e.done[c], at(i, "aT"))
                    nc.scalar.activation(aT[c][:, :], pa[c][:, :], ACT.Copy).then_inc(e.done[c], 1)
                for c in L:
                    act.wait_ge(kept[c], i * 16 + 1)
                    act.wait_ge(e.done[c], at(i, "relu"))
                    nc.scalar.activation(flat(g[c][:, :, :]), pm[c][:, :], ACT.Relu).then_inc(e.done[c], 1)
                for c in L:
                    keep_sums(nc, act, e, tb, at, i, c, ps[c])

        @block.tensor
        def _(pe):
            with pe.Fori(0, RD) as i:
                for c in L:
                    pe.wait_ge(e.gathered[c], (i + 1) * T * 16)
                    pe.wait_ge(h_in[c], (i + 1) * 16)
                    pe.wait_ge(e.done[c], at(i, "turn"))
                    transpose4(nc, pa[c], a[c], k.ident[:, :])
                    transpose4(nc, ph[c], h[c], k.ident[:, :]).then_inc(e.done[c], 1)
                for c in L:
                    pe.wait_ge(e.done[c], at(i, "mix"))
                    rows_matmul(nc, pm[c], [(aT[c], k.wT[:, 0, :]), (hT[c], k.wT[:, 1, :])],
                                (lambda t: k.ones[:, :], k.brow[:, 0, :])).then_inc(e.done[c], 1)
                for c in L:
                    pe.wait_ge(e.done[c], at(i, "combine"))
                    combine_messages(nc, ps[c], e.same[c], g[c]).then_inc(e.done[c], 1)


def edge_mlp_phase(nc, k, tb):
    with ExitStack() as ctx:
        sb, sem, banks = phase_tools(ctx, nc, "mlp")
        L = range(G)
        e = EdgeSide(ctx, nc, sb, sem)

        def each(name, shape):
            return [sb(f"{name}{c}", shape, F32) for c in L]
        a2, gs, xs, x2s, h2s = (each(n, [P, T, D]) for n in ("a2", "gs", "xs", "x2s", "h2s"))
        sa, sg = each("sa", [P, CH]), each("sg", [P, CH])
        w3 = each("w3", [P, T, 3 * D])
        h1d, x2d, h2d = (each(n, [P, T, D]) for n in ("h1d", "x2d", "h2d"))
        dh, da, dg = each("dh", [P, CH]), each("da", [P, CH]), each("dg", [P, CH])
        ea, eaT = each("ea", [P, P]), each("eaT", [P, P])
        hidT, msg = each("hidT", [P, CH]), each("msg", [P, T, D])
        ns, nd1, nd2 = ([Norm(sb, f"{n}{c}", k.ticks) for c in L] for n in ("ns", "nd1", "nd2"))
        sdone = [sem(f"sdone{c}") for c in L]
        ddone = [sem(f"ddone{c}") for c in L]
        side_in = [sem(f"side_in{c}") for c in L]
        ea_in = [sem(f"ea_in{c}") for c in L]
        kept = [sem(f"kept{c}") for c in L]
        ea_zero = sem("ea_zero")
        ps0, ps1, pd0, pd1 = banks("ps_a", G), banks("ps_b", G), banks("pd_a", G), banks("pd_b", G)
        block = ctx.enter_context(nc.Block())
        sat = counter(["turn", "aT", "gT", "mix", "x2"] + ln("h2_") + ["turn_h2", "h2T"])
        dat = counter(ln("h1_") + ["turn", "h1T", "aT", "mix", "relu", "turn2", "a2T", "mix2", "x2"] + ln("h2_")
                      + ["turn_h2", "h2T"])
        at = counter(["match", "turn_ea", "eaT", "hidden", "relu", "message", "msg", "combine", "keep"])
        RD = NCH // G
        rows3 = tb.node3.rearrange("r k f -> (r k) f")
        whole = tb.node3.rearrange("r k f -> r (k f)")

        @block.sync
        def _(sp):
            def load_side(i, c):
                sp.dma_start(flat(gs[c][:, :, :]).unsqueeze(1), chunk_rows(tb.g1s, i, c)).then_inc(side_in[c], 16)
                sp.dma_start(flat(xs[c][:, :, :]).unsqueeze(1), chunk_rows(tb.x1s, i, c)).then_inc(side_in[c], 16)

            def load_ea(i, c):
                sp.dma_start(ea[c][:, 0:2 * T].unsqueeze(1),
                             tb.ea.rearrange("(c p t) k -> c p (t k)", p=P, t=T)[DynSlice(i * G + c, 1)]
                             .rearrange("c p f -> p c f")).then_inc(ea_in[c], 16)

            def keep_rows(i, c):
                sp.wait_ge(ddone[c], dat(i, "turn_h2"))
                sp.dma_start(chunk_rows(tb.x2d, i, c), flat(x2d[c][:, :, :]).unsqueeze(1)).then_inc(kept[c], 16)
                sp.dma_start(chunk_rows(tb.h2d, i, c), flat(h2d[c][:, :, :]).unsqueeze(1)).then_inc(kept[c], 16)

            sp.wait_ge(ea_zero, 1)
            for c in L:
                load_gather_rows(sp, e, tb, 0, c)
                load_side(0, c)
                load_ea(0, c)
                load_records(sp, e, tb, tb.dst, 0, c)
            with sp.Fori(0, RD - 1) as i:
                for c in L:
                    sp.wait_ge(e.gathered[c], (i + 1) * 2 * T * 16)
                    load_gather_rows(sp, e, tb, i + 1, c)
                for c in L:
                    sp.wait_ge(sdone[c], sat(i, "h2_stats"))
                    load_side(i + 1, c)
                for c in L:
                    keep_rows(i, c)
                for c in L:
                    sp.wait_ge(e.done[c], at(i, "eaT"))
                    load_ea(i + 1, c)
                    load_records(sp, e, tb, tb.dst, i + 1, c)
            for c in L:
                keep_rows(RD - 1, c)
            for c in L:
                sp.wait_ge(kept[c], RD * 32 + 1)

        @block.gpsimd
        def _(pool):
            for c in L:
                last = nc.gpsimd.memset(ea[c][:, :], 0.0)
            last.then_inc(ea_zero, 1)

            def gathers(c):
                for t in range(T):
                    gather(pool, w3[c][:, t, :], whole, e.gidx[c], G_DST * T + t, e.gathered[c])
                for t in range(T):
                    gather(pool, a2[c][:, t, :], rows3, e.gidx[c], G_SRC3 * T + t, e.gathered[c], 2 * D)

            def free(i, c):
                pool.wait_ge(ddone[c], dat(i, "h2_stats"))
                pool.wait_ge(sdone[c], sat(i, "aT"))
            pool_program(pool, k.ticks, e, at, RD, gathers, free, tb.sum3, A_DST, 0)

        @block.vector
        def _(dve):
            start(dve, *e.done, *sdone, *ddone, e.turns, *kept)

            with dve.Fori(0, RD) as i:
                for c in L:
                    dve.wait_ge(e.gathered[c], (i + 1) * 2 * T * 16)
                    norm_vector_1(nc, dve, ddone[c], dat, i, "h1_", nd1[c], w3[c][:, :, 0:D])
                for c in L:
                    norm_vector_2(nc, dve, ddone[c], dat, i, "h1_", nd1[c])
                for c in L:
                    norm_vector_3(nc, dve, ddone[c], dat, i, "h1_", nd1[c])
                for c in L:
                    norm_vector_4(nc, dve, ddone[c], dat, i, "h1_", nd1[c])
                for c in L:
                    dve.wait_ge(sdone[c], sat(i, "gT"))
                    nc.vector.tensor_copy(sg[c][:, :], ps1[c][:, :]).then_inc(sdone[c], 1)
                for c in L:
                    match_keys(nc, dve, e, at, i, c, F_KEYD, F_INVD)
                for c in L:
                    dve.wait_ge(sdone[c], sat(i, "x2"))
                    nc.vector.scalar_tensor_tensor(out=flat(x2s[c][:, :, :]), in0=ps0[c][:, :], scalar=0.0,
                                                   in1=flat(xs[c][:, :, :]), op0=ALU.max, op1=ALU.add).then_inc(sdone[c], 1)
                for c in L:
                    norm_vector_1(nc, dve, sdone[c], sat, i, "h2_", ns[c], x2s[c])
                for c in L:
                    norm_vector_2(nc, dve, sdone[c], sat, i, "h2_", ns[c])
                for c in L:
                    dve.wait_ge(ddone[c], dat(i, "aT"))
                    nc.vector.tensor_copy(da[c][:, :], pd1[c][:, :]).then_inc(ddone[c], 1)
                for c in L:
                    norm_vector_3(nc, dve, sdone[c], sat, i, "h2_", ns[c])
                for c in L:
                    norm_vector_4(nc, dve, sdone[c], sat, i, "h2_", ns[c])
                for c in L:
                    dve.wait_ge(ddone[c], dat(i, "a2T"))
                    nc.vector.tensor_copy(da[c][:, :], pd1[c][:, :]).then_inc(ddone[c], 1)
                for c in L:
                    dve.wait_ge(kept[c], i * 32 + 1)
                    dve.wait_ge(ddone[c], dat(i, "x2"))
                    nc.vector.scalar_tensor_tensor(out=x2d[c][:, :, :], in0=pd0[c][:, :].rearrange("p (t f) -> p t f", f=D),
                                                   scalar=0.0, in1=w3[c][:, :, 0:D], op0=ALU.max, op1=ALU.add).then_inc(ddone[c], 1)
                for c in L:
                    norm_vector_1(nc, dve, ddone[c], dat, i, "h2_", nd2[c], x2d[c])
                for c in L:
                    norm_vector_2(nc, dve, ddone[c], dat, i, "h2_", nd2[c])
                for c in L:
                    norm_vector_3(nc, dve, ddone[c], dat, i, "h2_", nd2[c])
                for c in L:
                    norm_vector_4(nc, dve, ddone[c], dat, i, "h2_", nd2[c])
                for c in L:
                    dve.wait_ge(e.done[c], at(i, "eaT"))
                    nc.vector.tensor_copy(eaT[c][:, :], ps0[c][:, 0:P]).then_inc(e.done[c], 1)
                for c in L:
                    dve.wait_ge(e.done[c], at(i, "msg"))
                    nc.vector.tensor_copy(flat(msg[c][:, :, :]), pd0[c][:, :]).then_inc(e.done[c], 1)

        @block.scalar
        def _(act):
            with act.Fori(0, RD) as i:
                for c in L:
                    act.wait_ge(sdone[c], sat(i, "aT"))
                    nc.scalar.activation(sa[c][:, :], ps0[c][:, :], ACT.Copy).then_inc(sdone[c], 1)
                for c in L:
                    norm_scalar_1(nc, act, ddone[c], dat, i, "h1_", nd1[c], k.eps[:, :])
                for c in L:
                    norm_scalar_2(nc, act, ddone[c], dat, i, "h1_", nd1[c], h1d[c], w3[c][:, :, 0:D], ACT.Relu)
                for c in L:
                    act.wait_ge(ddone[c], dat(i, "h1T"))
                    nc.scalar.activation(dh[c][:, :], pd0[c][:, :], ACT.Copy).then_inc(ddone[c], 1)
                for c in L:
                    norm_scalar_1(nc, act, sdone[c], sat, i, "h2_", ns[c], k.eps[:, :])
                for c in L:
                    act.wait_ge(ddone[c], dat(i, "relu"))
                    nc.scalar.activation(dg[c][:, :], pd0[c][:, :], ACT.Relu, bias=k.bcol[:, 0:1]).then_inc(ddone[c], 1)
                for c in L:
                    norm_scalar_2(nc, act, sdone[c], sat, i, "h2_", ns[c], h2s[c], x2s[c], ACT.Relu)
                for c in L:
                    act.wait_ge(sdone[c], sat(i, "h2T"))
                    nc.scalar.activation(sa[c][:, :], ps1[c][:, :], ACT.Copy).then_inc(sdone[c], 1)
                for c in L:
                    norm_scalar_1(nc, act, ddone[c], dat, i, "h2_", nd2[c], k.eps[:, :])
                for c in L:
                    norm_scalar_2(nc, act, ddone[c], dat, i, "h2_", nd2[c], h2d[c], x2d[c], ACT.Relu)
                for c in L:
                    act.wait_ge(ddone[c], dat(i, "h2T"))
                    nc.scalar.activation(dh[c][:, :], pd1[c][:, :], ACT.Copy).then_inc(ddone[c], 1)
                for c in L:
                    act.wait_ge(e.done[c], at(i, "relu"))
                    nc.scalar.activation(hidT[c][:, :], ps1[c][:, :], ACT.Relu, bias=k.bcol[:, 1:2]).then_inc(e.done[c], 1)
                for c in L:
                    keep_sums(nc, act, e, tb, at, i, c, pd1[c])

        @block.tensor
        def _(pe):
            with pe.Fori(0, RD) as i:
                for c in L:
                    pe.wait_ge(e.gathered[c], (i + 1) * 2 * T * 16)
                    pe.wait_ge(side_in[c], (i + 1) * 32)
                    pe.wait_ge(e.done[c], at(i, "match"))
                    pe.wait_ge(sdone[c], sat(i, "turn"))
                    transpose4(nc, ps0[c], a2[c], k.ident[:, :])
                    transpose4(nc, ps1[c], gs[c], k.ident[:, :]).then_inc(sdone[c], 1)
                for c in L:
                    pe.wait_ge(sdone[c], sat(i, "mix"))
                    rows_matmul(nc, ps0[c], [(sa[c], k.wT[:, 2, :]), (sg[c], k.wT[:, 3, :])],
                                (lambda t: k.ones[:, :], k.brow[:, 1, :])).then_inc(sdone[c], 1)
                for c in L:
                    pe.wait_ge(ddone[c], dat(i, "turn"))
                    transpose4(nc, pd0[c], h1d[c], k.ident[:, :])
                    transpose4(nc, pd1[c], w3[c][:, :, D:2 * D], k.ident[:, :]).then_inc(ddone[c], 1)
                for c in L:
                    pe.wait_ge(ddone[c], dat(i, "mix"))
                    nc.tensor.matmul(pd0[c][:, :], k.wT[:, 0, :], da[c][:, :], start=True, stop=False)
                    nc.tensor.matmul(pd0[c][:, :], k.wT[:, 1, :], dh[c][:, :], start=False, stop=True).then_inc(ddone[c], 1)
                for c in L:
                    pe.wait_ge(ddone[c], dat(i, "turn2"))
                    transpose4(nc, pd1[c], w3[c][:, :, 2 * D:3 * D], k.ident[:, :]).then_inc(ddone[c], 1)
                for c in L:
                    pe.wait_ge(ddone[c], dat(i, "mix2"))
                    rows_matmul(nc, pd0[c], [(da[c], k.wT[:, 2, :]), (dg[c], k.wT[:, 3, :])],
                                (lambda t: k.ones[:, :], k.brow[:, 1, :])).then_inc(ddone[c], 1)
                for c in L:
                    pe.wait_ge(sdone[c], sat(i, "turn_h2"))
                    transpose4(nc, ps1[c], h2s[c], k.ident[:, :]).then_inc(sdone[c], 1)
                for c in L:
                    pe.wait_ge(ddone[c], dat(i, "turn_h2"))
                    transpose4(nc, pd1[c], h2d[c], k.ident[:, :]).then_inc(ddone[c], 1)
                for c in L:
                    pe.wait_ge(ea_in[c], (i + 1) * 16)
                    pe.wait_ge(sdone[c], sat(i, "end"))
                    pe.wait_ge(e.done[c], at(i, "turn_ea"))
                    nc.tensor.transpose(ps0[c][:, 0:P], ea[c][:, :], k.ident[:, :]).then_inc(e.done[c], 1)
                for c in L:
                    pe.wait_ge(ddone[c], dat(i, "end"))
                    pe.wait_ge(e.done[c], at(i, "hidden"))
                    for t in range(T):
                        o = ps1[c][:, t * P:(t + 1) * P]
                        nc.tensor.matmul(o, k.wD[:, 0, :], sa[c][:, t * P:(t + 1) * P], start=True, stop=False)
                        nc.tensor.matmul(o, k.wD[:, 1, :], dh[c][:, t * P:(t + 1) * P], start=False, stop=False)
                        last = nc.tensor.matmul(o, k.wC[:, t, :], eaT[c][:, :], start=False, stop=True)
                    last.then_inc(e.done[c], 1)
                for c in L:
                    pe.wait_ge(e.done[c], at(i, "message"))
                    rows_matmul(nc, pd0[c], [(hidT[c], k.wD[:, 2, :])],
                                (lambda t: k.ones[:, :], k.brow[:, 2, :])).then_inc(e.done[c], 1)
                for c in L:
                    pe.wait_ge(e.done[c], at(i, "combine"))
                    combine_messages(nc, pd1[c], e.same[c], msg[c]).then_inc(e.done[c], 1)


UPDATE = ["turn_u", "uhT", "usT", "mix_u", "relu_u", "mix_u2", "res"] + ln("t_") + ["gamma", "addx", "beta"]


def update_vector(nc, dve, k, done, at, i, part, usT, p1, p2, h, y, x2, x3, n):
    if part == "usT":
        dve.wait_ge(done, at(i, "usT"))
        nc.vector.tensor_copy(usT[:, :], p1[:, :]).then_inc(done, 1)
    if part == "res":
        dve.wait_ge(done, at(i, "res"))
        nc.vector.tensor_tensor(flat(y[:, :, :]), p2[:, :], flat(h[:, :, :]), ALU.add).then_inc(done, 1)
    if part == "gamma":
        dve.wait_ge(done, at(i, "gamma"))
        nc.vector.tensor_tensor(y[:, :, :], y[:, :, :], k.gamma[:, :].unsqueeze(1).to_broadcast([P, T, D]), ALU.mult).then_inc(done, 1)
    if part == "addx":
        dve.wait_ge(done, at(i, "addx"))
        nc.vector.tensor_tensor(flat(y[:, :, :]), flat(y[:, :, :]), flat(x2[:, :, :]), ALU.add).then_inc(done, 1)
    if part == "beta":
        dve.wait_ge(done, at(i, "beta"))
        nc.vector.tensor_tensor(x3[:, :, :], y[:, :, :], k.beta[:, :].unsqueeze(1).to_broadcast([P, T, D]), ALU.add).then_inc(done, 1)


def mean_phase(nc, k, tb):
    with ExitStack() as ctx:
        sb, sem, banks = phase_tools(ctx, nc, "mean")
        L = range(G)
        e = EdgeSide(ctx, nc, sb, sem)

        def each(name, shape):
            return [sb(f"{name}{c}", shape, F32) for c in L]
        s3, x2, h2, y, x3, h3 = (each(n, [P, T, D]) for n in ("s3", "x2", "h2", "y", "x3", "h3"))
        uhT, usT, uT = (each(n, [P, CH]) for n in ("uhT", "usT", "uT"))
        nt, n3 = ([Norm(sb, f"{n}{c}", k.ticks) for c in L] for n in ("nt", "n3"))
        side_in = [sem(f"side_in{c}") for c in L]
        p0, p1, p2, p3 = banks("p0", G), banks("p1", G), banks("p2", G), banks("p3", G)
        block = ctx.enter_context(nc.Block())
        at = counter(UPDATE + ln("h3_") + ["match", "combine", "keep"])
        RD = NCH // G

        @block.sync
        def _(sp):
            def load_side(i, c):
                sp.dma_start(flat(x2[c][:, :, :]).unsqueeze(1), chunk_rows(tb.x2d, i, c)).then_inc(side_in[c], 16)
                sp.dma_start(flat(h2[c][:, :, :]).unsqueeze(1), chunk_rows(tb.h2d, i, c)).then_inc(side_in[c], 16)

            for c in L:
                load_gather_rows(sp, e, tb, 0, c)
                load_side(0, c)
                load_records(sp, e, tb, tb.src, 0, c)
            with sp.Fori(0, RD - 1) as i:
                for c in L:
                    sp.wait_ge(e.gathered[c], (i + 1) * T * 16)
                    load_gather_rows(sp, e, tb, i + 1, c)
                for c in L:
                    sp.wait_ge(e.done[c], at(i, "beta"))
                    load_side(i + 1, c)
                for c in L:
                    sp.wait_ge(e.done[c], at(i, "combine"))
                    load_records(sp, e, tb, tb.src, i + 1, c)

        @block.gpsimd
        def _(pool):
            def gathers(c):
                for t in range(T):
                    gather(pool, s3[c][:, t, :], tb.sum3, e.gidx[c], G_DST * T + t, e.gathered[c])

            def free(i, c):
                pool.wait_ge(e.done[c], at(i, "uhT"))
            pool_program(pool, k.ticks, e, at, RD, gathers, free, tb.sum4, A_SRC, 0)

        @block.vector
        def _(dve):
            start(dve, *e.done, e.turns)

            def update(i, part):
                for c in L:
                    update_vector(nc, dve, k, e.done[c], at, i, part, usT[c], p1[c], p3[c], h2[c], y[c], x2[c], x3[c], nt[c])
            with dve.Fori(0, RD) as i:
                update(i, "usT")
                update(i, "res")
                for pre, n, x in (("t_", nt, y), ("h3_", n3, x3)):
                    for c in L:
                        norm_vector_1(nc, dve, e.done[c], at, i, pre, n[c], x[c])
                    for c in L:
                        norm_vector_2(nc, dve, e.done[c], at, i, pre, n[c])
                    for c in L:
                        norm_vector_3(nc, dve, e.done[c], at, i, pre, n[c])
                    for c in L:
                        norm_vector_4(nc, dve, e.done[c], at, i, pre, n[c])
                    if pre == "t_":
                        update(i, "gamma")
                        update(i, "addx")
                        update(i, "beta")
                for c in L:
                    match_keys(nc, dve, e, at, i, c, F_KEYS, F_INVS)

        @block.scalar
        def _(act):
            with act.Fori(0, RD) as i:
                for c in L:
                    act.wait_ge(e.done[c], at(i, "uhT"))
                    nc.scalar.activation(uhT[c][:, :], p0[c][:, :], ACT.Copy).then_inc(e.done[c], 1)
                for c in L:
                    act.wait_ge(e.done[c], at(i, "relu_u"))
                    nc.scalar.activation(uT[c][:, :], p2[c][:, :], ACT.Relu, bias=k.bcol[:, 2:3]).then_inc(e.done[c], 1)
                for c in L:
                    norm_scalar_1(nc, act, e.done[c], at, i, "t_", nt[c], k.eps[:, :])
                for c in L:
                    norm_scalar_2(nc, act, e.done[c], at, i, "t_", nt[c], y[c], y[c], ACT.Identity)
                for c in L:
                    norm_scalar_1(nc, act, e.done[c], at, i, "h3_", n3[c], k.eps[:, :])
                for c in L:
                    norm_scalar_2(nc, act, e.done[c], at, i, "h3_", n3[c], h3[c], x3[c], ACT.Relu)
                for c in L:
                    keep_sums(nc, act, e, tb, at, i, c, p2[c])

        @block.tensor
        def _(pe):
            with pe.Fori(0, RD) as i:
                for c in L:
                    pe.wait_ge(e.gathered[c], (i + 1) * T * 16)
                    pe.wait_ge(side_in[c], (i + 1) * 32)
                    pe.wait_ge(e.done[c], at(i, "turn_u"))
                    transpose4(nc, p0[c], h2[c], k.ident[:, :])
                    transpose4(nc, p1[c], s3[c], k.ident[:, :]).then_inc(e.done[c], 1)
                for c in L:
                    pe.wait_ge(e.done[c], at(i, "mix_u"))
                    nc.tensor.matmul(p2[c][:, :], k.wD[:, 3, :], uhT[c][:, :], start=True, stop=False)
                    nc.tensor.matmul(p2[c][:, :], k.wD[:, 4, :], usT[c][:, :], start=False, stop=True).then_inc(e.done[c], 1)
                for c in L:
                    pe.wait_ge(e.done[c], at(i, "mix_u2"))
                    rows_matmul(nc, p3[c], [(uT[c], k.wD[:, 5, :])],
                                (lambda t: k.ones[:, :], k.brow[:, 3, :])).then_inc(e.done[c], 1)
                for c in L:
                    pe.wait_ge(e.done[c], at(i, "combine"))
                    combine_messages(nc, p2[c], e.same[c], h3[c]).then_inc(e.done[c], 1)


def node_phase(nc, k, tb, out):
    with ExitStack() as ctx:
        sb, sem, banks = phase_tools(ctx, nc, "node")
        C = range(GD)

        def each(name, shape):
            return [sb(f"{name}{c}", shape, F32) for c in C]
        w3 = each("w3", [P, T, 3 * D])
        s3, s4, h, x2, y, o = (each(n, [P, T, D]) for n in ("s3", "s4", "h", "x2", "y", "o"))
        hT, sT, gT = (each(n, [P, CH]) for n in ("hT", "sT", "gT"))
        ind = [sb(f"ind{c}", [P, CH], BF16) for c in C]
        nrm = [Norm(sb, f"n{c}", k.ticks) for c in C]
        loaded = [sem(f"loaded{c}") for c in C]
        stored = [sem(f"stored{c}") for c in C]
        done = [sem(f"done{c}") for c in C]
        ind_set = sem("ind_set")
        pa, pb = banks("pa", GD), banks("pb", GD)
        block = ctx.enter_context(nc.Block())
        at = counter(ln("h1_") + ["turn", "hT", "aT", "mix", "relu", "turn2", "a2T", "mix2", "x2"] + ln("h2_") + UPDATE
                     + ln("h3_") + ["turn3", "h3T", "s4T", "mix3", "out"])

        @block.sync
        def _(sp):
            sp.wait_ge(ind_set, 2)

            def load(i, c):
                rows = DynSlice(i * CH + stream_base(c), CH)
                sp.dma_start(w3[c][:, :, :], tb.node3[rows].rearrange("(p t) k f -> p t (k f)", t=T)).then_inc(loaded[c], 16)
                sp.dma_start(s3[c][:, :, :], tb.sum3[rows].rearrange("(p t) f -> p t f", t=T)).then_inc(loaded[c], 16)
                sp.dma_start(s4[c][:, :, :], tb.sum4[rows].rearrange("(p t) f -> p t f", t=T)).then_inc(loaded[c], 16)
                sp.dma_start(ind[c][3:6, :], tb.ind[rows].partition_broadcast(3)).then_inc(loaded[c], 16)

            def store(i, c):
                rows = DynSlice(i * CH + stream_base(c), CH)
                sp.wait_ge(done[c], at(i, "end"))
                sp.dma_start(out[rows].rearrange("(p t) f -> p t f", t=T), o[c][:, :, :]).then_inc(stored[c], 16)

            for c in C:
                load(0, c)
            with sp.Fori(0, NBLK - 1) as i:
                for c in C:
                    store(i, c)
                    load(i + 1, c)
            for c in C:
                store(NBLK - 1, c)
            for c in C:
                sp.wait_ge(stored[c], NBLK * 16 + 1)

        @block.gpsimd
        def _(pool):
            for c in C:
                last = nc.gpsimd.memset(ind[c][:, :], 0.0)
            last.then_inc(ind_set, 1)
            pool.wait_ge(ind_set, 1)
            for c in C:
                last = nc.gpsimd.memset(ind[c][0:3, :], 1.0)
            last.then_inc(ind_set, 1)

        @block.vector
        def _(dve):
            start(dve, *done, *stored)

            def norm(i, pre, x):
                for c in C:
                    norm_vector_1(nc, dve, done[c], at, i, pre, nrm[c], x(c))
                for c in C:
                    norm_vector_2(nc, dve, done[c], at, i, pre, nrm[c])
                for c in C:
                    norm_vector_3(nc, dve, done[c], at, i, pre, nrm[c])
                for c in C:
                    norm_vector_4(nc, dve, done[c], at, i, pre, nrm[c])

            def copy(i, step):
                for c in C:
                    dve.wait_ge(done[c], at(i, step))
                    nc.vector.tensor_copy(sT[c][:, :], pb[c][:, :]).then_inc(done[c], 1)

            def update(i, part):
                for c in C:
                    update_vector(nc, dve, k, done[c], at, i, part, sT[c], pb[c], pb[c], h[c], y[c], x2[c], y[c], nrm[c])

            with dve.Fori(0, NBLK) as i:
                for c in C:
                    dve.wait_ge(loaded[c], (i + 1) * 64)
                norm(i, "h1_", lambda c: w3[c][:, :, 0:D])
                copy(i, "aT")
                copy(i, "a2T")
                for c in C:
                    dve.wait_ge(done[c], at(i, "x2"))
                    nc.vector.scalar_tensor_tensor(out=x2[c][:, :, :], in0=pa[c][:, :].rearrange("p (t f) -> p t f", f=D),
                                                   scalar=0.0, in1=w3[c][:, :, 0:D], op0=ALU.max, op1=ALU.add).then_inc(done[c], 1)
                norm(i, "h2_", lambda c: x2[c])
                update(i, "usT")
                update(i, "res")
                norm(i, "t_", lambda c: y[c])
                update(i, "gamma")
                update(i, "addx")
                update(i, "beta")
                norm(i, "h3_", lambda c: y[c])
                copy(i, "s4T")
                for c in C:
                    dve.wait_ge(stored[c], i * 16 + 1)
                    dve.wait_ge(done[c], at(i, "out"))
                    nc.vector.scalar_tensor_tensor(out=flat(o[c][:, :, :]), in0=pa[c][:, :], scalar=0.0,
                                                   in1=flat(y[c][:, :, :]), op0=ALU.max, op1=ALU.add).then_inc(done[c], 1)

        @block.scalar
        def _(act):
            def norm(i, pre, out_, x, func):
                for c in C:
                    norm_scalar_1(nc, act, done[c], at, i, pre, nrm[c], k.eps[:, :])
                for c in C:
                    norm_scalar_2(nc, act, done[c], at, i, pre, nrm[c], out_(c), x(c), func)

            def copy(i, step, dst, src, func=ACT.Copy, bias=None):
                for c in C:
                    act.wait_ge(done[c], at(i, step))
                    if bias is None:
                        nc.scalar.activation(dst[c][:, :], src[c][:, :], func).then_inc(done[c], 1)
                    else:
                        nc.scalar.activation(dst[c][:, :], src[c][:, :], func, bias=bias).then_inc(done[c], 1)

            with act.Fori(0, NBLK) as i:
                norm(i, "h1_", lambda c: h[c], lambda c: w3[c][:, :, 0:D], ACT.Relu)
                copy(i, "hT", hT, pa)
                copy(i, "relu", gT, pa, ACT.Relu, k.bcol[:, 0:1])
                norm(i, "h2_", lambda c: h[c], lambda c: x2[c], ACT.Relu)
                copy(i, "uhT", hT, pa)
                copy(i, "relu_u", gT, pa, ACT.Relu, k.bcol[:, 2:3])
                norm(i, "t_", lambda c: y[c], lambda c: y[c], ACT.Identity)
                norm(i, "h3_", lambda c: h[c], lambda c: y[c], ACT.Relu)
                copy(i, "h3T", hT, pa)

        @block.tensor
        def _(pe):
            def turn(i, step, first, second):
                for c in C:
                    pe.wait_ge(done[c], at(i, step))
                    if first is not None:
                        transpose4(nc, pa[c], first(c), k.ident[:, :])
                    transpose4(nc, pb[c], second(c), k.ident[:, :]).then_inc(done[c], 1)

            with pe.Fori(0, NBLK) as i:
                turn(i, "turn", lambda c: h[c], lambda c: w3[c][:, :, D:2 * D])
                for c in C:
                    pe.wait_ge(done[c], at(i, "mix"))
                    nc.tensor.matmul(pa[c][:, :], k.wT[:, 0, :], sT[c][:, :], start=True, stop=False)
                    nc.tensor.matmul(pa[c][:, :], k.wT[:, 1, :], hT[c][:, :], start=False, stop=True).then_inc(done[c], 1)
                turn(i, "turn2", None, lambda c: w3[c][:, :, 2 * D:3 * D])
                for c in C:
                    pe.wait_ge(done[c], at(i, "mix2"))
                    rows_matmul(nc, pa[c], [(sT[c], k.wT[:, 2, :]), (gT[c], k.wT[:, 3, :])],
                                (lambda t: k.ones[:, :], k.brow[:, 1, :])).then_inc(done[c], 1)
                turn(i, "turn_u", lambda c: h[c], lambda c: s3[c])
                for c in C:
                    pe.wait_ge(done[c], at(i, "mix_u"))
                    nc.tensor.matmul(pa[c][:, :], k.wD[:, 3, :], hT[c][:, :], start=True, stop=False)
                    nc.tensor.matmul(pa[c][:, :], k.wD[:, 4, :], sT[c][:, :], start=False, stop=True).then_inc(done[c], 1)
                for c in C:
                    pe.wait_ge(done[c], at(i, "mix_u2"))
                    rows_matmul(nc, pb[c], [(gT[c], k.wD[:, 5, :])],
                                (lambda t: k.ones[:, :], k.brow[:, 3, :])).then_inc(done[c], 1)
                turn(i, "turn3", lambda c: h[c], lambda c: s4[c])
                for c in C:
                    pe.wait_ge(done[c], at(i, "mix3"))
                    rows_matmul(nc, pa[c], [(hT[c], k.wT[:, 4, :]), (sT[c], k.wT[:, 5, :])],
                                (lambda t: ind[c][:, t:CH:T], k.brow[:, 4, :])).then_inc(done[c], 1)


def gnn_program(nc, inp, out):
    tb = Tables(nc)
    with ExitStack() as ctx:
        k = Consts(lambda name, shape, dt: ctx.enter_context(nc.sbuf_tensor(name, shape, dt)),
                   ctx.enter_context(nc.semaphore("ticks")))
        with nc.psum_tensor("hist", [P, 2, 1024], F32) as hist:
            setup_phase(nc, k, tb, inp, hist)
            small_table_phase(nc, tb, hist)
        first_rows_phase(nc, k, tb, inp)
        gcn_phase(nc, k, tb, inp, True)
        gcn_phase(nc, k, tb, inp, False)
        sage2_phase(nc, k, tb)
        edge_mlp_phase(nc, k, tb)
        mean_phase(nc, k, tb)
        node_phase(nc, k, tb, out)


_INS = ["x", "src", "dst", "edge_attr_2", "edge_weight", "L1_gnn_W1_l", "L1_gnn_W1_r", "L1_gnn_b1", "L1_gnn_W2_l",
        "L1_gnn_W2_r", "L1_gnn_b2", "L2_gnn_mW1", "L2_gnn_mb1", "L2_gnn_mW2", "L2_gnn_mb2", "L2_gnn_uW1", "L2_gnn_ub1",
        "L2_gnn_uW2", "L2_gnn_ub2", "L2_gnn_gamma", "L2_gnn_beta", "L3_gnn_W_self", "L3_gnn_b_self",
        "L3_gnn_W_neighbor", "L3_gnn_b_neighbor"]


def kernel(**inputs):
    import numpy as _np
    import concourse.bacc as _bacc
    from concourse import mybir as _mybir
    from concourse.bass_utils import run_bass_kernel_spmd as _run

    nc = _bacc.Bacc("TRN2", target_bir_lowering=False, num_devices=1)
    arrays, inp = {}, {}
    for name in _INS:
        a = _np.ascontiguousarray(inputs[name])
        arrays["in_" + name] = a
        inp[name] = nc.dram_tensor("in_" + name, a.shape, _mybir.dt.from_np(a.dtype), kind="ExternalInput").ap()
    out = nc.dram_tensor("out_0", (N, D), F32, kind="ExternalOutput").ap()
    gnn_program(nc, inp, out)
    r = _run(nc, [arrays], core_ids=[0])
    return r.results[0]["out_0"]
```

```python
import concourse.bass as bass
from concourse import mybir
from concourse.bass import DynSlice
from contextlib import ExitStack

F32, I32 = mybir.dt.float32, mybir.dt.int32
BF16, F16 = mybir.dt.bfloat16, mybir.dt.float16
ALU = mybir.AluOpType
ACT = mybir.ActivationFunctionType

N, E, D = 100000, 25000, 128
P = 128
T = 4
CH = P * T
G = 4
NCH = -(-E // (G * CH)) * G
EP = NCH * CH
PAD = EP - E
HIQ = -(-(N + PAD) // (P * P))
NT = HIQ * P * P
DUMP = -(-(N + PAD) // P) * P
ZR = 9
R = -(-(DUMP + CH) // (P * ZR)) * P * ZR
S = 2
GD = 4
NBLK = -(-N // (CH * GD))
EPS = 1e-5

C_DIS, C_INVS, C_INVD, C_IND = range(4)
G_SRC, G_DST, G_SRC3, G_DSTC = range(4)
A_SRC3, A_DST3, A_DST, A_SRC = range(4)
F_KEYS, F_KEYD, F_W, F_INVD, F_INVS = range(5)


def stream_base(c):
    return c * (N - NBLK * CH) // (GD - 1)


def rounds(eng, step, order, streams, n):
    size = len(order)

    def one_round(i, head=True, tail=True):
        for slot in range(size):
            for c in range(streams):
                at = slot - c * size // streams
                if at >= 0 and head:
                    step(order[at], i, c)
                if at < 0 and tail:
                    step(order[at + size], i - 1, c)

    one_round(0, tail=False)
    with eng.Fori(1, n - 1) as i:
        one_round(i)
    one_round(n - 1)
    one_round(n, head=False)


def tiles(f):
    for t in range(T):
        last = f(t)
    return last


def counter(order):
    return lambda i, step, n=len(order): i * n + (order + ["end"]).index(step) + 1


def start(eng, *sems):
    for s in sems:
        eng.sem_inc(s, 1)


LN = ["stats", "mean_var", "std", "rstd", "shift", "norm"]


def ln(prefix):
    return [prefix + s for s in LN]


def wait_alone(eng, ticks, sem, value):
    eng.wait_ge(sem, value)
    eng.sem_inc(ticks, 1)


class Norm:

    def __init__(self, sb, name, ticks):
        self.ticks = ticks
        self.st = sb(name + "_stats", [P, T, 6], F32)
        self.mv = sb(name + "_mean_var", [P, T, 2], F32)
        self.sd = sb(name + "_std", [P, T], F32)
        self.rs = sb(name + "_rstd", [P, T], F32)
        self.sh = sb(name + "_shift", [P, T], F32)


def norm_vector(nc, dve, done, at, i, pre, name, b, x):
    if name == pre + "stats":
        dve.wait_ge(done, at(i, name))
        tiles(lambda t: nc.vector.bn_stats(b.st[:, t, :], x[:, t, :])).then_inc(done, 1)
    if name == pre + "mean_var":
        wait_alone(dve, b.ticks, done, at(i, name))
        tiles(lambda t: nc.vector.bn_aggr(b.mv[:, t, :], b.st[:, t, :])).then_inc(done, 1)
    if name == pre + "rstd":
        dve.wait_ge(done, at(i, name))
        nc.vector.reciprocal(b.rs[:, :], b.sd[:, :]).then_inc(done, 1)
    if name == pre + "shift":
        dve.wait_ge(done, at(i, name))
        nc.vector.scalar_tensor_tensor(out=b.sh[:, :], in0=b.mv[:, :, 0], scalar=-1.0, in1=b.rs[:, :],
                                       op0=ALU.mult, op1=ALU.mult).then_inc(done, 1)


def norm_scalar(nc, act, done, at, i, pre, name, b, eps, out, x, func):
    if name == pre + "std":
        act.wait_ge(done, at(i, name))
        nc.scalar.activation(b.sd[:, :], b.mv[:, :, 1], ACT.Sqrt, bias=eps).then_inc(done, 1)
    if name == pre + "norm":
        act.wait_ge(done, at(i, name))
        tiles(lambda t: nc.scalar.activation(out[:, t, :], x[:, t, :], func,
                                             bias=b.sh[:, t:t + 1], scale=b.rs[:, t:t + 1])).then_inc(done, 1)


def transpose4(nc, ps, x, ident):
    return tiles(lambda t: nc.tensor.transpose(ps[:, t * P:(t + 1) * P], x[:, t, :], ident))


def rows_matmul(nc, ps, pairs, bias=None):
    for t in range(T):
        o = ps[:, t * P:(t + 1) * P]
        for n, (xT, w) in enumerate(pairs):
            last = nc.tensor.matmul(o, xT[:, t * P:(t + 1) * P], w, start=(n == 0),
                                    stop=(bias is None and n == len(pairs) - 1))
        if bias is not None:
            last = nc.tensor.matmul(o, bias[0](t), bias[1], start=False, stop=True)
    return last


def columns_plus(nc, ps, w, xT, rows, ident):
    nc.tensor.matmul(ps[:, :], w, xT[:, :], start=True, stop=False)
    return tiles(lambda t: nc.tensor.matmul(ps[:, t * P:(t + 1) * P], rows[:, t, :], ident, is_transpose=True,
                                            start=False, stop=(t == T - 1)))


def combine_rows(nc, ps, same, msg):
    for a in range(T):
        for b in range(T):
            last = nc.tensor.matmul(ps[:, a * P:(a + 1) * P], same[:, b, a:CH:T], msg[:, b, :],
                                    start=(b == 0), stop=(b == T - 1))
    return last


def combine_columns(nc, ps, same, msg):
    return tiles(lambda b: nc.tensor.matmul(ps[:, :], msg[:, b, :], same[:, b, :], start=(b == 0), stop=(b == T - 1)))


def apply_columns(nc, ps, sumT, w):
    return tiles(lambda a: nc.tensor.matmul(ps[:, a * P:(a + 1) * P], sumT[:, a:CH:T], w, start=True, stop=True))


class Tables:

    def __init__(self, nc):
        def dram(name, shape, dt):
            return nc.dram_tensor(name, shape, dt, kind="Internal").ap()
        self.node3 = dram("node3", (R, 3, D), F32)
        self.sum3 = dram("sum3", (R, D), F32)
        self.sum4 = dram("sum4", (R, D), F32)
        self.small = dram("small", (NT, 4), F32)
        self.ind = dram("ind", (NT,), BF16)
        self.src = dram("src_padded", (EP,), I32)
        self.dst = dram("dst_padded", (EP,), I32)
        self.ew = dram("ew_padded", (EP,), F32)
        self.ea = dram("ea_padded", (EP, 2), F32)
        self.rec_g = dram("rec_gather", (NCH, P, 16), I32)
        self.rec_a = dram("rec_add", (NCH, P, 16), I32)
        self.rec_f = dram("rec_float", (NCH, P, 20), F32)
        self.x1s = dram("x1_src", (NCH, P, T * D), F32)
        self.h1s = dram("h1_src", (NCH, P, T * D), F32)
        self.g1s = dram("g1_src", (NCH, P, T * D), F32)
        self.x2d = dram("x2_dst", (NCH, P, T * D), F32)
        self.h2d = dram("h2_dst", (NCH, P, T * D), F32)
        self.split = dram("bias_split", (6, 3, D), BF16)


class Consts:

    def __init__(self, sb, ticks):
        self.ticks = ticks
        self.ident = sb("ident", [P, P], F32)
        self.eps = sb("eps", [P, 1], F32)
        self.wT = sb("wT", [P, 6, D], F32)
        self.wD = sb("wD", [P, 6, D], F32)
        self.wC = sb("wC", [P, T, D], F32)
        self.bcol = sb("bcol", [P, 3], F32)
        self.brow = sb("brow", [P, 5, D], BF16)
        self.ones = sb("ones", [P, P], BF16)
        self.gamma = sb("gamma", [P, D], F32)
        self.beta = sb("beta", [P, D], F32)


def setup_phase(nc, k, tb, inp, hist):
    with ExitStack() as ctx:
        def sb(name, shape, dt):
            return ctx.enter_context(nc.sbuf_tensor(name, shape, dt))

        def sem(name):
            return ctx.enter_context(nc.semaphore(name))

        zero = sb("zero", [P, max(ZR * 2 * D, 2 * PAD)], F32)
        padkey = sb("padkey", [1, PAD], I32)
        wraw = sb("wraw", [P, 6, D], F32)
        brows = sb("brows", [6, D], F32)
        bres = sb("bres", [6, 2, D], F32)
        bsplit = sb("bsplit", [6, 3, D], BF16)
        srcI = sb("srcI", [P, NCH, T], I32)
        dstI = sb("dstI", [P, NCH, T], I32)
        digit = sb("digit", [P, NCH, T], I32)
        parts = sb("parts", [P, NCH, 6 * T], F32)
        counts = sb("counts", [P, NCH, 2 * T], F32)
        spare = sb("spare", [P, NCH, T], F32)
        dup = sb("dup", [P, NCH, T], F32)
        lead = sb("lead", [P, NCH, T], F32)
        recg = sb("recg", [P, NCH, 16], I32)
        reca = sb("reca", [P, NCH, 16], I32)
        iota = sb("iota", [P, HIQ * P], F16)
        earlier = sb("earlier", [P, T, CH], BF16)
        zh = sb("zh", [P, 512], F16)
        part = [sb(f"part{c}", [P, 6 * T], F32) for c in range(S)]
        krow = [sb(f"krow{c}", [P, 2, CH], I32) for c in range(S)]
        hi = [sb(f"hi{c}", [P, 2, T, HIQ * P], F16) for c in range(S)]
        lo = [sb(f"lo{c}", [P, 2, T, P], F16) for c in range(S)]
        junk = [sb(f"junk{c}", [P, 2 * T, CH], BF16) for c in range(S)]
        prev = [sb(f"prev{c}", [P, 2 * T], F32) for c in range(S)]
        tps = ctx.enter_context(nc.psum_tensor("tps", [P, 2, 512], F32))

        zero_set, const_set, cleared, padded = sem("zero_set"), sem("const_set"), sem("cleared"), sem("padded")
        edges_in, weights_in, bias_in, split_out = sem("edges_in"), sem("weights_in"), sem("bias_in"), sem("split_out")
        split_in, recs_out = sem("split_in"), sem("recs_out")
        transposed, linked, weights_ready, memzero = sem("transposed"), sem("linked"), sem("weights_ready"), sem("memzero")
        keys_in = [sem(f"keys_in{c}") for c in range(S)]
        led = [sem(f"led{c}") for c in range(S)]
        counted = [sem(f"counted{c}") for c in range(S)]
        block = ctx.enter_context(nc.Block())
        order = ["pick", "onehots", "earlier", "keep"]
        at = counter(order)

        @block.gpsimd
        def _(pool):
            nc.gpsimd.memset(zero[:, :], 0.0).then_inc(zero_set, 1)
            nc.gpsimd.iota(padkey[:, :], pattern=[[1, PAD]], base=N, channel_multiplier=0).then_inc(zero_set, 1)
            nc.gpsimd.memset(k.ident[:, :], 0.0).then_inc(memzero, 1)
            nc.gpsimd.memset(earlier[:, :, :], 1.0).then_inc(memzero, 1)
            nc.gpsimd.memset(k.wC[:, :, :], 0.0).then_inc(memzero, 1)
            nc.gpsimd.memset(k.brow[:, :, :], 0.0).then_inc(memzero, 1)
            nc.gpsimd.memset(k.ones[:, :], 1.0)
            nc.gpsimd.memset(k.eps[:, :], EPS)
            nc.gpsimd.memset(zh[:, :], 0.0)
            nc.gpsimd.iota(iota[:, :], pattern=[[1, HIQ * P]], base=0, channel_multiplier=0,
                           allow_small_or_imprecise_dtypes=True)
            nc.gpsimd.iota(spare[:, :, :], pattern=[[0, NCH], [1, T]], base=DUMP, channel_multiplier=T,
                           allow_small_or_imprecise_dtypes=True)
            pool.wait_ge(memzero, 2)
            nc.gpsimd.affine_select(out=k.ident[:, :], in_=k.ident[:, :], compare_op=ALU.not_equal, fill=1.0,
                                    base=0, pattern=[[-1, P]], channel_multiplier=1)
            for t in range(T):
                last = nc.gpsimd.affine_select(out=earlier[:, t, :], in_=earlier[:, t, :], compare_op=ALU.is_gt,
                                               fill=0.0, base=t, pattern=[[-1, CH]], channel_multiplier=T)
            last.then_inc(const_set, 1)

        @block.sync
        def _(sp):
            sp.wait_ge(padded, 128)
            with sp.Fori(0, NCH // S) as i:
                for c in range(S):
                    sp.wait_ge(led[c], at(i, "pick"))
                    for n, key in enumerate((tb.src, tb.dst)):
                        row = key.rearrange("(c e) -> c e", e=CH)[DynSlice(i * S + c, 1), :]
                        sp.dma_start(krow[c][:, n, :], row.partition_broadcast(P)).then_inc(keys_in[c], 16)
            sp.wait_ge(linked, 9 + 10)
            sp.dma_start(tb.rec_g.rearrange("c p k -> p c k"), recg[:, :, :]).then_inc(recs_out, 16)
            sp.dma_start(tb.rec_a.rearrange("c p k -> p c k"), reca[:, :, :]).then_inc(recs_out, 16)
            sp.wait_ge(recs_out, 32)

        @block.scalar
        def _(act):
            act.wait_ge(zero_set, 2)
            z = zero[0:1, :]
            act.dma_start(tb.src[0:E], inp["src"]).then_inc(padded, 16)
            act.dma_start(tb.dst[0:E], inp["dst"]).then_inc(padded, 16)
            act.dma_start(tb.ew[0:E], inp["edge_weight"]).then_inc(padded, 16)
            act.dma_start(tb.ea[0:E, :], inp["edge_attr_2"]).then_inc(padded, 16)
            act.dma_start(tb.src[E:EP].unsqueeze(0), padkey[:, :]).then_inc(padded, 16)
            act.dma_start(tb.dst[E:EP].unsqueeze(0), padkey[:, :]).then_inc(padded, 16)
            act.dma_start(tb.ew[E:EP].unsqueeze(0), z[:, 0:PAD]).then_inc(padded, 16)
            act.dma_start(tb.ea[E:EP, :].rearrange("e k -> (e k)").unsqueeze(0), z[:, 0:2 * PAD]).then_inc(padded, 16)
            for n, name in enumerate(("L1_gnn_W1_l", "L1_gnn_W1_r", "L1_gnn_W2_l", "L1_gnn_W2_r",
                                      "L3_gnn_W_self", "L3_gnn_W_neighbor")):
                act.dma_start(wraw[:, n, :], inp[name]).then_inc(weights_in, 16)
            for n, name in enumerate(("L1_gnn_b1", "L1_gnn_b2", "L2_gnn_mb2", "L2_gnn_ub2",
                                      "L3_gnn_b_self", "L3_gnn_b_neighbor")):
                act.dma_start(brows[n:n + 1, :], inp[name].unsqueeze(0)).then_inc(bias_in, 16)
            act.wait_ge(padded, 128)
            act.dma_start(srcI[:, :, :], tb.src.rearrange("(c p t) -> p c t", p=P, t=T)).then_inc(edges_in, 16)
            act.dma_start(dstI[:, :, :], tb.dst.rearrange("(c p t) -> p c t", p=P, t=T)).then_inc(edges_in, 16)
            m = inp["L2_gnn_mW1"]
            u = inp["L2_gnn_uW1"]
            for n, w in enumerate((m[0:D, :], m[D:2 * D, :], inp["L2_gnn_mW2"], u[0:D, :], u[D:2 * D, :],
                                   inp["L2_gnn_uW2"])):
                act.dma_start(k.wD[:, n, :], w).then_inc(weights_in, 16)
            for n, name in enumerate(("L1_gnn_b1", "L2_gnn_mb1", "L2_gnn_ub1")):
                act.dma_start(k.bcol[:, n:n + 1], inp[name].unsqueeze(1)).then_inc(weights_in, 16)
            act.dma_start(k.gamma[:, :], inp["L2_gnn_gamma"].partition_broadcast(P)).then_inc(weights_in, 16)
            act.dma_start(k.beta[:, :], inp["L2_gnn_beta"].partition_broadcast(P)).then_inc(weights_in, 16)
            act.wait_ge(memzero, 4)
            for t in range(T):
                act.dma_start(k.wC[2 * t:2 * t + 2, t, :], m[2 * D:2 * D + 2, :]).then_inc(weights_in, 16)
            rows3 = tb.node3.rearrange("(p b) k f -> p b k f", p=P)
            rows1 = [s.rearrange("(p b) f -> p b f", p=P) for s in (tb.sum3, tb.sum4)]
            z2 = zero[:, 0:ZR * 2 * D].rearrange("p (b k f) -> p b k f", b=ZR, k=2)
            z1 = zero[:, 0:ZR * D].rearrange("p (b f) -> p b f", b=ZR)
            act.dma_start(tb.node3[N:R, 0, :].rearrange("(p b) f -> p b f", p=32),
                          zero[0:32, 0:D].unsqueeze(1).to_broadcast([32, (R - N) // 32, D])).then_inc(cleared, 16)
            with act.Fori(0, R // P // ZR) as i:
                act.dma_start(rows3[:, DynSlice(i * ZR, ZR), 1:3, :], z2).then_inc(cleared, 16)
                for r in rows1:
                    act.dma_start(r[:, DynSlice(i * ZR, ZR), :], z1).then_inc(cleared, 16)
            act.wait_ge(split_out, 1)
            act.dma_start(tb.split, bsplit[:, :, :]).then_inc(split_in, 16)
            act.wait_ge(split_in, 16)
            act.dma_start(k.brow[0:3, :, :], tb.split[0:5].rearrange("b s f -> s b f")).then_inc(split_in, 16)
            act.dma_start(k.brow[3:6, 4, :], tb.split[5]).then_inc(split_in, 16)
            act.wait_ge(split_in, 48)
            act.wait_ge(weights_in, 16 * (6 + 6 + 3 + 2 + T))
            act.wait_ge(cleared, 16 * (3 * (R // P // ZR) + 1))

        @block.vector
        def _(dve):
            start(dve, *led, *counted)
            links = [0]

            def link(ins):
                links[0] += 1
                ins.then_inc(linked, 1)
                dve.wait_ge(linked, links[0])

            dve.wait_ge(edges_in, 32)
            for n, key in enumerate((srcI, dstI)):
                a = 2 * n * T
                link(nc.vector.tensor_scalar(digit[:, :, :], key[:, :, :], 7, None, ALU.arith_shift_right))
                link(nc.vector.tensor_copy(parts[:, :, a:a + T], digit[:, :, :]))
                link(nc.vector.tensor_scalar(digit[:, :, :], key[:, :, :], P - 1, None, ALU.bitwise_and))
                nc.vector.tensor_copy(parts[:, :, a + T:a + 2 * T], digit[:, :, :])
                link(nc.vector.tensor_copy(parts[:, :, (4 + n) * T:(5 + n) * T], key[:, :, :]))
            assert links[0] == 8
            dve.wait_ge(const_set, 1)
            with dve.Fori(0, NCH // S) as i:
                for c in range(S):
                    dve.wait_ge(led[c], at(i, "pick"))
                    dve.wait_ge(counted[c], i + 1)
                    nc.vector.tensor_copy(part[c][:, :].unsqueeze(1), parts[:, DynSlice(i * S + c, 1), :]).then_inc(led[c], 1)
                for c in range(S):
                    dve.wait_ge(led[c], at(i, "onehots"))
                    for n in range(2):
                        for t in range(T):
                            a = 2 * n * T + t
                            nc.vector.tensor_scalar(hi[c][:, n, t, :], iota[:, :], part[c][:, a:a + 1], None, ALU.is_equal)
                            last = nc.vector.tensor_scalar(lo[c][:, n, t, :], iota[:, 0:P], part[c][:, a + T:a + T + 1],
                                                           None, ALU.is_equal)
                    last.then_inc(led[c], 1)
                for c in range(S):
                    dve.wait_ge(keys_in[c], (i + 1) * 32)
                    dve.wait_ge(led[c], at(i, "earlier"))
                    for n in range(2):
                        for t in range(T):
                            last = nc.vector.scalar_tensor_tensor(
                                out=junk[c][:, n * T + t, :], in0=krow[c][:, n, :],
                                scalar=part[c][:, (4 + n) * T + t:(4 + n) * T + t + 1], in1=earlier[:, t, :],
                                op0=ALU.is_equal, op1=ALU.mult, accum_out=prev[c][:, n * T + t:n * T + t + 1])
                    last.then_inc(led[c], 1)
                for c in range(S):
                    dve.wait_ge(led[c], at(i, "keep"))
                    nc.vector.tensor_copy(counts[:, DynSlice(i * S + c, 1), :], prev[c][:, :].unsqueeze(1)).then_inc(led[c], 1)
            for c in range(S):
                dve.wait_ge(led[c], at(NCH // S, "pick"))
            for n, (src, a, b) in enumerate(((srcI, 0.0, 1.0), (dstI, 0.0, 1.0), (srcI, 0.0, 3.0))):
                nc.vector.tensor_scalar(recg[:, :, n * T:(n + 1) * T], src[:, :, :], b, None, ALU.mult)
            link(nc.vector.tensor_scalar(recg[:, :, G_DSTC * T:(G_DSTC + 1) * T], dstI[:, :, :], float(N - 1), None, ALU.min))
            for n, (one, three) in enumerate(((A_SRC, A_SRC3), (A_DST, A_DST3))):
                key = parts[:, :, (4 + n) * T:(5 + n) * T]
                link(nc.vector.tensor_scalar(dup[:, :, :], counts[:, :, n * T:(n + 1) * T], 0.0, None, ALU.is_gt))
                link(nc.vector.tensor_tensor(lead[:, :, :], spare[:, :, :], key, ALU.subtract))
                link(nc.vector.tensor_tensor(dup[:, :, :], dup[:, :, :], lead[:, :, :], ALU.mult))
                link(nc.vector.tensor_tensor(lead[:, :, :], dup[:, :, :], key, ALU.add))
                nc.vector.tensor_copy(reca[:, :, one * T:(one + 1) * T], lead[:, :, :])
                link(nc.vector.tensor_scalar(reca[:, :, three * T:(three + 1) * T], lead[:, :, :], 3.0, None, ALU.mult))
            assert links[0] == 9 + 10
            dve.wait_ge(bias_in, 96)
            link(nc.vector.tensor_copy(bsplit[:, 0, :], brows[:, :]))
            link(nc.vector.tensor_tensor(bres[:, 0, :], brows[:, :], bsplit[:, 0, :], ALU.subtract))
            link(nc.vector.tensor_copy(bsplit[:, 1, :], bres[:, 0, :]))
            link(nc.vector.tensor_tensor(bres[:, 1, :], bres[:, 0, :], bsplit[:, 1, :], ALU.subtract))
            nc.vector.tensor_copy(bsplit[:, 2, :], bres[:, 1, :]).then_inc(split_out, 1)
            dve.wait_ge(transposed, 1)
            nc.vector.tensor_copy(k.wT[:, 0:4, :], tps[:, 0, :].rearrange("p (n f) -> p n f", f=D))
            nc.vector.tensor_copy(k.wT[:, 4:6, :], tps[:, 1, 0:2 * D].rearrange("p (n f) -> p n f", f=D)).then_inc(weights_ready, 1)

        @block.tensor
        def _(pe):
            pe.wait_ge(const_set, 1)
            pe.wait_ge(weights_in, 16 * (6 + 6 + 3 + 2 + T))
            for n in range(6):
                last = nc.tensor.transpose(tps[:, n // 4, n % 4 * D:(n % 4 + 1) * D], wraw[:, n, :], k.ident[:, :])
            last.then_inc(transposed, 1)
            for n in range(2):
                for b in range(2):
                    nc.tensor.matmul(hist[:, n, b * 512:(b + 1) * 512], zh[:, 0:P], zh[:, :], start=True, stop=False,
                                     skip_group_check=True)
            with pe.Fori(0, NCH // S) as i:
                for c in range(S):
                    pe.wait_ge(led[c], at(i, "earlier"))
                    for n in range(2):
                        for t in range(T):
                            for q in range(HIQ):
                                last = nc.tensor.matmul(hist[:, n, q * P:(q + 1) * P], hi[c][:, n, t, q * P:(q + 1) * P],
                                                        lo[c][:, n, t, :], start=False, stop=False, skip_group_check=True)
                    last.then_inc(counted[c], 1)


def small_table_phase(nc, tb, hist):
    with ExitStack() as ctx:
        def sb(name, shape, dt):
            return ctx.enter_context(nc.sbuf_tensor(name, shape, dt))
        W = HIQ * P
        val = sb("val", [P, W, 4], F32)
        atl = sb("atl", [P, 2, W], F32)
        root = sb("root", [P, W], F32)
        rroot = sb("rroot", [P, W], F32)
        indb = sb("indb", [P, W], BF16)
        step = ctx.enter_context(nc.semaphore("table_step"))
        stored = ctx.enter_context(nc.semaphore("table_stored"))
        block = ctx.enter_context(nc.Block())

        @block.vector
        def _(dve):
            nc.vector.tensor_scalar(val[:, :, C_IND], hist[:, 0, 0:W], 0.0, None, ALU.is_gt)
            nc.vector.tensor_scalar(indb[:, :], hist[:, 0, 0:W], 0.0, None, ALU.is_gt)
            nc.vector.tensor_scalar(atl[:, 1, :], hist[:, 1, 0:W], 1.0, None, ALU.max)
            nc.vector.tensor_scalar(atl[:, 0, :], hist[:, 0, 0:W], 1.0, None, ALU.max).then_inc(step, 1)
            dve.wait_ge(step, 2)
            nc.vector.reciprocal(val[:, :, C_INVS], atl[:, 0, :])
            nc.vector.reciprocal(val[:, :, C_INVD], atl[:, 1, :])
            nc.vector.reciprocal(rroot[:, :], root[:, :]).then_inc(step, 1)
            dve.wait_ge(step, 3)
            nc.vector.tensor_tensor(val[:, :, C_DIS], rroot[:, :], val[:, :, C_IND], ALU.mult).then_inc(step, 1)

        @block.scalar
        def _(act):
            act.wait_ge(step, 1)
            nc.scalar.activation(root[:, :], atl[:, 0, :], ACT.Sqrt).then_inc(step, 1)
            act.wait_ge(step, 4)
            act.dma_start(tb.small.rearrange("(q h l) k -> h q (l k)", h=P, l=P),
                          val[:, :, :].rearrange("h (q l) k -> h q (l k)", l=P)).then_inc(stored, 16)
            act.dma_start(tb.ind.rearrange("(q h l) -> h q l", h=P, l=P),
                          indb[:, :].rearrange("h (q l) -> h q l", l=P)).then_inc(stored, 16)
            act.wait_ge(stored, 32)


def gather(pool, out, table, idx, t, signal, offset=0, bound=None):
    pool.indirect_dma_start(out, None, table, bass.IndirectOffsetOnAxis(ap=idx[:, t:t + 1], axis=0),
                            element_offset=offset).then_inc(signal, 16)


def add_rows(pool, table, rows, idx, signal, offset=0):
    for t in range(T):
        pool.indirect_dma_start(table, bass.IndirectOffsetOnAxis(ap=idx[:, t:t + 1], axis=0), rows[:, t, :], None,
                                element_offset=offset, compute_op=ALU.add).then_inc(signal, 16)


def phase_tools(ctx, nc, phase):
    sems = []

    def finish():
        nc.clear_and_free_semaphores(sems)
        nc.all_engine_barrier()
    ctx.callback(finish)

    def sb(name, shape, dt):
        return ctx.enter_context(nc.sbuf_tensor(f"{phase}_{name}", shape, dt))

    def sem(name):
        sems.append(nc.alloc_semaphore(f"{phase}_{name}"))
        return sems[-1]

    def banks(name, n):
        return [ctx.enter_context(nc.psum_tensor(f"{phase}_{name}{c}", [P, 512], F32)) for c in range(n)]
    return sb, sem, banks


def chunk_rows(table, i, c):
    return table[DynSlice(i * G + c, 1)].rearrange("c p f -> p c f")


def flat(x):
    return x.rearrange("p t f -> p (t f)")


def first_rows_phase(nc, k, tb, inp):
    with ExitStack() as ctx:
        sb, sem, _ = phase_tools(ctx, nc, "first")
        C = range(GD)
        x = [sb(f"x{c}", [P, T, D], F32) for c in C]
        h = [sb(f"h{c}", [P, T, D], F32) for c in C]
        y = [sb(f"y{c}", [P, T, D], F32) for c in C]
        deg = [sb(f"deg{c}", [P, T, 4], F32) for c in C]
        dis2 = [sb(f"dis2{c}", [P, T], F32) for c in C]
        b = [Norm(sb, f"n{c}", k.ticks) for c in C]
        loaded = [sem(f"loaded{c}") for c in C]
        stored = [sem(f"stored{c}") for c in C]
        done = [sem(f"done{c}") for c in C]
        L = range(G)
        all_idx = sb("all_idx", [P, NCH, 16], I32)
        all_ew = sb("all_ew", [P, NCH, T], F32)
        all_ends = sb("all_ends", [P, NCH, 2, T, 4], F32)
        rec = sb("rec", [P, NCH, 5, T], F32)
        neq = sb("neq", [P, NCH, T], F32)
        prod = sb("prod", [P, 2, NCH, T], F32)
        idx = [sb(f"idx{c}", [P, 2 * T], I32) for c in L]
        ends = [sb(f"ends{c}", [P, 2, T, 4], F32) for c in L]
        all_in, copied, rec_out, weighed = sem("all_in"), sem("copied"), sem("rec_out"), sem("weighed")
        idx_set = [sem(f"idx_set{c}") for c in L]
        ends_in = [sem(f"ends_in{c}") for c in L]
        block = ctx.enter_context(nc.Block())
        order = ln("x_") + ["square", "first"]
        at = counter(order)
        ER = NCH // G

        @block.sync
        def _(sp):
            def load(i, c):
                rows = DynSlice(i * CH + stream_base(c), CH)
                sp.dma_start(x[c][:, :, :], inp["x"][rows, :].rearrange("(p t) f -> p t f", t=T)).then_inc(loaded[c], 16)
                sp.dma_start(deg[c][:, :, :], tb.small[rows, :].rearrange("(p t) k -> p t k", t=T)).then_inc(loaded[c], 16)

            def step(name, i, c):
                if name == "first":
                    rows = DynSlice(i * CH + stream_base(c), CH)
                    sp.wait_ge(done[c], at(i, "end"))
                    sp.dma_start(tb.node3[rows, 0, :].rearrange("(p t) f -> p t f", t=T), y[c][:, :, :]).then_inc(stored[c], 16)
                    if not (isinstance(i, int) and i == NBLK - 1):
                        load(i + 1, c)
            for c in C:
                load(0, c)
            sp.dma_start(all_idx[:, :, :], tb.rec_g.rearrange("c p k -> p c k")).then_inc(all_in, 16)
            sp.dma_start(all_ew[:, :, :], tb.ew.rearrange("(c p t) -> p c t", p=P, t=T)).then_inc(all_in, 16)
            rounds(sp, step, order, GD, NBLK)
            sp.wait_ge(weighed, 4)
            sp.dma_start(tb.rec_f.rearrange("c p f -> p c f"), rec[:, :, :, :].rearrange("p c a t -> p c (a t)")).then_inc(rec_out, 16)
            sp.wait_ge(rec_out, 16)
            for c in C:
                sp.wait_ge(stored[c], NBLK * 16 + 1)

        @block.scalar
        def _(act):
            def step(name, i, c):
                norm_scalar(nc, act, done[c], at, i, "x_", name, b[c], k.eps[:, :], h[c], x[c], ACT.Relu)
            rounds(act, step, order, GD, NBLK)

        @block.vector
        def _(dve):
            start(dve, *done, *stored)

            def edge_weights():
                dve.wait_ge(all_in, 32)
                dve.wait_ge(copied, NCH)
                for n, a in ((0, F_KEYS), (1, F_KEYD)):
                    nc.vector.tensor_copy(rec[:, :, a, :], all_idx[:, :, n * T:(n + 1) * T])
                nc.vector.tensor_copy(rec[:, :, F_INVD, :], all_ends[:, :, 1, :, C_INVD])
                nc.vector.tensor_copy(rec[:, :, F_INVS, :], all_ends[:, :, 0, :, C_INVS])
                nc.vector.tensor_tensor(prod[:, 0, :, :], all_ends[:, :, 0, :, C_DIS], all_ew[:, :, :], ALU.mult).then_inc(weighed, 1)
                dve.wait_ge(weighed, 1)
                nc.vector.tensor_tensor(neq[:, :, :], rec[:, :, F_KEYS, :], rec[:, :, F_KEYD, :], ALU.not_equal).then_inc(weighed, 1)
                nc.vector.tensor_tensor(prod[:, 1, :, :], prod[:, 0, :, :], all_ends[:, :, 1, :, C_DIS], ALU.mult).then_inc(weighed, 1)
                dve.wait_ge(weighed, 3)
                nc.vector.tensor_tensor(rec[:, :, F_W, :], prod[:, 1, :, :], neq[:, :, :], ALU.mult).then_inc(weighed, 1)

            def step(name, i, c):
                if name == "x_stats":
                    dve.wait_ge(loaded[c], (i + 1) * 32)
                norm_vector(nc, dve, done[c], at, i, "x_", name, b[c], x[c])
                if name == "square":
                    dve.wait_ge(done[c], at(i, "square"))
                    nc.vector.tensor_tensor(dis2[c][:, :], deg[c][:, :, C_DIS], deg[c][:, :, C_DIS], ALU.mult).then_inc(done[c], 1)
                if name == "first":
                    dve.wait_ge(stored[c], i * 16 + 1)
                    dve.wait_ge(done[c], at(i, "first"))
                    tiles(lambda t: nc.vector.scalar_tensor_tensor(
                        out=y[c][:, t, :], in0=h[c][:, t, :], scalar=dis2[c][:, t:t + 1], in1=x[c][:, t, :],
                        op0=ALU.mult, op1=ALU.add)).then_inc(done[c], 1)

            rounds(dve, step, order, GD, NBLK)
            edge_weights()

        @block.gpsimd
        def _(pool):
            def look_up(i, c):
                nc.gpsimd.tensor_copy(idx[c][:, :].unsqueeze(1), all_idx[:, DynSlice(i * G + c, 1), 0:2 * T]).then_inc(idx_set[c], 1)
                wait_alone(pool, k.ticks, idx_set[c], i + 1)
                for n in range(2):
                    for t in range(T):
                        gather(pool, ends[c][:, n, t, :], tb.small, idx[c], n * T + t, ends_in[c])

            def keep(i, c):
                pool.wait_ge(ends_in[c], (i + 1) * 2 * T * 16)
                nc.gpsimd.tensor_copy(all_ends[:, DynSlice(i * G + c, 1), :, :, :].rearrange("p c n t k -> p (c n t k)"),
                                      ends[c][:, :, :, :].rearrange("p n t k -> p (n t k)")).then_inc(copied, 1)

            pool.wait_ge(all_in, 32)
            for c in L:
                look_up(0, c)
            with pool.Fori(1, ER) as i:
                for c in L:
                    keep(i - 1, c)
                    pool.wait_ge(copied, (i - 1) * G + c + 1)
                    look_up(i, c)
            for c in L:
                keep(ER - 1, c)

        @block.tensor
        def _(pe):
            pass


class EdgeSide:

    def __init__(self, sb, sem):
        L = range(G)
        self.gidx = [sb(f"gidx{c}", [P, 16], I32) for c in L]
        self.aidx = [sb(f"aidx{c}", [P, 16], I32) for c in L]
        self.rec = [sb(f"rec{c}", [P, 5, T], F32) for c in L]
        self.krow = [sb(f"krow{c}", [P, CH], I32) for c in L]
        self.same = [sb(f"same{c}", [P, T, CH], F32) for c in L]
        self.comb = [sb(f"comb{c}", [P, T, D], F32) for c in L]
        self.gidx_in = [sem(f"gidx_in{c}") for c in L]
        self.aidx_in = [sem(f"aidx_in{c}") for c in L]
        self.rec_in = [sem(f"rec_in{c}") for c in L]
        self.gathered = [sem(f"gathered{c}") for c in L]
        self.done = [sem(f"done{c}") for c in L]
        self.summed = sem("summed")
        self.turns = sem("turns")


def is_last(i):
    return isinstance(i, int) and i == NCH // G - 1


def load_gather_rows(sp, e, tb, i, c):
    sp.dma_start(e.gidx[c][:, :].unsqueeze(1), chunk_rows(tb.rec_g, i, c)).then_inc(e.gidx_in[c], 16)


def load_records(sp, e, tb, key, i, c):
    sp.dma_start(e.rec[c][:, :, :].rearrange("p a t -> p (a t)").unsqueeze(1), chunk_rows(tb.rec_f, i, c)).then_inc(e.rec_in[c], 16)
    sp.dma_start(e.krow[c][:, :], key.rearrange("(c e) -> c e", e=CH)[DynSlice(i * G + c, 1), :].partition_broadcast(P)).then_inc(e.rec_in[c], 16)


def match_keys(nc, dve, e, at, i, c, key, weight):
    dve.wait_ge(e.rec_in[c], (i + 1) * 32)
    dve.wait_ge(e.done[c], at(i, "match"))
    tiles(lambda b: nc.vector.tensor_scalar(e.same[c][:, b, :], e.krow[c][:, :], e.rec[c][:, key, b:b + 1],
                                            e.rec[c][:, weight, b:b + 1], ALU.is_equal, ALU.mult)).then_inc(e.done[c], 1)


def keep_sums(nc, act, e, tb, at, i, c, ps):
    act.wait_ge(e.turns, i * G + c + 1)
    act.dma_start(e.aidx[c][:, :].unsqueeze(1), chunk_rows(tb.rec_a, i, c)).then_inc(e.aidx_in[c], 16)
    act.wait_ge(e.done[c], at(i, "keep"))
    nc.scalar.activation(flat(e.comb[c][:, :, :]), ps[:, :], ACT.Copy).then_inc(e.done[c], 1)


def start_edge_side(dve, e, *sems):
    start(dve, *e.done, *sems)
    dve.sem_inc(e.turns, G - 1)


def pool_program(pool, ticks, e, order, at, gathers, free_step, free, table, group, offset):
    def fetch(i, c):
        wait_alone(pool, ticks, e.gidx_in[c], (i + 1) * 16)
        gathers(c)

    def step(name, i, c):
        if name == free_step and not is_last(i):
            free(i, c)
            fetch(i + 1, c)
        if name == "keep":
            pool.wait_ge(e.aidx_in[c], (i + 1) * 16)
            pool.wait_ge(e.done[c], at(i, "end"))
            if not (isinstance(i, int) and i * G + c == 0):
                pool.wait_ge(e.summed, (i * G + c) * T * 16)
            pool.sem_inc(e.turns, 1)
            add_rows(pool, table, e.comb[c], e.aidx[c][:, group * T:(group + 1) * T], e.summed, offset)

    for c in range(G):
        fetch(0, c)
    rounds(pool, step, order, G, NCH // G)
    pool.wait_ge(e.summed, NCH * T * 16)


def gcn_phase(nc, k, tb, inp, first):
    with ExitStack() as ctx:
        sb, sem, banks = phase_tools(ctx, nc, "gcn" if first else "sage1")
        L = range(G)
        e = EdgeSide(sb, sem)
        x = [sb(f"x{c}", [P, T, D], F32) for c in L]
        h = [sb(f"h{c}", [P, T, D], F32) for c in L]
        sumT = [sb(f"sumT{c}", [P, CH], F32) for c in L]
        b = [Norm(sb, f"n{c}", k.ticks) for c in L]
        kept = [sem(f"kept{c}") for c in L]
        p0, p1 = banks("p0", G), banks("p1", G)
        block = ctx.enter_context(nc.Block())
        order = ln("x_") + (["match", "combine", "keep"] if first else ["match", "combine", "sumT", "apply", "keep"])
        at = counter(order)
        RD = NCH // G
        key, weight, target, offset, krow, group = (F_KEYS, F_W, A_SRC3, 0, tb.src, G_DSTC) if first else \
            (F_KEYD, F_INVD, A_DST3, D, tb.dst, G_SRC3)
        rows3 = tb.node3.rearrange("r k f -> (r k) f")
        source = inp["x"] if first else rows3

        @block.sync
        def _(sp):
            def step(name, i, c):
                if name == "x_mean_var" and not is_last(i):
                    sp.wait_ge(e.gathered[c], (i + 1) * T * 16)
                    load_gather_rows(sp, e, tb, i + 1, c)
                if name == "match" and not first:
                    sp.wait_ge(e.done[c], at(i, "match"))
                    sp.dma_start(chunk_rows(tb.x1s, i, c), flat(x[c][:, :, :]).unsqueeze(1)).then_inc(kept[c], 16)
                    sp.dma_start(chunk_rows(tb.h1s, i, c), flat(h[c][:, :, :]).unsqueeze(1)).then_inc(kept[c], 16)
                if name == "combine" and not is_last(i):
                    sp.wait_ge(e.done[c], at(i, "combine"))
                    load_records(sp, e, tb, krow, i + 1, c)

            for c in L:
                load_gather_rows(sp, e, tb, 0, c)
            for c in L:
                load_records(sp, e, tb, krow, 0, c)
            rounds(sp, step, order, G, RD)
            if not first:
                for c in L:
                    sp.wait_ge(kept[c], RD * 32 + 1)

        @block.gpsimd
        def _(pool):
            def gathers(c):
                for t in range(T):
                    gather(pool, x[c][:, t, :], source, e.gidx[c], group * T + t, e.gathered[c])

            def free(i, c):
                pool.wait_ge(e.done[c], at(i, "match"))
                if not first:
                    pool.wait_ge(kept[c], (i + 1) * 32 + 1)
            pool_program(pool, k.ticks, e, order, at, gathers, "combine", free, rows3, target, offset)

        @block.vector
        def _(dve):
            def step(name, i, c):
                if name == "x_stats":
                    dve.wait_ge(e.gathered[c], (i + 1) * T * 16)
                norm_vector(nc, dve, e.done[c], at, i, "x_", name, b[c], x[c])
                if name == "match":
                    match_keys(nc, dve, e, at, i, c, key, weight)
                if name == "sumT":
                    dve.wait_ge(e.done[c], at(i, "sumT"))
                    nc.vector.tensor_copy(sumT[c][:, :], p0[c][:, :]).then_inc(e.done[c], 1)
            start_edge_side(dve, e, *kept)
            rounds(dve, step, order, G, RD)

        @block.scalar
        def _(act):
            def step(name, i, c):
                if name == "x_norm" and not first:
                    act.wait_ge(kept[c], i * 32 + 1)
                norm_scalar(nc, act, e.done[c], at, i, "x_", name, b[c], k.eps[:, :], h[c], x[c], ACT.Relu)
                if name == "keep":
                    keep_sums(nc, act, e, tb, at, i, c, p0[c] if first else p1[c])
            rounds(act, step, order, G, RD)

        @block.tensor
        def _(pe):
            def step(name, i, c):
                if name == "combine":
                    pe.wait_ge(e.done[c], at(i, "combine"))
                    (combine_rows if first else combine_columns)(nc, p0[c], e.same[c], h[c]).then_inc(e.done[c], 1)
                if name == "apply":
                    pe.wait_ge(e.done[c], at(i, "apply"))
                    apply_columns(nc, p1[c], sumT[c], k.wT[:, 0, :]).then_inc(e.done[c], 1)
            rounds(pe, step, order, G, RD)


def sage2_phase(nc, k, tb):
    with ExitStack() as ctx:
        sb, sem, banks = phase_tools(ctx, nc, "sage2")
        L = range(G)
        e = EdgeSide(sb, sem)
        a = [sb(f"a{c}", [P, T, D], F32) for c in L]
        h = [sb(f"h{c}", [P, T, D], F32) for c in L]
        g = [sb(f"g{c}", [P, T, D], F32) for c in L]
        hT = [sb(f"hT{c}", [P, CH], F32) for c in L]
        h_in = [sem(f"h_in{c}") for c in L]
        kept = [sem(f"kept{c}") for c in L]
        p0, p1 = banks("p0", G), banks("p1", G)
        block = ctx.enter_context(nc.Block())
        order = ["turn", "hT", "mix", "plus", "relu", "match", "combine", "sumT", "apply", "keep"]
        at = counter(order)
        RD = NCH // G
        rows3 = tb.node3.rearrange("r k f -> (r k) f")

        @block.sync
        def _(sp):
            def load_h(i, c):
                sp.dma_start(flat(h[c][:, :, :]).unsqueeze(1), chunk_rows(tb.h1s, i, c)).then_inc(h_in[c], 16)

            def step(name, i, c):
                if name == "mix" and not is_last(i):
                    sp.wait_ge(e.done[c], at(i, "hT"))
                    load_h(i + 1, c)
                    sp.wait_ge(e.gathered[c], (i + 1) * T * 16)
                    load_gather_rows(sp, e, tb, i + 1, c)
                if name == "match":
                    sp.wait_ge(e.done[c], at(i, "match"))
                    sp.dma_start(chunk_rows(tb.g1s, i, c), flat(g[c][:, :, :]).unsqueeze(1)).then_inc(kept[c], 16)
                if name == "combine" and not is_last(i):
                    sp.wait_ge(e.done[c], at(i, "combine"))
                    load_records(sp, e, tb, tb.dst, i + 1, c)

            for c in L:
                load_gather_rows(sp, e, tb, 0, c)
                load_h(0, c)
            for c in L:
                load_records(sp, e, tb, tb.dst, 0, c)
            rounds(sp, step, order, G, RD)
            for c in L:
                sp.wait_ge(kept[c], RD * 16 + 1)

        @block.gpsimd
        def _(pool):
            def gathers(c):
                for t in range(T):
                    gather(pool, a[c][:, t, :], rows3, e.gidx[c], G_SRC3 * T + t, e.gathered[c], D)

            def free(i, c):
                pool.wait_ge(e.done[c], at(i, "relu"))
            pool_program(pool, k.ticks, e, order, at, gathers, "relu", free, rows3, A_DST3, 2 * D)

        @block.vector
        def _(dve):
            def step(name, i, c):
                if name == "plus":
                    dve.wait_ge(kept[c], i * 16 + 1)
                    dve.wait_ge(e.gathered[c], (i + 1) * T * 16)
                    dve.wait_ge(e.done[c], at(i, "plus"))
                    nc.vector.tensor_tensor(flat(g[c][:, :, :]), p1[c][:, :], flat(a[c][:, :, :]), ALU.add).then_inc(e.done[c], 1)
                if name == "match":
                    match_keys(nc, dve, e, at, i, c, F_KEYD, F_INVD)
                if name == "sumT":
                    dve.wait_ge(e.done[c], at(i, "sumT"))
                    nc.vector.tensor_copy(hT[c][:, :], p0[c][:, :]).then_inc(e.done[c], 1)
            start_edge_side(dve, e, *kept)
            rounds(dve, step, order, G, RD)

        @block.scalar
        def _(act):
            def step(name, i, c):
                if name == "hT":
                    act.wait_ge(e.done[c], at(i, "hT"))
                    nc.scalar.activation(hT[c][:, :], p0[c][:, :], ACT.Copy).then_inc(e.done[c], 1)
                if name == "relu":
                    act.wait_ge(e.done[c], at(i, "relu"))
                    nc.scalar.activation(flat(g[c][:, :, :]), flat(g[c][:, :, :]), ACT.Relu).then_inc(e.done[c], 1)
                if name == "keep":
                    keep_sums(nc, act, e, tb, at, i, c, p1[c])
            rounds(act, step, order, G, RD)

        @block.tensor
        def _(pe):
            def step(name, i, c):
                if name == "turn":
                    pe.wait_ge(h_in[c], (i + 1) * 16)
                    pe.wait_ge(e.done[c], at(i, "turn"))
                    transpose4(nc, p0[c], h[c], k.ident[:, :]).then_inc(e.done[c], 1)
                if name == "mix":
                    pe.wait_ge(e.done[c], at(i, "mix"))
                    rows_matmul(nc, p1[c], [(hT[c], k.wT[:, 1, :])],
                                (lambda t: k.ones[:, :], k.brow[:, 0, :])).then_inc(e.done[c], 1)
                if name == "combine":
                    pe.wait_ge(e.done[c], at(i, "combine"))
                    combine_columns(nc, p0[c], e.same[c], g[c]).then_inc(e.done[c], 1)
                if name == "apply":
                    pe.wait_ge(e.done[c], at(i, "apply"))
                    apply_columns(nc, p1[c], hT[c], k.wT[:, 2, :]).then_inc(e.done[c], 1)
            rounds(pe, step, order, G, RD)


def edge_mlp_phase(nc, k, tb):
    with ExitStack() as ctx:
        sb, sem, banks = phase_tools(ctx, nc, "mlp")
        L = range(G)
        e = EdgeSide(sb, sem)

        def each(name, shape):
            return [sb(f"{name}{c}", shape, F32) for c in L]
        a2, gs, xs, v, h, x2d, h2d = (each(n, [P, T, D]) for n in ("a2", "gs", "xs", "v", "h", "x2d", "h2d"))
        w3 = each("w3", [P, T, 3 * D])
        col, srcT, dstT = (each(n, [P, CH]) for n in ("col", "srcT", "dstT"))
        ea, eaT = each("ea", [P, P]), each("eaT", [P, P])
        b = [Norm(sb, f"n{c}", k.ticks) for c in L]
        side_in = [sem(f"side_in{c}") for c in L]
        ea_in = [sem(f"ea_in{c}") for c in L]
        kept = [sem(f"kept{c}") for c in L]
        ea_zero = sem("ea_zero")
        p0, p1 = banks("p0", G), banks("p1", G)
        block = ctx.enter_context(nc.Block())
        order = (["turn_g", "gT", "mix_s", "plus_s", "x2s"] + ln("s_") + ["turn_s", "srcT"]
                 + ln("d_") + ["turn_d", "hT", "mix_d", "relu_d", "mix2_d", "plus_d", "x2d"] + ln("e_")
                 + ["turn_e", "dstT", "turn_ea", "eaT", "hidden", "relu_m", "message", "msg",
                    "match", "combine", "sumT", "apply", "keep"])
        at = counter(order)
        RD = NCH // G
        rows3 = tb.node3.rearrange("r k f -> (r k) f")
        whole = tb.node3.rearrange("r k f -> r (k f)")

        @block.sync
        def _(sp):
            def load_side(i, c):
                sp.dma_start(flat(gs[c][:, :, :]).unsqueeze(1), chunk_rows(tb.g1s, i, c)).then_inc(side_in[c], 16)
                sp.dma_start(flat(xs[c][:, :, :]).unsqueeze(1), chunk_rows(tb.x1s, i, c)).then_inc(side_in[c], 16)

            def load_ea(i, c):
                sp.dma_start(ea[c][:, 0:2 * T].unsqueeze(1),
                             chunk_rows(tb.ea.rearrange("(c p t) k -> c p (t k)", p=P, t=T), i, c)).then_inc(ea_in[c], 16)

            def step(name, i, c):
                if name == "s_stats" and not is_last(i):
                    sp.wait_ge(e.gathered[c], (i + 1) * 2 * T * 16)
                    load_gather_rows(sp, e, tb, i + 1, c)
                    sp.wait_ge(e.done[c], at(i, "s_stats"))
                    load_side(i + 1, c)
                if name == "turn_e":
                    sp.wait_ge(e.done[c], at(i, "turn_e"))
                    sp.dma_start(chunk_rows(tb.x2d, i, c), flat(x2d[c][:, :, :]).unsqueeze(1)).then_inc(kept[c], 16)
                    sp.dma_start(chunk_rows(tb.h2d, i, c), flat(h2d[c][:, :, :]).unsqueeze(1)).then_inc(kept[c], 16)
                if name == "combine" and not is_last(i):
                    sp.wait_ge(e.done[c], at(i, "combine"))
                    load_ea(i + 1, c)
                    load_records(sp, e, tb, tb.dst, i + 1, c)

            sp.wait_ge(ea_zero, 1)
            for c in L:
                load_gather_rows(sp, e, tb, 0, c)
                load_side(0, c)
            for c in L:
                load_ea(0, c)
                load_records(sp, e, tb, tb.dst, 0, c)
            rounds(sp, step, order, G, RD)
            for c in L:
                sp.wait_ge(kept[c], RD * 32 + 1)

        @block.gpsimd
        def _(pool):
            for c in L:
                last = nc.gpsimd.memset(ea[c][:, :], 0.0)
            last.then_inc(ea_zero, 1)

            def gathers(c):
                for t in range(T):
                    gather(pool, a2[c][:, t, :], rows3, e.gidx[c], G_SRC3 * T + t, e.gathered[c], 2 * D)
                for t in range(T):
                    gather(pool, w3[c][:, t, :], whole, e.gidx[c], G_DST * T + t, e.gathered[c])

            def free(i, c):
                pool.wait_ge(e.done[c], at(i, "e_stats"))
            pool_program(pool, k.ticks, e, order, at, gathers, "e_stats", free, tb.sum3, A_DST, 0)

        @block.vector
        def _(dve):
            def step(name, i, c):
                if name == "plus_s":
                    dve.wait_ge(e.gathered[c], (i + 1) * 2 * T * 16)
                    dve.wait_ge(e.done[c], at(i, "plus_s"))
                    nc.vector.tensor_tensor(flat(v[c][:, :, :]), p1[c][:, :], flat(a2[c][:, :, :]), ALU.add).then_inc(e.done[c], 1)
                if name == "x2s":
                    dve.wait_ge(e.done[c], at(i, "x2s"))
                    nc.vector.scalar_tensor_tensor(out=flat(v[c][:, :, :]), in0=flat(v[c][:, :, :]), scalar=0.0,
                                                   in1=flat(xs[c][:, :, :]), op0=ALU.max, op1=ALU.add).then_inc(e.done[c], 1)
                norm_vector(nc, dve, e.done[c], at, i, "s_", name, b[c], v[c])
                norm_vector(nc, dve, e.done[c], at, i, "d_", name, b[c], w3[c][:, :, 0:D])
                if name == "plus_d":
                    dve.wait_ge(kept[c], i * 32 + 1)
                    dve.wait_ge(e.done[c], at(i, "plus_d"))
                    nc.vector.tensor_tensor(x2d[c][:, :, :], p0[c][:, :].rearrange("p (t f) -> p t f", f=D),
                                            w3[c][:, :, 2 * D:3 * D], ALU.add).then_inc(e.done[c], 1)
                if name == "x2d":
                    dve.wait_ge(e.done[c], at(i, "x2d"))
                    nc.vector.scalar_tensor_tensor(out=x2d[c][:, :, :], in0=x2d[c][:, :, :], scalar=0.0,
                                                   in1=w3[c][:, :, 0:D], op0=ALU.max, op1=ALU.add).then_inc(e.done[c], 1)
                norm_vector(nc, dve, e.done[c], at, i, "e_", name, b[c], x2d[c])
                if name == "eaT":
                    dve.wait_ge(e.done[c], at(i, "eaT"))
                    nc.vector.tensor_copy(eaT[c][:, :], p0[c][:, 0:P]).then_inc(e.done[c], 1)
                if name == "msg":
                    dve.wait_ge(e.done[c], at(i, "msg"))
                    nc.vector.tensor_copy(flat(v[c][:, :, :]), p0[c][:, :]).then_inc(e.done[c], 1)
                if name == "match":
                    match_keys(nc, dve, e, at, i, c, F_KEYD, F_INVD)
                if name == "sumT":
                    dve.wait_ge(e.done[c], at(i, "sumT"))
                    nc.vector.tensor_copy(col[c][:, :], p1[c][:, :]).then_inc(e.done[c], 1)
            start_edge_side(dve, e, *kept)
            rounds(dve, step, order, G, RD)

        @block.scalar
        def _(act):
            def step(name, i, c):
                copies = {"gT": (col[c], p0[c]), "srcT": (srcT[c], p0[c]), "hT": (col[c], p0[c]), "dstT": (dstT[c], p1[c])}
                if name in copies:
                    act.wait_ge(e.done[c], at(i, name))
                    nc.scalar.activation(copies[name][0][:, :], copies[name][1][:, :], ACT.Copy).then_inc(e.done[c], 1)
                if name == "relu_d":
                    act.wait_ge(e.done[c], at(i, "relu_d"))
                    nc.scalar.activation(col[c][:, :], p1[c][:, :], ACT.Relu, bias=k.bcol[:, 0:1]).then_inc(e.done[c], 1)
                if name == "relu_m":
                    act.wait_ge(e.done[c], at(i, "relu_m"))
                    nc.scalar.activation(col[c][:, :], p1[c][:, :], ACT.Relu, bias=k.bcol[:, 1:2]).then_inc(e.done[c], 1)
                norm_scalar(nc, act, e.done[c], at, i, "s_", name, b[c], k.eps[:, :], h[c], v[c], ACT.Relu)
                norm_scalar(nc, act, e.done[c], at, i, "d_", name, b[c], k.eps[:, :], h[c], w3[c][:, :, 0:D], ACT.Relu)
                norm_scalar(nc, act, e.done[c], at, i, "e_", name, b[c], k.eps[:, :], h2d[c], x2d[c], ACT.Relu)
                if name == "keep":
                    keep_sums(nc, act, e, tb, at, i, c, p0[c])
            rounds(act, step, order, G, RD)

        @block.tensor
        def _(pe):
            def step(name, i, c):
                if name == "turn_g":
                    pe.wait_ge(side_in[c], (i + 1) * 32)
                if name == "turn_ea":
                    pe.wait_ge(ea_in[c], (i + 1) * 16)
                turns = {"turn_g": (p0[c], gs[c]), "turn_s": (p0[c], h[c]), "turn_d": (p0[c], h[c]), "turn_e": (p1[c], h2d[c])}
                if name in turns:
                    pe.wait_ge(e.done[c], at(i, name))
                    transpose4(nc, turns[name][0], turns[name][1], k.ident[:, :]).then_inc(e.done[c], 1)
                if name == "mix_s":
                    pe.wait_ge(e.done[c], at(i, "mix_s"))
                    rows_matmul(nc, p1[c], [(col[c], k.wT[:, 3, :])],
                                (lambda t: k.ones[:, :], k.brow[:, 1, :])).then_inc(e.done[c], 1)
                if name == "mix_d":
                    pe.wait_ge(e.gathered[c], (i + 1) * 2 * T * 16)
                    pe.wait_ge(e.done[c], at(i, "mix_d"))
                    columns_plus(nc, p1[c], k.wT[:, 1, :], col[c], w3[c][:, :, D:2 * D], k.ident[:, :]).then_inc(e.done[c], 1)
                if name == "mix2_d":
                    pe.wait_ge(e.done[c], at(i, "mix2_d"))
                    rows_matmul(nc, p0[c], [(col[c], k.wT[:, 3, :])],
                                (lambda t: k.ones[:, :], k.brow[:, 1, :])).then_inc(e.done[c], 1)
                if name == "turn_ea":
                    pe.wait_ge(e.done[c], at(i, "turn_ea"))
                    nc.tensor.transpose(p0[c][:, 0:P], ea[c][:, :], k.ident[:, :]).then_inc(e.done[c], 1)
                if name == "hidden":
                    pe.wait_ge(e.done[c], at(i, "hidden"))
                    for t in range(T):
                        o = p1[c][:, t * P:(t + 1) * P]
                        nc.tensor.matmul(o, k.wD[:, 0, :], srcT[c][:, t * P:(t + 1) * P], start=True, stop=False)
                        nc.tensor.matmul(o, k.wD[:, 1, :], dstT[c][:, t * P:(t + 1) * P], start=False, stop=False)
                        last = nc.tensor.matmul(o, k.wC[:, t, :], eaT[c][:, :], start=False, stop=True)
                    last.then_inc(e.done[c], 1)
                if name == "message":
                    pe.wait_ge(e.done[c], at(i, "message"))
                    rows_matmul(nc, p0[c], [(col[c], k.wD[:, 2, :])],
                                (lambda t: k.ones[:, :], k.brow[:, 2, :])).then_inc(e.done[c], 1)
                if name == "combine":
                    pe.wait_ge(e.done[c], at(i, "combine"))
                    combine_columns(nc, p1[c], e.same[c], v[c]).then_inc(e.done[c], 1)
                if name == "apply":
                    pe.wait_ge(e.done[c], at(i, "apply"))
                    apply_columns(nc, p0[c], col[c], k.wD[:, 4, :]).then_inc(e.done[c], 1)
            rounds(pe, step, order, G, RD)


def update_matmuls(nc, pe, k, done, at, i, name, h2, s3, hT, uT, pa, pb):
    if name == "turn_u":
        pe.wait_ge(done, at(i, "turn_u"))
        transpose4(nc, pa, h2, k.ident[:, :]).then_inc(done, 1)
    if name == "mix_u":
        pe.wait_ge(done, at(i, "mix_u"))
        columns_plus(nc, pb, k.wD[:, 3, :], hT, s3, k.ident[:, :]).then_inc(done, 1)
    if name == "mix_u2":
        pe.wait_ge(done, at(i, "mix_u2"))
        rows_matmul(nc, pa, [(uT, k.wD[:, 5, :])], (lambda t: k.ones[:, :], k.brow[:, 3, :])).then_inc(done, 1)


def update_scalar(nc, act, k, done, at, i, name, hT, uT, pa, pb):
    if name == "uhT":
        act.wait_ge(done, at(i, "uhT"))
        nc.scalar.activation(hT[:, :], pa[:, :], ACT.Copy).then_inc(done, 1)
    if name == "relu_u":
        act.wait_ge(done, at(i, "relu_u"))
        nc.scalar.activation(uT[:, :], pb[:, :], ACT.Relu, bias=k.bcol[:, 2:3]).then_inc(done, 1)


def update_vector(nc, dve, k, done, at, i, name, pa, h2, y, x2b):
    if name == "res":
        dve.wait_ge(done, at(i, "res"))
        nc.vector.tensor_tensor(flat(y[:, :, :]), pa[:, :], flat(h2[:, :, :]), ALU.add).then_inc(done, 1)
    if name == "gamma":
        dve.wait_ge(done, at(i, "gamma"))
        nc.vector.tensor_tensor(y[:, :, :], y[:, :, :], k.gamma[:, :].unsqueeze(1).to_broadcast([P, T, D]), ALU.mult).then_inc(done, 1)
    if name == "addx":
        dve.wait_ge(done, at(i, "addx"))
        nc.vector.tensor_tensor(flat(y[:, :, :]), flat(y[:, :, :]), flat(x2b[:, :, :]), ALU.add).then_inc(done, 1)


UPDATE = ["turn_u", "uhT", "mix_u", "relu_u", "mix_u2", "res"] + ln("t_") + ["gamma", "addx"]


def mean_phase(nc, k, tb):
    with ExitStack() as ctx:
        sb, sem, banks = phase_tools(ctx, nc, "mean")
        L = range(G)
        e = EdgeSide(sb, sem)

        def each(name, shape):
            return [sb(f"{name}{c}", shape, F32) for c in L]
        s3, x2, h2, y, h3 = (each(n, [P, T, D]) for n in ("s3", "x2", "h2", "y", "h3"))
        hT, uT = each("hT", [P, CH]), each("uT", [P, CH])
        b = [Norm(sb, f"n{c}", k.ticks) for c in L]
        side_in = [sem(f"side_in{c}") for c in L]
        p0, p1 = banks("p0", G), banks("p1", G)
        block = ctx.enter_context(nc.Block())
        order = ["beta"] + UPDATE + ln("h3_") + ["match", "combine", "sumT", "apply", "keep"]
        at = counter(order)
        RD = NCH // G

        @block.sync
        def _(sp):
            def load_side(i, c):
                sp.dma_start(flat(x2[c][:, :, :]).unsqueeze(1), chunk_rows(tb.x2d, i, c)).then_inc(side_in[c], 16)
                sp.dma_start(flat(h2[c][:, :, :]).unsqueeze(1), chunk_rows(tb.h2d, i, c)).then_inc(side_in[c], 16)

            def step(name, i, c):
                if name == "t_stats" and not is_last(i):
                    sp.wait_ge(e.gathered[c], (i + 1) * T * 16)
                    load_gather_rows(sp, e, tb, i + 1, c)
                if name == "h3_stats" and not is_last(i):
                    sp.wait_ge(e.done[c], at(i, "h3_stats"))
                    load_side(i + 1, c)
                if name == "combine" and not is_last(i):
                    sp.wait_ge(e.done[c], at(i, "combine"))
                    load_records(sp, e, tb, tb.src, i + 1, c)

            for c in L:
                load_gather_rows(sp, e, tb, 0, c)
                load_side(0, c)
            for c in L:
                load_records(sp, e, tb, tb.src, 0, c)
            rounds(sp, step, order, G, RD)

        @block.gpsimd
        def _(pool):
            def gathers(c):
                for t in range(T):
                    gather(pool, s3[c][:, t, :], tb.sum3, e.gidx[c], G_DST * T + t, e.gathered[c])

            def free(i, c):
                pool.wait_ge(e.done[c], at(i, "relu_u"))
            pool_program(pool, k.ticks, e, order, at, gathers, "mix_u2", free, tb.sum4, A_SRC, 0)

        @block.vector
        def _(dve):
            def step(name, i, c):
                if name == "beta":
                    dve.wait_ge(side_in[c], (i + 1) * 32)
                    dve.wait_ge(e.done[c], at(i, "beta"))
                    nc.vector.tensor_tensor(x2[c][:, :, :], x2[c][:, :, :], k.beta[:, :].unsqueeze(1).to_broadcast([P, T, D]),
                                            ALU.add).then_inc(e.done[c], 1)
                update_vector(nc, dve, k, e.done[c], at, i, name, p0[c], h2[c], y[c], x2[c])
                norm_vector(nc, dve, e.done[c], at, i, "t_", name, b[c], y[c])
                norm_vector(nc, dve, e.done[c], at, i, "h3_", name, b[c], y[c])
                if name == "match":
                    match_keys(nc, dve, e, at, i, c, F_KEYS, F_INVS)
                if name == "sumT":
                    dve.wait_ge(e.done[c], at(i, "sumT"))
                    nc.vector.tensor_copy(hT[c][:, :], p0[c][:, :]).then_inc(e.done[c], 1)
            start_edge_side(dve, e)
            rounds(dve, step, order, G, RD)

        @block.scalar
        def _(act):
            def step(name, i, c):
                update_scalar(nc, act, k, e.done[c], at, i, name, hT[c], uT[c], p0[c], p1[c])
                norm_scalar(nc, act, e.done[c], at, i, "t_", name, b[c], k.eps[:, :], y[c], y[c], ACT.Identity)
                norm_scalar(nc, act, e.done[c], at, i, "h3_", name, b[c], k.eps[:, :], h3[c], y[c], ACT.Relu)
                if name == "keep":
                    keep_sums(nc, act, e, tb, at, i, c, p1[c])
            rounds(act, step, order, G, RD)

        @block.tensor
        def _(pe):
            def step(name, i, c):
                if name == "turn_u":
                    pe.wait_ge(side_in[c], (i + 1) * 32)
                if name == "mix_u":
                    pe.wait_ge(e.gathered[c], (i + 1) * T * 16)
                update_matmuls(nc, pe, k, e.done[c], at, i, name, h2[c], s3[c], hT[c], uT[c], p0[c], p1[c])
                if name == "combine":
                    pe.wait_ge(e.done[c], at(i, "combine"))
                    combine_columns(nc, p0[c], e.same[c], h3[c]).then_inc(e.done[c], 1)
                if name == "apply":
                    pe.wait_ge(e.done[c], at(i, "apply"))
                    apply_columns(nc, p1[c], hT[c], k.wT[:, 5, :]).then_inc(e.done[c], 1)
            rounds(pe, step, order, G, RD)


def node_phase(nc, k, tb, out):
    with ExitStack() as ctx:
        sb, sem, banks = phase_tools(ctx, nc, "node")
        C = range(GD)

        def each(name, shape):
            return [sb(f"{name}{c}", shape, F32) for c in C]
        w3 = each("w3", [P, T, 3 * D])
        s3, s4, h, x2, x2b, y, o = (each(n, [P, T, D]) for n in ("s3", "s4", "h", "x2", "x2b", "y", "o"))
        hT, gT = each("hT", [P, CH]), each("gT", [P, CH])
        ind = [sb(f"ind{c}", [P, CH], BF16) for c in C]
        b = [Norm(sb, f"n{c}", k.ticks) for c in C]
        loaded = [sem(f"loaded{c}") for c in C]
        stored = [sem(f"stored{c}") for c in C]
        done = [sem(f"done{c}") for c in C]
        ind_set = sem("ind_set")
        pa, pb = banks("pa", GD), banks("pb", GD)
        block = ctx.enter_context(nc.Block())
        order = (ln("h1_") + ["turn", "hT", "mix", "relu", "mix2", "plus2", "x2", "beta"] + ln("h2_") + UPDATE
                 + ln("h3_") + ["turn3", "h3T", "mix3", "plus4", "out"])
        at = counter(order)

        @block.sync
        def _(sp):
            sp.wait_ge(ind_set, 2)

            def load(i, c):
                rows = DynSlice(i * CH + stream_base(c), CH)
                sp.dma_start(w3[c][:, :, :], tb.node3[rows].rearrange("(p t) k f -> p t (k f)", t=T)).then_inc(loaded[c], 16)
                sp.dma_start(s3[c][:, :, :], tb.sum3[rows].rearrange("(p t) f -> p t f", t=T)).then_inc(loaded[c], 16)
                sp.dma_start(s4[c][:, :, :], tb.sum4[rows].rearrange("(p t) f -> p t f", t=T)).then_inc(loaded[c], 16)
                sp.dma_start(ind[c][3:6, :], tb.ind[rows].partition_broadcast(3)).then_inc(loaded[c], 16)

            def step(name, i, c):
                if name == "out":
                    rows = DynSlice(i * CH + stream_base(c), CH)
                    sp.wait_ge(done[c], at(i, "out"))
                    if not (isinstance(i, int) and i == NBLK - 1):
                        load(i + 1, c)
                    sp.wait_ge(done[c], at(i, "end"))
                    sp.dma_start(out[rows].rearrange("(p t) f -> p t f", t=T), o[c][:, :, :]).then_inc(stored[c], 16)

            for c in C:
                load(0, c)
            rounds(sp, step, order, GD, NBLK)
            for c in C:
                sp.wait_ge(stored[c], NBLK * 16 + 1)

        @block.gpsimd
        def _(pool):
            for c in C:
                last = nc.gpsimd.memset(ind[c][:, :], 0.0)
            last.then_inc(ind_set, 1)
            pool.wait_ge(ind_set, 1)
            for c in C:
                last = nc.gpsimd.memset(ind[c][0:3, :], 1.0)
            last.then_inc(ind_set, 1)

            def step(name, i, c):
                if name == "beta":
                    pool.wait_ge(done[c], at(i, "beta"))
                    nc.gpsimd.tensor_tensor(x2b[c][:, :, :], x2[c][:, :, :], k.beta[:, :].unsqueeze(1).to_broadcast([P, T, D]),
                                            ALU.add).then_inc(done[c], 1)
            rounds(pool, step, order, GD, NBLK)

        @block.vector
        def _(dve):
            def step(name, i, c):
                if name == "h1_stats":
                    dve.wait_ge(loaded[c], (i + 1) * 64)
                norm_vector(nc, dve, done[c], at, i, "h1_", name, b[c], w3[c][:, :, 0:D])
                if name == "plus2":
                    dve.wait_ge(done[c], at(i, "plus2"))
                    nc.vector.tensor_tensor(x2[c][:, :, :], pa[c][:, :].rearrange("p (t f) -> p t f", f=D),
                                            w3[c][:, :, 2 * D:3 * D], ALU.add).then_inc(done[c], 1)
                if name == "x2":
                    dve.wait_ge(done[c], at(i, "x2"))
                    nc.vector.scalar_tensor_tensor(out=x2[c][:, :, :], in0=x2[c][:, :, :], scalar=0.0,
                                                   in1=w3[c][:, :, 0:D], op0=ALU.max, op1=ALU.add).then_inc(done[c], 1)
                norm_vector(nc, dve, done[c], at, i, "h2_", name, b[c], x2[c])
                update_vector(nc, dve, k, done[c], at, i, name, pa[c], h[c], y[c], x2b[c])
                norm_vector(nc, dve, done[c], at, i, "t_", name, b[c], y[c])
                norm_vector(nc, dve, done[c], at, i, "h3_", name, b[c], y[c])
                if name == "plus4":
                    dve.wait_ge(stored[c], i * 16 + 1)
                    dve.wait_ge(done[c], at(i, "plus4"))
                    nc.vector.tensor_tensor(flat(o[c][:, :, :]), pb[c][:, :], flat(s4[c][:, :, :]), ALU.add).then_inc(done[c], 1)
                if name == "out":
                    dve.wait_ge(done[c], at(i, "out"))
                    nc.vector.scalar_tensor_tensor(out=flat(o[c][:, :, :]), in0=flat(o[c][:, :, :]), scalar=0.0,
                                                   in1=flat(y[c][:, :, :]), op0=ALU.max, op1=ALU.add).then_inc(done[c], 1)
            start(dve, *done, *stored)
            rounds(dve, step, order, GD, NBLK)

        @block.scalar
        def _(act):
            def step(name, i, c):
                norm_scalar(nc, act, done[c], at, i, "h1_", name, b[c], k.eps[:, :], h[c], w3[c][:, :, 0:D], ACT.Relu)
                norm_scalar(nc, act, done[c], at, i, "h2_", name, b[c], k.eps[:, :], h[c], x2[c], ACT.Relu)
                norm_scalar(nc, act, done[c], at, i, "t_", name, b[c], k.eps[:, :], y[c], y[c], ACT.Identity)
                norm_scalar(nc, act, done[c], at, i, "h3_", name, b[c], k.eps[:, :], h[c], y[c], ACT.Relu)
                update_scalar(nc, act, k, done[c], at, i, name, hT[c], gT[c], pa[c], pb[c])
                if name in ("hT", "h3T"):
                    act.wait_ge(done[c], at(i, name))
                    nc.scalar.activation(hT[c][:, :], pa[c][:, :], ACT.Copy).then_inc(done[c], 1)
                if name == "relu":
                    act.wait_ge(done[c], at(i, "relu"))
                    nc.scalar.activation(gT[c][:, :], pb[c][:, :], ACT.Relu, bias=k.bcol[:, 0:1]).then_inc(done[c], 1)
            rounds(act, step, order, GD, NBLK)

        @block.tensor
        def _(pe):
            def step(name, i, c):
                if name in ("turn", "turn3"):
                    pe.wait_ge(done[c], at(i, name))
                    transpose4(nc, pa[c], h[c], k.ident[:, :]).then_inc(done[c], 1)
                if name == "mix":
                    pe.wait_ge(done[c], at(i, "mix"))
                    columns_plus(nc, pb[c], k.wT[:, 1, :], hT[c], w3[c][:, :, D:2 * D], k.ident[:, :]).then_inc(done[c], 1)
                if name == "mix2":
                    pe.wait_ge(done[c], at(i, "mix2"))
                    rows_matmul(nc, pa[c], [(gT[c], k.wT[:, 3, :])],
                                (lambda t: k.ones[:, :], k.brow[:, 1, :])).then_inc(done[c], 1)
                update_matmuls(nc, pe, k, done[c], at, i, name, h[c], s3[c], hT[c], gT[c], pa[c], pb[c])
                if name == "mix3":
                    pe.wait_ge(done[c], at(i, "mix3"))
                    rows_matmul(nc, pb[c], [(hT[c], k.wT[:, 4, :])],
                                (lambda t: ind[c][:, t:CH:T], k.brow[:, 4, :])).then_inc(done[c], 1)
            rounds(pe, step, order, GD, NBLK)


def gnn_program(nc, inp, out):
    tb = Tables(nc)
    with ExitStack() as ctx:
        k = Consts(lambda name, shape, dt: ctx.enter_context(nc.sbuf_tensor(name, shape, dt)),
                   ctx.enter_context(nc.semaphore("ticks")))
        with nc.psum_tensor("hist", [P, 2, 1024], F32) as hist:
            setup_phase(nc, k, tb, inp, hist)
            small_table_phase(nc, tb, hist)
        first_rows_phase(nc, k, tb, inp)
        gcn_phase(nc, k, tb, inp, True)
        gcn_phase(nc, k, tb, inp, False)
        sage2_phase(nc, k, tb)
        edge_mlp_phase(nc, k, tb)
        mean_phase(nc, k, tb)
        node_phase(nc, k, tb, out)


_INS = ["x", "src", "dst", "edge_attr_2", "edge_weight", "L1_gnn_W1_l", "L1_gnn_W1_r", "L1_gnn_b1", "L1_gnn_W2_l",
        "L1_gnn_W2_r", "L1_gnn_b2", "L2_gnn_mW1", "L2_gnn_mb1", "L2_gnn_mW2", "L2_gnn_mb2", "L2_gnn_uW1", "L2_gnn_ub1",
        "L2_gnn_uW2", "L2_gnn_ub2", "L2_gnn_gamma", "L2_gnn_beta", "L3_gnn_W_self", "L3_gnn_b_self",
        "L3_gnn_W_neighbor", "L3_gnn_b_neighbor"]


def kernel(**inputs):
    import numpy as _np
    import concourse.bacc as _bacc
    from concourse import mybir as _mybir
    from concourse.bass_utils import run_bass_kernel_spmd as _run

    nc = _bacc.Bacc("TRN2", target_bir_lowering=False, num_devices=1)
    arrays, inp = {}, {}
    for name in _INS:
        a = _np.ascontiguousarray(inputs[name])
        arrays["in_" + name] = a
        inp[name] = nc.dram_tensor("in_" + name, a.shape, _mybir.dt.from_np(a.dtype), kind="ExternalInput").ap()
    out = nc.dram_tensor("out_0", (N, D), F32, kind="ExternalOutput").ap()
    gnn_program(nc, inp, out)
    r = _run(nc, [arrays], core_ids=[0])
    return r.results[0]["out_0"]
```

```python
import concourse.bass as bass
from concourse import mybir
from concourse.bass import DynSlice
from contextlib import ExitStack

F32, I32 = mybir.dt.float32, mybir.dt.int32
BF16, F16 = mybir.dt.bfloat16, mybir.dt.float16
ALU = mybir.AluOpType
ACT = mybir.ActivationFunctionType

N, E, D = 100000, 25000, 128
P = 128
T = 4
CH = P * T
G = 5
NCH = -(-E // (G * CH)) * G
EP = NCH * CH
PAD = EP - E
HIQ = -(-(N + PAD) // (P * P))
NT = HIQ * P * P
DUMP = -(-(N + PAD) // P) * P
R = -(-(DUMP + CH) // (P * NCH)) * P * NCH
ZR = R // (P * NCH)
S = 2
GF = 8
GD = 8
EPS = 1e-5

C_DIS, C_INVS, C_INVD, C_IND = range(4)
G_SRC, G_DST, G_SRC3, G_DSTC = range(4)
A_SRC3, A_DST3, A_DST, A_SRC = range(4)
F_KEYS, F_KEYD, F_W, F_INVD, F_INVS = range(5)


def blocks(streams):
    return -(-N // (CH * streams))


def stream_base(c, streams=GD):
    return c * (N - blocks(streams) * CH) // (streams - 1)


VECTOR, SCALAR, TENSOR, GPSIMD = "vector", "scalar", "tensor", "gpsimd"
LENGTH = {"stats": (VECTOR, 810), "mean_var": (VECTOR, 300), "std": (SCALAR, 190), "rstd": (VECTOR, 94),
          "shift": (VECTOR, 73), "norm": (SCALAR, 1550), "h1_norm": (VECTOR, 1030), "square": (VECTOR, 73), "scale": (VECTOR, 73), "first": (VECTOR, 600),
          "hidden": (TENSOR, 2600), "eaT": (VECTOR, 200), "match": (VECTOR, 1830), "combine": (TENSOR, 3400)}
LENGTH.update({n: (SCALAR, 500) for n in ("hT", "uhT", "h3T", "gT", "srcT", "dstT", "keep")})
LENGTH.update({n: (SCALAR, 570) for n in ("relu", "relu_u", "relu_d", "relu_m")})
LENGTH.update({n: (VECTOR, 600) for n in ("plus", "x2", "res", "gamma", "addx", "plus4", "out", "plus_s", "x2s",
                                          "plus_d", "x2d", "msg", "sumT", "beta")})
LENGTH.update({n: (TENSOR, 430) for n in ("turn", "turn_u", "turn3", "turn_g", "turn_s", "turn_d", "turn_e")})
LENGTH.update({n: (TENSOR, 1300) for n in ("mix", "mix_u", "mix_u2", "mix3", "mix_d", "message")})
LENGTH.update({n: (TENSOR, 870) for n in ("apply", "mix_s", "mix2_d")})
LENGTH.update({"mix2": (TENSOR, 1750), "turn_ea": (TENSOR, 110)})
LOAD = "load"
LENGTH["load"] = (LOAD, 5000)
HANDOFF = {LOAD: 0, VECTOR: 150, SCALAR: 300, TENSOR: 220, GPSIMD: 180}


def play(steps, streams, count, pick, slow=1.0):
    free, ready, starts = {}, [0] * streams, {}
    for i, n, c in pick(lambda n, c: max(ready[c], free.get(steps[n][0], 0)), ready, count):
        eng, length, beside = steps[n]
        length *= slow if eng == TENSOR else 1.0
        starts[i, n, c] = now = max(ready[c], free.get(eng, 0))
        if eng != LOAD:
            free[eng] = now + length
        ready[c] = now + length + HANDOFF[eng]
        if beside:
            free[GPSIMD] = max(free.get(GPSIMD, 0), now + length) + beside
    return starts


def stagger(order, streams, elsewhere=None, beside=None):
    steps = []
    for name in order:
        eng, length = (elsewhere or {}).get(name) or LENGTH.get(name) or LENGTH[name.split("_", 1)[1]]
        steps.append((eng, length, (beside or {}).get(name, 0)))
    size, best = len(order), None

    for apart in (0, 1000, 2000, 3000, 5000, 7000, 9000):
        def first_ready(start_of, ready, count):
            ready[:] = [c * apart for c in range(streams)]
            at = [0] * streams
            while min(at) < count * size:
                c = min((c for c in range(streams) if at[c] < count * size),
                        key=lambda c: (start_of(at[c] % size, c), ready[c], c))
                yield at[c] // size, at[c] % size, c
                at[c] += 1
        starts = play(steps, streams, 16, first_ready)
        for r in range(3, 12):
            begin = starts[r, 0, 0]
            period = (starts[15, 0, 0] - begin) / (15 - r)
            plan = []
            for c in range(streams):
                for n in range(size):
                    late, slot = divmod(starts[r, n, c] - begin, period)
                    plan.append((slot, int(late), c, n, order[n]))
            plan.sort()
            if (max(p[1] for p in plan) > 1 or min(p[1] for p in plan) < 0
                    or any(starts[r, size - 1, c] >= starts[r, 0, c] + period for c in range(streams))):
                continue
            ends = [starts[r, size - 1, c] for c in range(streams)]
            if order[-1] == "keep" and (ends != sorted(ends) or ends[-1] >= ends[0] + period):
                continue

            def planned(start_of, ready, count):
                for i in range(count + 1):
                    for _, late, c, n, _ in plan:
                        if 0 <= i - late < count:
                            yield i - late, n, c
            length = 0
            for slow in (1.0, 1.15):
                trial = play(steps, streams, 12, planned, slow)
                length += max(trial[11, size - 1, c] for c in range(streams)) - max(trial[5, size - 1, c] for c in range(streams))
            if best is None or length < best[0]:
                best = (length, plan)
    return best[1]


def rounds(eng, step, plan, n):
    def one_round(i, head=True, tail=True):
        for _, late, c, _, name in plan:
            if late == 0 and head:
                step(name, i, c)
            if late == 1 and tail:
                step(name, i - 1, c)

    one_round(0, tail=False)
    with eng.Fori(1, n - 1) as i:
        one_round(i)
    one_round(n - 1)
    one_round(n, head=False)


def tiles(f):
    for t in range(T):
        last = f(t)
    return last


def counter(order):
    return lambda i, step, n=len(order): i * n + (order + ["end"]).index(step) + 1


def start(eng, *sems):
    for s in sems:
        eng.sem_inc(s, 1)


LN = ["stats", "mean_var", "std", "rstd", "shift", "norm"]


def ln(prefix):
    return [prefix + s for s in LN]


def wait_alone(eng, ticks, sem, value):
    eng.wait_ge(sem, value)
    eng.sem_inc(ticks, 1)


class Norm:

    def __init__(self, sb, name, ticks):
        self.ticks = ticks
        self.st = sb(name + "_stats", [P, T, 6], F32)
        self.mv = sb(name + "_mean_var", [P, T, 2], F32)
        self.sd = sb(name + "_std", [P, T], F32)
        self.rs = sb(name + "_rstd", [P, T], F32)
        self.sh = sb(name + "_shift", [P, T], F32)


def norm_vector(nc, dve, done, at, i, pre, name, b, x):
    if name == pre + "stats":
        dve.wait_ge(done, at(i, name))
        tiles(lambda t: nc.vector.bn_stats(b.st[:, t, :], x[:, t, :])).then_inc(done, 1)
    if name == pre + "mean_var":
        wait_alone(dve, b.ticks, done, at(i, name))
        tiles(lambda t: nc.vector.bn_aggr(b.mv[:, t, :], b.st[:, t, :])).then_inc(done, 1)
    if name == pre + "rstd":
        dve.wait_ge(done, at(i, name))
        nc.vector.reciprocal(b.rs[:, :], b.sd[:, :]).then_inc(done, 1)
    if name == pre + "shift":
        dve.wait_ge(done, at(i, name))
        nc.vector.scalar_tensor_tensor(out=b.sh[:, :], in0=b.mv[:, :, 0], scalar=-1.0, in1=b.rs[:, :],
                                       op0=ALU.mult, op1=ALU.mult).then_inc(done, 1)


def norm_scalar(nc, act, done, at, i, pre, name, b, eps, out, x, func):
    if name == pre + "std":
        act.wait_ge(done, at(i, name))
        nc.scalar.activation(b.sd[:, :], b.mv[:, :, 1], ACT.Sqrt, bias=eps).then_inc(done, 1)
    if name == pre + "norm":
        act.wait_ge(done, at(i, name))
        tiles(lambda t: nc.scalar.activation(out[:, t, :], x[:, t, :], func,
                                             bias=b.sh[:, t:t + 1], scale=b.rs[:, t:t + 1])).then_inc(done, 1)


def transpose4(nc, ps, x, ident):
    return tiles(lambda t: nc.tensor.transpose(ps[:, t * P:(t + 1) * P], x[:, t, :], ident))


def rows_matmul(nc, ps, pairs, bias=None):
    for t in range(T):
        o = ps[:, t * P:(t + 1) * P]
        for n, (xT, w) in enumerate(pairs):
            last = nc.tensor.matmul(o, xT[:, t * P:(t + 1) * P], w, start=(n == 0),
                                    stop=(bias is None and n == len(pairs) - 1))
        if bias is not None:
            last = nc.tensor.matmul(o, bias[0](t), bias[1], start=False, stop=True)
    return last


def columns_plus(nc, ps, w, xT, rows, ident):
    nc.tensor.matmul(ps[:, :], w, xT[:, :], start=True, stop=False)
    return tiles(lambda t: nc.tensor.matmul(ps[:, t * P:(t + 1) * P], rows[:, t, :], ident, is_transpose=True,
                                            start=False, stop=(t == T - 1)))


def combine_rows(nc, ps, same, msg):
    for a in range(T):
        for b in range(T):
            last = nc.tensor.matmul(ps[:, a * P:(a + 1) * P], same[:, b, a:CH:T], msg[:, b, :],
                                    start=(b == 0), stop=(b == T - 1))
    return last


def combine_columns(nc, ps, same, msg):
    return tiles(lambda b: nc.tensor.matmul(ps[:, :], msg[:, b, :], same[:, b, :], start=(b == 0), stop=(b == T - 1)))


def apply_columns(nc, ps, sumT, w):
    return tiles(lambda a: nc.tensor.matmul(ps[:, a * P:(a + 1) * P], sumT[:, a:CH:T], w, start=True, stop=True))


class Tables:

    def __init__(self, nc):
        def dram(name, shape, dt):
            return nc.dram_tensor(name, shape, dt, kind="Internal").ap()
        self.node3 = dram("node3", (R, 3, D), F32)
        self.sum3 = dram("sum3", (R, D), F32)
        self.sum4 = dram("sum4", (R, D), F32)
        self.small = dram("small", (NT, 4), F32)
        self.ind = dram("ind", (NT,), BF16)
        self.src = dram("src_padded", (EP,), I32)
        self.dst = dram("dst_padded", (EP,), I32)
        self.ew = dram("ew_padded", (EP,), F32)
        self.ea = dram("ea_padded", (EP, 2), F32)
        self.rec_g = dram("rec_gather", (NCH, P, 16), I32)
        self.rec_a = dram("rec_add", (NCH, P, 16), I32)
        self.rec_f = dram("rec_float", (NCH, P, 20), F32)
        self.x1s = dram("x1_src", (NCH, P, T * D), F32)
        self.h1s = dram("h1_src", (NCH, P, T * D), F32)
        self.g1s = dram("g1_src", (NCH, P, T * D), F32)
        self.x2d = dram("x2_dst", (NCH, P, T * D), F32)
        self.h2d = dram("h2_dst", (NCH, P, T * D), F32)
        self.split = dram("bias_split", (4, 3, D), BF16)


class Consts:

    def __init__(self, sb, ticks):
        self.ticks = ticks
        self.ident = sb("ident", [P, P], F32)
        self.eps = sb("eps", [P, 1], F32)
        self.wT = sb("wT", [P, 6, D], F32)
        self.wD = sb("wD", [P, 6, D], F32)
        self.wC = sb("wC", [P, T, D], F32)
        self.bcol = sb("bcol", [P, 2], F32)
        self.brow = sb("brow", [P, 3, D], BF16)
        self.b12 = sb("b12", [P, 2, D], F32)
        self.ones = sb("ones", [P, P], BF16)
        self.gamma = sb("gamma", [P, D], F32)
        self.beta = sb("beta", [P, D], F32)


def setup_phase(nc, k, tb, inp, hist):
    with ExitStack() as ctx:
        def sb(name, shape, dt):
            return ctx.enter_context(nc.sbuf_tensor(name, shape, dt))

        def sem(name):
            return ctx.enter_context(nc.semaphore(name))

        zero = sb("zero", [P, 2 * PAD], F32)
        padkey = sb("padkey", [1, PAD], I32)
        wraw = sb("wraw", [P, 6, D], F32)
        brows = sb("brows", [4, D], F32)
        bres = sb("bres", [4, 2, D], F32)
        bsplit = sb("bsplit", [4, 3, D], BF16)
        srcI = sb("srcI", [P, NCH, T], I32)
        dstI = sb("dstI", [P, NCH, T], I32)
        digit = sb("digit", [P, NCH, T], I32)
        parts = sb("parts", [P, NCH, 6 * T], F32)
        counts = sb("counts", [P, NCH, 2 * T], F32)
        spare = sb("spare", [P, NCH, T], F32)
        dup = sb("dup", [P, NCH, T], F32)
        lead = sb("lead", [P, NCH, T], F32)
        recg = sb("recg", [P, NCH, 16], I32)
        reca = sb("reca", [P, NCH, 16], I32)
        iota = sb("iota", [P, HIQ * P], F16)
        earlier = sb("earlier", [P, T, CH], BF16)
        zh = sb("zh", [P, 512], F16)
        part = [sb(f"part{c}", [P, 6 * T], F32) for c in range(S)]
        krow = [sb(f"krow{c}", [P, 2, CH], I32) for c in range(S)]
        hi = [sb(f"hi{c}", [P, 2, T, HIQ * P], F16) for c in range(S)]
        lo = [sb(f"lo{c}", [P, 2, T, P], F16) for c in range(S)]
        junk = [sb(f"junk{c}", [P, 2 * T, CH], BF16) for c in range(S)]
        prev = [sb(f"prev{c}", [P, 2 * T], F32) for c in range(S)]
        tps = ctx.enter_context(nc.psum_tensor("tps", [P, 2, 512], F32))

        zero_set, const_set, cleared, padded = sem("zero_set"), sem("const_set"), sem("cleared"), sem("padded")
        edges_in, weights_in, bias_in, split_out = sem("edges_in"), sem("weights_in"), sem("bias_in"), sem("split_out")
        split_in, recs_out, rows_in, filled = sem("split_in"), sem("recs_out"), sem("rows_in"), sem("filled")
        first_sum = tb.node3[:, 1, :].rearrange("(c p b) f -> c p b f", p=P, b=ZR)
        transposed, linked, weights_ready, memzero = sem("transposed"), sem("linked"), sem("weights_ready"), sem("memzero")
        keys_in = [sem(f"keys_in{c}") for c in range(S)]
        led = [sem(f"led{c}") for c in range(S)]
        counted = [sem(f"counted{c}") for c in range(S)]
        block = ctx.enter_context(nc.Block())
        order = ["pick", "onehots", "earlier", "keep"]
        at = counter(order)

        @block.gpsimd
        def _(pool):
            nc.gpsimd.memset(zero[:, :], 0.0).then_inc(zero_set, 1)
            nc.gpsimd.iota(padkey[:, :], pattern=[[1, PAD]], base=N, channel_multiplier=0).then_inc(zero_set, 1)
            nc.gpsimd.memset(k.ident[:, :], 0.0).then_inc(memzero, 1)
            nc.gpsimd.memset(earlier[:, :, :], 1.0).then_inc(memzero, 1)
            nc.gpsimd.memset(k.wC[:, :, :], 0.0).then_inc(memzero, 1)
            nc.gpsimd.memset(k.brow[:, :, :], 0.0).then_inc(memzero, 1)
            nc.gpsimd.memset(k.ones[:, :], 1.0)
            nc.gpsimd.memset(k.eps[:, :], EPS)
            nc.gpsimd.memset(zh[:, :], 0.0)
            nc.gpsimd.iota(iota[:, :], pattern=[[1, HIQ * P]], base=0, channel_multiplier=0,
                           allow_small_or_imprecise_dtypes=True)
            nc.gpsimd.iota(spare[:, :, :], pattern=[[0, NCH], [1, T]], base=DUMP, channel_multiplier=T,
                           allow_small_or_imprecise_dtypes=True)
            pool.wait_ge(memzero, 2)
            nc.gpsimd.affine_select(out=k.ident[:, :], in_=k.ident[:, :], compare_op=ALU.not_equal, fill=1.0,
                                    base=0, pattern=[[-1, P]], channel_multiplier=1)
            for t in range(T):
                last = nc.gpsimd.affine_select(out=earlier[:, t, :], in_=earlier[:, t, :], compare_op=ALU.is_gt,
                                               fill=0.0, base=t, pattern=[[-1, CH]], channel_multiplier=T)
            last.then_inc(const_set, 1)

        @block.sync
        def _(sp):
            sp.wait_ge(padded, 128)
            sp.wait_ge(rows_in, 32)
            with sp.Fori(0, NCH // S) as i:
                for c in range(S):
                    sp.wait_ge(led[c], at(i, "pick"))
                    for n, key in enumerate((tb.src, tb.dst)):
                        row = key.rearrange("(c e) -> c e", e=CH)[DynSlice(i * S + c, 1), :]
                        sp.dma_start(krow[c][:, n, :], row.partition_broadcast(P)).then_inc(keys_in[c], 16)
                    sp.dma_start(first_sum[DynSlice(i * S + c, 1)].rearrange("c p b f -> (c p) b f"),
                                 k.b12[:, 0, :].unsqueeze(1).to_broadcast([P, ZR, D])).then_inc(filled, 16)
            sp.wait_ge(linked, 9 + 10)
            sp.dma_start(tb.rec_g.rearrange("c p k -> p c k"), recg[:, :, :]).then_inc(recs_out, 16)
            sp.dma_start(tb.rec_a.rearrange("c p k -> p c k"), reca[:, :, :]).then_inc(recs_out, 16)
            sp.wait_ge(recs_out, 32)
            sp.wait_ge(filled, NCH * 16)

        @block.scalar
        def _(act):
            for n, name in enumerate(("L1_gnn_b1", "L1_gnn_b2")):
                act.dma_start(k.b12[:, n, :], inp[name].partition_broadcast(P)).then_inc(rows_in, 16)
            act.wait_ge(zero_set, 2)
            z = zero[0:1, :]
            act.dma_start(tb.src[0:E], inp["src"]).then_inc(padded, 16)
            act.dma_start(tb.dst[0:E], inp["dst"]).then_inc(padded, 16)
            act.dma_start(tb.ew[0:E], inp["edge_weight"]).then_inc(padded, 16)
            act.dma_start(tb.ea[0:E, :], inp["edge_attr_2"]).then_inc(padded, 16)
            act.dma_start(tb.src[E:EP].unsqueeze(0), padkey[:, :]).then_inc(padded, 16)
            act.dma_start(tb.dst[E:EP].unsqueeze(0), padkey[:, :]).then_inc(padded, 16)
            act.dma_start(tb.ew[E:EP].unsqueeze(0), z[:, 0:PAD]).then_inc(padded, 16)
            act.dma_start(tb.ea[E:EP, :].rearrange("e k -> (e k)").unsqueeze(0), z[:, 0:2 * PAD]).then_inc(padded, 16)
            for n, name in enumerate(("L1_gnn_W1_l", "L1_gnn_W1_r", "L1_gnn_W2_l", "L1_gnn_W2_r",
                                      "L3_gnn_W_self", "L3_gnn_W_neighbor")):
                act.dma_start(wraw[:, n, :], inp[name]).then_inc(weights_in, 16)
            for n, name in enumerate(("L2_gnn_mb2", "L2_gnn_ub2", "L3_gnn_b_self", "L3_gnn_b_neighbor")):
                act.dma_start(brows[n:n + 1, :], inp[name].unsqueeze(0)).then_inc(bias_in, 16)
            act.wait_ge(padded, 128)
            act.dma_start(srcI[:, :, :], tb.src.rearrange("(c p t) -> p c t", p=P, t=T)).then_inc(edges_in, 16)
            act.dma_start(dstI[:, :, :], tb.dst.rearrange("(c p t) -> p c t", p=P, t=T)).then_inc(edges_in, 16)
            m = inp["L2_gnn_mW1"]
            u = inp["L2_gnn_uW1"]
            for n, w in enumerate((m[0:D, :], m[D:2 * D, :], inp["L2_gnn_mW2"], u[0:D, :], u[D:2 * D, :],
                                   inp["L2_gnn_uW2"])):
                act.dma_start(k.wD[:, n, :], w).then_inc(weights_in, 16)
            for n, name in enumerate(("L2_gnn_mb1", "L2_gnn_ub1")):
                act.dma_start(k.bcol[:, n:n + 1], inp[name].unsqueeze(1)).then_inc(weights_in, 16)
            act.dma_start(k.gamma[:, :], inp["L2_gnn_gamma"].partition_broadcast(P)).then_inc(weights_in, 16)
            act.dma_start(k.beta[:, :], inp["L2_gnn_beta"].partition_broadcast(P)).then_inc(weights_in, 16)
            act.wait_ge(memzero, 4)
            for t in range(T):
                act.dma_start(k.wC[2 * t:2 * t + 2, t, :], m[2 * D:2 * D + 2, :]).then_inc(weights_in, 16)
            act.dma_start(tb.node3[N:R, 0, :].rearrange("(p b) f -> p b f", p=32),
                          zero[0:32, 0:D].unsqueeze(1).to_broadcast([32, (R - N) // 32, D])).then_inc(cleared, 16)
            act.wait_ge(split_out, 1)
            act.dma_start(tb.split, bsplit[:, :, :]).then_inc(split_in, 16)
            act.wait_ge(split_in, 16)
            act.dma_start(k.brow[0:3, :, :], tb.split[0:3].rearrange("b s f -> s b f")).then_inc(split_in, 16)
            act.dma_start(k.brow[3:6, 2, :], tb.split[3]).then_inc(split_in, 16)
            act.wait_ge(split_in, 48)
            act.wait_ge(weights_in, 16 * (6 + 6 + 2 + 2 + T))
            act.wait_ge(cleared, 16)

        @block.vector
        def _(dve):
            start(dve, *led, *counted)
            links = [0]

            def link(ins):
                links[0] += 1
                ins.then_inc(linked, 1)
                dve.wait_ge(linked, links[0])

            dve.wait_ge(edges_in, 32)
            for n, key in enumerate((srcI, dstI)):
                a = 2 * n * T
                link(nc.vector.tensor_scalar(digit[:, :, :], key[:, :, :], 7, None, ALU.arith_shift_right))
                link(nc.vector.tensor_copy(parts[:, :, a:a + T], digit[:, :, :]))
                link(nc.vector.tensor_scalar(digit[:, :, :], key[:, :, :], P - 1, None, ALU.bitwise_and))
                nc.vector.tensor_copy(parts[:, :, a + T:a + 2 * T], digit[:, :, :])
                link(nc.vector.tensor_copy(parts[:, :, (4 + n) * T:(5 + n) * T], key[:, :, :]))
            assert links[0] == 8
            dve.wait_ge(const_set, 1)
            with dve.Fori(0, NCH // S) as i:
                for c in range(S):
                    dve.wait_ge(led[c], at(i, "pick"))
                    dve.wait_ge(counted[c], i + 1)
                    nc.vector.tensor_copy(part[c][:, :].unsqueeze(1), parts[:, DynSlice(i * S + c, 1), :]).then_inc(led[c], 1)
                for c in range(S):
                    dve.wait_ge(led[c], at(i, "onehots"))
                    for n in range(2):
                        for t in range(T):
                            a = 2 * n * T + t
                            nc.vector.tensor_scalar(hi[c][:, n, t, :], iota[:, :], part[c][:, a:a + 1], None, ALU.is_equal)
                            last = nc.vector.tensor_scalar(lo[c][:, n, t, :], iota[:, 0:P], part[c][:, a + T:a + T + 1],
                                                           None, ALU.is_equal)
                    last.then_inc(led[c], 1)
                for c in range(S):
                    dve.wait_ge(keys_in[c], (i + 1) * 32)
                    dve.wait_ge(led[c], at(i, "earlier"))
                    for n in range(2):
                        for t in range(T):
                            last = nc.vector.scalar_tensor_tensor(
                                out=junk[c][:, n * T + t, :], in0=krow[c][:, n, :],
                                scalar=part[c][:, (4 + n) * T + t:(4 + n) * T + t + 1], in1=earlier[:, t, :],
                                op0=ALU.is_equal, op1=ALU.mult, accum_out=prev[c][:, n * T + t:n * T + t + 1])
                    last.then_inc(led[c], 1)
                for c in range(S):
                    dve.wait_ge(led[c], at(i, "keep"))
                    nc.vector.tensor_copy(counts[:, DynSlice(i * S + c, 1), :], prev[c][:, :].unsqueeze(1)).then_inc(led[c], 1)
            for c in range(S):
                dve.wait_ge(led[c], at(NCH // S, "pick"))
            for n, (src, a, b) in enumerate(((srcI, 0.0, 1.0), (dstI, 0.0, 1.0), (srcI, 0.0, 3.0))):
                nc.vector.tensor_scalar(recg[:, :, n * T:(n + 1) * T], src[:, :, :], b, None, ALU.mult)
            link(nc.vector.tensor_scalar(recg[:, :, G_DSTC * T:(G_DSTC + 1) * T], dstI[:, :, :], float(N - 1), None, ALU.min))
            for n, (one, three) in enumerate(((A_SRC, A_SRC3), (A_DST, A_DST3))):
                key = parts[:, :, (4 + n) * T:(5 + n) * T]
                link(nc.vector.tensor_scalar(dup[:, :, :], counts[:, :, n * T:(n + 1) * T], 0.0, None, ALU.is_gt))
                link(nc.vector.tensor_tensor(lead[:, :, :], spare[:, :, :], key, ALU.subtract))
                link(nc.vector.tensor_tensor(dup[:, :, :], dup[:, :, :], lead[:, :, :], ALU.mult))
                link(nc.vector.tensor_tensor(lead[:, :, :], dup[:, :, :], key, ALU.add))
                nc.vector.tensor_copy(reca[:, :, one * T:(one + 1) * T], lead[:, :, :])
                link(nc.vector.tensor_scalar(reca[:, :, three * T:(three + 1) * T], lead[:, :, :], 3.0, None, ALU.mult))
            assert links[0] == 9 + 10
            dve.wait_ge(bias_in, 64)
            link(nc.vector.tensor_copy(bsplit[:, 0, :], brows[:, :]))
            link(nc.vector.tensor_tensor(bres[:, 0, :], brows[:, :], bsplit[:, 0, :], ALU.subtract))
            link(nc.vector.tensor_copy(bsplit[:, 1, :], bres[:, 0, :]))
            link(nc.vector.tensor_tensor(bres[:, 1, :], bres[:, 0, :], bsplit[:, 1, :], ALU.subtract))
            nc.vector.tensor_copy(bsplit[:, 2, :], bres[:, 1, :]).then_inc(split_out, 1)
            dve.wait_ge(transposed, 1)
            nc.vector.tensor_copy(k.wT[:, 0:4, :], tps[:, 0, :].rearrange("p (n f) -> p n f", f=D))
            nc.vector.tensor_copy(k.wT[:, 4:6, :], tps[:, 1, 0:2 * D].rearrange("p (n f) -> p n f", f=D)).then_inc(weights_ready, 1)

        @block.tensor
        def _(pe):
            pe.wait_ge(const_set, 1)
            pe.wait_ge(weights_in, 16 * (6 + 6 + 2 + 2 + T))
            for n in range(6):
                last = nc.tensor.transpose(tps[:, n // 4, n % 4 * D:(n % 4 + 1) * D], wraw[:, n, :], k.ident[:, :])
            last.then_inc(transposed, 1)
            for n in range(2):
                for b in range(2):
                    nc.tensor.matmul(hist[:, n, b * 512:(b + 1) * 512], zh[:, 0:P], zh[:, :], start=True, stop=False,
                                     skip_group_check=True)
            with pe.Fori(0, NCH // S) as i:
                for c in range(S):
                    pe.wait_ge(led[c], at(i, "earlier"))
                    for n in range(2):
                        for t in range(T):
                            for q in range(HIQ):
                                last = nc.tensor.matmul(hist[:, n, q * P:(q + 1) * P], hi[c][:, n, t, q * P:(q + 1) * P],
                                                        lo[c][:, n, t, :], start=False, stop=False, skip_group_check=True)
                    last.then_inc(counted[c], 1)


def small_table_phase(nc, tb, hist):
    with ExitStack() as ctx:
        def sb(name, shape, dt):
            return ctx.enter_context(nc.sbuf_tensor(name, shape, dt))
        W = HIQ * P
        val = sb("val", [P, W, 4], F32)
        atl = sb("atl", [P, 2, W], F32)
        root = sb("root", [P, W], F32)
        rroot = sb("rroot", [P, W], F32)
        indb = sb("indb", [P, W], BF16)
        step = ctx.enter_context(nc.semaphore("table_step"))
        stored = ctx.enter_context(nc.semaphore("table_stored"))
        block = ctx.enter_context(nc.Block())

        @block.vector
        def _(dve):
            nc.vector.tensor_scalar(val[:, :, C_IND], hist[:, 0, 0:W], 0.0, None, ALU.is_gt)
            nc.vector.tensor_scalar(indb[:, :], hist[:, 0, 0:W], 0.0, None, ALU.is_gt)
            nc.vector.tensor_scalar(atl[:, 1, :], hist[:, 1, 0:W], 1.0, None, ALU.max)
            nc.vector.tensor_scalar(atl[:, 0, :], hist[:, 0, 0:W], 1.0, None, ALU.max).then_inc(step, 1)
            dve.wait_ge(step, 2)
            nc.vector.reciprocal(val[:, :, C_INVS], atl[:, 0, :])
            nc.vector.reciprocal(val[:, :, C_INVD], atl[:, 1, :])
            nc.vector.reciprocal(rroot[:, :], root[:, :]).then_inc(step, 1)
            dve.wait_ge(step, 3)
            nc.vector.tensor_tensor(val[:, :, C_DIS], rroot[:, :], val[:, :, C_IND], ALU.mult).then_inc(step, 1)

        @block.scalar
        def _(act):
            act.wait_ge(step, 1)
            nc.scalar.activation(root[:, :], atl[:, 0, :], ACT.Sqrt).then_inc(step, 1)
            act.wait_ge(step, 4)
            act.dma_start(tb.small.rearrange("(q h l) k -> h q (l k)", h=P, l=P),
                          val[:, :, :].rearrange("h (q l) k -> h q (l k)", l=P)).then_inc(stored, 16)
            act.dma_start(tb.ind.rearrange("(q h l) -> h q l", h=P, l=P),
                          indb[:, :].rearrange("h (q l) -> h q l", l=P)).then_inc(stored, 16)
            act.wait_ge(stored, 32)


def gather(pool, out, table, idx, t, signal, offset=0, bound=None):
    pool.indirect_dma_start(out, None, table, bass.IndirectOffsetOnAxis(ap=idx[:, t:t + 1], axis=0),
                            element_offset=offset).then_inc(signal, 16)


def add_rows(pool, table, rows, idx, signal, offset=0):
    for t in range(T):
        pool.indirect_dma_start(table, bass.IndirectOffsetOnAxis(ap=idx[:, t:t + 1], axis=0), rows[:, t, :], None,
                                element_offset=offset, compute_op=ALU.add).then_inc(signal, 16)


def phase_tools(ctx, nc, phase):
    sems = []

    def finish():
        nc.clear_and_free_semaphores(sems)
        nc.all_engine_barrier()
    ctx.callback(finish)

    def sb(name, shape, dt):
        return ctx.enter_context(nc.sbuf_tensor(f"{phase}_{name}", shape, dt))

    def sem(name):
        sems.append(nc.alloc_semaphore(f"{phase}_{name}"))
        return sems[-1]

    def banks(name, n):
        return [ctx.enter_context(nc.psum_tensor(f"{phase}_{name}{c}", [P, 512], F32)) for c in range(n)]
    return sb, sem, banks


def chunk_rows(table, i, c):
    return table[DynSlice(i * G + c, 1)].rearrange("c p f -> p c f")


def flat(x):
    return x.rearrange("p t f -> p (t f)")


def first_rows_phase(nc, k, tb, inp):
    with ExitStack() as ctx:
        sb, sem, _ = phase_tools(ctx, nc, "first")
        C = range(GF)
        NB = blocks(GF)
        x = [sb(f"x{c}", [P, T, D], F32) for c in C]
        h = [sb(f"h{c}", [P, T, D], F32) for c in C]
        y = [sb(f"y{c}", [P, T, D], F32) for c in C]
        deg = [sb(f"deg{c}", [P, T, 4], F32) for c in C]
        dis2 = [sb(f"dis2{c}", [P, T], F32) for c in C]
        b = [Norm(sb, f"n{c}", k.ticks) for c in C]
        loaded = [sem(f"loaded{c}") for c in C]
        stored = [sem(f"stored{c}") for c in C]
        done = [sem(f"done{c}") for c in C]
        L = range(G)
        all_idx = sb("all_idx", [P, NCH, 16], I32)
        all_ew = sb("all_ew", [P, NCH, T], F32)
        all_ends = sb("all_ends", [P, NCH, 2, T, 4], F32)
        rec = sb("rec", [P, NCH, 5, T], F32)
        neq = sb("neq", [P, NCH, T], F32)
        prod = sb("prod", [P, 2, NCH, T], F32)
        idx = [sb(f"idx{c}", [P, 2 * T], I32) for c in L]
        ends = [sb(f"ends{c}", [P, 2, T, 4], F32) for c in L]
        all_in, copied, rec_out, weighed = sem("all_in"), sem("copied"), sem("rec_out"), sem("weighed")
        idx_set = [sem(f"idx_set{c}") for c in L]
        ends_in = [sem(f"ends_in{c}") for c in L]
        block = ctx.enter_context(nc.Block())
        order = ["square"] + ln("x_")[:4] + ["scale"] + ln("x_")[4:] + ["first"]
        at = counter(order)
        plan = stagger(["load"] + order, GF)
        ER = NCH // G

        @block.sync
        def _(sp):
            def load(i, c):
                rows = DynSlice(i * CH + stream_base(c, GF), CH)
                sp.wait_ge(done[c], at(i, "square"))
                sp.dma_start(x[c][:, :, :], inp["x"][rows, :].rearrange("(p t) f -> p t f", t=T)).then_inc(loaded[c], 16)
                sp.dma_start(deg[c][:, :, :], tb.small[rows, :].rearrange("(p t) k -> p t k", t=T)).then_inc(loaded[c], 16)

            def step(name, i, c):
                if name == "load":
                    load(i, c)
                if name == "first":
                    rows = DynSlice(i * CH + stream_base(c, GF), CH)
                    sp.wait_ge(done[c], at(i, "end"))
                    sp.dma_start(tb.node3[rows, 0, :].rearrange("(p t) f -> p t f", t=T), y[c][:, :, :]).then_inc(stored[c], 16)
            sp.dma_start(all_idx[:, :, :], tb.rec_g.rearrange("c p k -> p c k")).then_inc(all_in, 16)
            sp.dma_start(all_ew[:, :, :], tb.ew.rearrange("(c p t) -> p c t", p=P, t=T)).then_inc(all_in, 16)
            rounds(sp, step, plan, NB)
            sp.wait_ge(weighed, 4)
            sp.dma_start(tb.rec_f.rearrange("c p f -> p c f"), rec[:, :, :, :].rearrange("p c a t -> p c (a t)")).then_inc(rec_out, 16)
            sp.wait_ge(rec_out, 16)
            for c in C:
                sp.wait_ge(stored[c], NB * 16 + 1)

        @block.scalar
        def _(act):
            def step(name, i, c):
                norm_scalar(nc, act, done[c], at, i, "x_", name, b[c], k.eps[:, :], h[c], x[c], ACT.Relu)
            rounds(act, step, plan, NB)

        @block.vector
        def _(dve):
            start(dve, *done, *stored)

            def edge_weights():
                dve.wait_ge(all_in, 32)
                dve.wait_ge(copied, NCH)
                for n, a in ((0, F_KEYS), (1, F_KEYD)):
                    nc.vector.tensor_copy(rec[:, :, a, :], all_idx[:, :, n * T:(n + 1) * T])
                nc.vector.tensor_copy(rec[:, :, F_INVD, :], all_ends[:, :, 1, :, C_INVD])
                nc.vector.tensor_copy(rec[:, :, F_INVS, :], all_ends[:, :, 0, :, C_INVS])
                nc.vector.tensor_tensor(prod[:, 0, :, :], all_ends[:, :, 0, :, C_DIS], all_ew[:, :, :], ALU.mult).then_inc(weighed, 1)
                dve.wait_ge(weighed, 1)
                nc.vector.tensor_tensor(neq[:, :, :], rec[:, :, F_KEYS, :], rec[:, :, F_KEYD, :], ALU.not_equal).then_inc(weighed, 1)
                nc.vector.tensor_tensor(prod[:, 1, :, :], prod[:, 0, :, :], all_ends[:, :, 1, :, C_DIS], ALU.mult).then_inc(weighed, 1)
                dve.wait_ge(weighed, 3)
                nc.vector.tensor_tensor(rec[:, :, F_W, :], prod[:, 1, :, :], neq[:, :, :], ALU.mult).then_inc(weighed, 1)

            def step(name, i, c):
                norm_vector(nc, dve, done[c], at, i, "x_", name, b[c], x[c])
                if name == "square":
                    dve.wait_ge(loaded[c], (i + 1) * 32)
                    dve.wait_ge(done[c], at(i, "square"))
                    nc.vector.tensor_tensor(dis2[c][:, :], deg[c][:, :, C_DIS], deg[c][:, :, C_DIS], ALU.mult).then_inc(done[c], 1)
                if name == "scale":
                    dve.wait_ge(done[c], at(i, "scale"))
                    nc.vector.tensor_tensor(b[c].rs[:, :], b[c].rs[:, :], dis2[c][:, :], ALU.mult).then_inc(done[c], 1)
                if name == "first":
                    dve.wait_ge(stored[c], i * 16 + 1)
                    dve.wait_ge(done[c], at(i, "first"))
                    nc.vector.tensor_tensor(flat(y[c][:, :, :]), flat(h[c][:, :, :]), flat(x[c][:, :, :]),
                                            ALU.add).then_inc(done[c], 1)

            rounds(dve, step, plan, NB)
            edge_weights()

        @block.gpsimd
        def _(pool):
            def look_up(i, c):
                nc.gpsimd.tensor_copy(idx[c][:, :].unsqueeze(1), all_idx[:, DynSlice(i * G + c, 1), 0:2 * T]).then_inc(idx_set[c], 1)
                wait_alone(pool, k.ticks, idx_set[c], i + 1)
                for n in range(2):
                    for t in range(T):
                        gather(pool, ends[c][:, n, t, :], tb.small, idx[c], n * T + t, ends_in[c])

            def keep(i, c):
                pool.wait_ge(ends_in[c], (i + 1) * 2 * T * 16)
                nc.gpsimd.tensor_copy(all_ends[:, DynSlice(i * G + c, 1), :, :, :].rearrange("p c n t k -> p (c n t k)"),
                                      ends[c][:, :, :, :].rearrange("p n t k -> p (n t k)")).then_inc(copied, 1)

            pool.wait_ge(all_in, 32)
            for c in L:
                look_up(0, c)
            with pool.Fori(1, ER) as i:
                for c in L:
                    keep(i - 1, c)
                    pool.wait_ge(copied, (i - 1) * G + c + 1)
                    look_up(i, c)
            for c in L:
                keep(ER - 1, c)

        @block.tensor
        def _(pe):
            pass


class Filling:

    def __init__(self, sb, sem, columns, row=None):
        self.zero = sb("zero", [P, D], F32) if row is None else None
        self.row = self.zero[:, :] if row is None else row
        self.zero_set, self.filled = sem("zero_set"), sem("filled")
        self.pieces = columns.rearrange("(c p b) f -> c p b f", p=P, b=ZR)

    def prepare(self, nc):
        if self.zero is not None:
            nc.gpsimd.memset(self.zero[:, :], 0.0).then_inc(self.zero_set, 1)

    def wait_prepared(self, eng):
        if self.zero is not None:
            eng.wait_ge(self.zero_set, 1)

    def piece(self, eng, i, c):
        to = self.pieces[DynSlice(i * G + c, 1)].rearrange("c p b f -> (c p) b f")
        eng.dma_start(to, self.row.unsqueeze(1).to_broadcast([P, ZR, D])).then_inc(self.filled, 16)


class EdgeSide:

    def __init__(self, sb, sem):
        L = range(G)
        self.gidx = [sb(f"gidx{c}", [P, 16], I32) for c in L]
        self.aidx = [sb(f"aidx{c}", [P, 16], I32) for c in L]
        self.rec = [sb(f"rec{c}", [P, 5, T], F32) for c in L]
        self.krow = [sb(f"krow{c}", [P, CH], I32) for c in L]
        self.same = [sb(f"same{c}", [P, T, CH], F32) for c in L]
        self.comb = [sb(f"comb{c}", [P, T, D], F32) for c in L]
        self.gidx_in = [sem(f"gidx_in{c}") for c in L]
        self.aidx_in = [sem(f"aidx_in{c}") for c in L]
        self.rec_in = [sem(f"rec_in{c}") for c in L]
        self.gathered = [sem(f"gathered{c}") for c in L]
        self.done = [sem(f"done{c}") for c in L]
        self.summed = sem("summed")
        self.turns = sem("turns")


def is_last(i):
    return isinstance(i, int) and i == NCH // G - 1


def load_gather_rows(sp, e, tb, i, c):
    sp.dma_start(e.gidx[c][:, :].unsqueeze(1), chunk_rows(tb.rec_g, i, c)).then_inc(e.gidx_in[c], 16)


def load_records(sp, e, tb, key, i, c):
    sp.dma_start(e.rec[c][:, :, :].rearrange("p a t -> p (a t)").unsqueeze(1), chunk_rows(tb.rec_f, i, c)).then_inc(e.rec_in[c], 16)
    sp.dma_start(e.krow[c][:, :], key.rearrange("(c e) -> c e", e=CH)[DynSlice(i * G + c, 1), :].partition_broadcast(P)).then_inc(e.rec_in[c], 16)


def match_keys(nc, dve, e, at, i, c, key, weight):
    dve.wait_ge(e.rec_in[c], (i + 1) * 32)
    dve.wait_ge(e.done[c], at(i, "match"))
    tiles(lambda b: nc.vector.tensor_scalar(e.same[c][:, b, :], e.krow[c][:, :], e.rec[c][:, key, b:b + 1],
                                            e.rec[c][:, weight, b:b + 1], ALU.is_equal, ALU.mult)).then_inc(e.done[c], 1)


def keep_sums(nc, act, e, tb, at, i, c, ps):
    act.wait_ge(e.turns, i * G + c + 1)
    act.dma_start(e.aidx[c][:, :].unsqueeze(1), chunk_rows(tb.rec_a, i, c)).then_inc(e.aidx_in[c], 16)
    act.wait_ge(e.done[c], at(i, "keep"))
    nc.scalar.activation(flat(e.comb[c][:, :, :]), ps[:, :], ACT.Copy).then_inc(e.done[c], 1)


def start_edge_side(dve, e, *sems):
    start(dve, *e.done, *sems)
    dve.sem_inc(e.turns, G - 1)


def pool_program(pool, ticks, e, plan, at, gathers, free_step, free, table, group, offset):
    def fetch(i, c):
        wait_alone(pool, ticks, e.gidx_in[c], (i + 1) * 16)
        gathers(c)

    def step(name, i, c):
        if name == free_step and not is_last(i):
            free(i, c)
            fetch(i + 1, c)
        if name == "keep":
            pool.wait_ge(e.aidx_in[c], (i + 1) * 16)
            pool.wait_ge(e.done[c], at(i, "end"))
            if not (isinstance(i, int) and i * G + c == 0):
                pool.wait_ge(e.summed, (i * G + c) * T * 16)
            pool.sem_inc(e.turns, 1)
            add_rows(pool, table, e.comb[c], e.aidx[c][:, group * T:(group + 1) * T], e.summed, offset)

    for c in range(G):
        fetch(0, c)
    rounds(pool, step, plan, NCH // G)
    pool.wait_ge(e.summed, NCH * T * 16)


def gcn_phase(nc, k, tb, inp, first):
    with ExitStack() as ctx:
        sb, sem, banks = phase_tools(ctx, nc, "gcn" if first else "sage1")
        L = range(G)
        e = EdgeSide(sb, sem)
        x = [sb(f"x{c}", [P, T, D], F32) for c in L]
        h = [sb(f"h{c}", [P, T, D], F32) for c in L]
        sumT = [sb(f"sumT{c}", [P, CH], F32) for c in L]
        b = [Norm(sb, f"n{c}", k.ticks) for c in L]
        kept = [sem(f"kept{c}") for c in L]
        filling = Filling(sb, sem, tb.node3[:, 2, :], k.b12[:, 1, :]) if first else Filling(sb, sem, tb.sum3)
        p0 = banks("p", G)
        block = ctx.enter_context(nc.Block())
        order = ln("x_") + (["match", "combine", "keep"] if first else ["match", "combine", "sumT", "apply", "keep"])
        at = counter(order)
        plan = stagger(order, G, beside={"combine": 4300, "keep": 4300})
        RD = NCH // G
        key, weight, target, offset, krow, group = (F_KEYS, F_W, A_SRC3, 0, tb.src, G_DSTC) if first else \
            (F_KEYD, F_INVD, A_DST3, D, tb.dst, G_SRC3)
        rows3 = tb.node3.rearrange("r k f -> (r k) f")
        source = inp["x"] if first else rows3

        @block.sync
        def _(sp):
            def step(name, i, c):
                if name == "x_mean_var" and not is_last(i):
                    sp.wait_ge(e.gathered[c], (i + 1) * T * 16)
                    load_gather_rows(sp, e, tb, i + 1, c)
                if name == "match" and not first:
                    sp.wait_ge(e.done[c], at(i, "match"))
                    sp.dma_start(chunk_rows(tb.x1s, i, c), flat(x[c][:, :, :]).unsqueeze(1)).then_inc(kept[c], 16)
                    sp.dma_start(chunk_rows(tb.h1s, i, c), flat(h[c][:, :, :]).unsqueeze(1)).then_inc(kept[c], 16)
                if name == "combine" and not is_last(i):
                    sp.wait_ge(e.done[c], at(i, "combine"))
                    load_records(sp, e, tb, krow, i + 1, c)

            for c in L:
                load_gather_rows(sp, e, tb, 0, c)
            for c in L:
                load_records(sp, e, tb, krow, 0, c)
            rounds(sp, step, plan, RD)
            if not first:
                for c in L:
                    sp.wait_ge(kept[c], RD * 32 + 1)

        @block.gpsimd
        def _(pool):
            filling.prepare(nc)

            def gathers(c):
                for t in range(T):
                    gather(pool, x[c][:, t, :], source, e.gidx[c], group * T + t, e.gathered[c])

            def free(i, c):
                pool.wait_ge(e.done[c], at(i, "match"))
                if not first:
                    pool.wait_ge(kept[c], (i + 1) * 32 + 1)
            pool_program(pool, k.ticks, e, plan, at, gathers, "combine", free, rows3, target, offset)

        @block.vector
        def _(dve):
            def step(name, i, c):
                if name == "x_stats":
                    dve.wait_ge(e.gathered[c], (i + 1) * T * 16)
                norm_vector(nc, dve, e.done[c], at, i, "x_", name, b[c], x[c])
                if name == "match":
                    match_keys(nc, dve, e, at, i, c, key, weight)
                if name == "sumT":
                    dve.wait_ge(e.done[c], at(i, "sumT"))
                    nc.vector.tensor_copy(sumT[c][:, :], p0[c][:, :]).then_inc(e.done[c], 1)
            start_edge_side(dve, e, *kept)
            rounds(dve, step, plan, RD)

        @block.scalar
        def _(act):
            def step(name, i, c):
                if name == "x_norm" and not first:
                    act.wait_ge(kept[c], i * 32 + 1)
                if name == "match":
                    filling.piece(act, i, c)
                norm_scalar(nc, act, e.done[c], at, i, "x_", name, b[c], k.eps[:, :], h[c], x[c], ACT.Relu)
                if name == "keep":
                    keep_sums(nc, act, e, tb, at, i, c, p0[c])
            filling.wait_prepared(act)
            rounds(act, step, plan, RD)
            act.wait_ge(filling.filled, NCH * 16)

        @block.tensor
        def _(pe):
            def step(name, i, c):
                if name == "combine":
                    pe.wait_ge(e.done[c], at(i, "combine"))
                    (combine_rows if first else combine_columns)(nc, p0[c], e.same[c], h[c]).then_inc(e.done[c], 1)
                if name == "apply":
                    pe.wait_ge(e.done[c], at(i, "apply"))
                    apply_columns(nc, p0[c], sumT[c], k.wT[:, 0, :]).then_inc(e.done[c], 1)
            rounds(pe, step, plan, RD)


def sage2_phase(nc, k, tb):
    with ExitStack() as ctx:
        sb, sem, banks = phase_tools(ctx, nc, "sage2")
        L = range(G)
        e = EdgeSide(sb, sem)
        filling = Filling(sb, sem, tb.sum4)
        a = [sb(f"a{c}", [P, T, D], F32) for c in L]
        h = [sb(f"h{c}", [P, T, D], F32) for c in L]
        g = [sb(f"g{c}", [P, T, D], F32) for c in L]
        hT = [sb(f"hT{c}", [P, CH], F32) for c in L]
        h_in = [sem(f"h_in{c}") for c in L]
        kept = [sem(f"kept{c}") for c in L]
        p0 = banks("p", G)
        block = ctx.enter_context(nc.Block())
        order = ["turn", "hT", "mix", "plus", "relu", "match", "combine", "sumT", "apply", "keep"]
        at = counter(order)
        plan = stagger(order, G, {"relu": (SCALAR, 570)}, {"relu": 4300, "keep": 4300})
        RD = NCH // G
        rows3 = tb.node3.rearrange("r k f -> (r k) f")

        @block.sync
        def _(sp):
            def load_h(i, c):
                sp.dma_start(flat(h[c][:, :, :]).unsqueeze(1), chunk_rows(tb.h1s, i, c)).then_inc(h_in[c], 16)

            def step(name, i, c):
                if name == "mix" and not is_last(i):
                    sp.wait_ge(e.done[c], at(i, "hT"))
                    load_h(i + 1, c)
                    sp.wait_ge(e.gathered[c], (i + 1) * T * 16)
                    load_gather_rows(sp, e, tb, i + 1, c)
                if name == "match":
                    sp.wait_ge(e.done[c], at(i, "match"))
                    sp.dma_start(chunk_rows(tb.g1s, i, c), flat(g[c][:, :, :]).unsqueeze(1)).then_inc(kept[c], 16)
                if name == "combine" and not is_last(i):
                    sp.wait_ge(e.done[c], at(i, "combine"))
                    load_records(sp, e, tb, tb.dst, i + 1, c)

            for c in L:
                load_gather_rows(sp, e, tb, 0, c)
                load_h(0, c)
            for c in L:
                load_records(sp, e, tb, tb.dst, 0, c)
            rounds(sp, step, plan, RD)
            for c in L:
                sp.wait_ge(kept[c], RD * 16 + 1)

        @block.gpsimd
        def _(pool):
            filling.prepare(nc)
            def gathers(c):
                for t in range(T):
                    gather(pool, a[c][:, t, :], rows3, e.gidx[c], G_SRC3 * T + t, e.gathered[c], D)

            def free(i, c):
                pool.wait_ge(e.done[c], at(i, "relu"))
            pool_program(pool, k.ticks, e, plan, at, gathers, "relu", free, rows3, A_DST3, 2 * D)

        @block.vector
        def _(dve):
            def step(name, i, c):
                if name == "plus":
                    dve.wait_ge(kept[c], i * 16 + 1)
                    dve.wait_ge(e.gathered[c], (i + 1) * T * 16)
                    dve.wait_ge(e.done[c], at(i, "plus"))
                    nc.vector.tensor_tensor(flat(g[c][:, :, :]), p0[c][:, :], flat(a[c][:, :, :]), ALU.add).then_inc(e.done[c], 1)
                if name == "match":
                    match_keys(nc, dve, e, at, i, c, F_KEYD, F_INVD)
                if name == "sumT":
                    dve.wait_ge(e.done[c], at(i, "sumT"))
                    nc.vector.tensor_copy(hT[c][:, :], p0[c][:, :]).then_inc(e.done[c], 1)
            start_edge_side(dve, e, *kept)
            rounds(dve, step, plan, RD)

        @block.scalar
        def _(act):
            def step(name, i, c):
                if name == "hT":
                    act.wait_ge(e.done[c], at(i, "hT"))
                    nc.scalar.activation(hT[c][:, :], p0[c][:, :], ACT.Copy).then_inc(e.done[c], 1)
                if name == "relu":
                    act.wait_ge(e.done[c], at(i, "relu"))
                    nc.scalar.activation(flat(g[c][:, :, :]), flat(g[c][:, :, :]), ACT.Relu).then_inc(e.done[c], 1)
                if name == "match":
                    filling.piece(act, i, c)
                if name == "keep":
                    keep_sums(nc, act, e, tb, at, i, c, p0[c])
            filling.wait_prepared(act)
            rounds(act, step, plan, RD)
            act.wait_ge(filling.filled, NCH * 16)

        @block.tensor
        def _(pe):
            def step(name, i, c):
                if name == "turn":
                    pe.wait_ge(h_in[c], (i + 1) * 16)
                    pe.wait_ge(e.done[c], at(i, "turn"))
                    transpose4(nc, p0[c], h[c], k.ident[:, :]).then_inc(e.done[c], 1)
                if name == "mix":
                    pe.wait_ge(e.done[c], at(i, "mix"))
                    rows_matmul(nc, p0[c], [(hT[c], k.wT[:, 1, :])]).then_inc(e.done[c], 1)
                if name == "combine":
                    pe.wait_ge(e.done[c], at(i, "combine"))
                    combine_columns(nc, p0[c], e.same[c], g[c]).then_inc(e.done[c], 1)
                if name == "apply":
                    pe.wait_ge(e.done[c], at(i, "apply"))
                    apply_columns(nc, p0[c], hT[c], k.wT[:, 2, :]).then_inc(e.done[c], 1)
            rounds(pe, step, plan, RD)


def edge_mlp_phase(nc, k, tb):
    with ExitStack() as ctx:
        sb, sem, banks = phase_tools(ctx, nc, "mlp")
        L = range(G)
        e = EdgeSide(sb, sem)

        def each(name, shape):
            return [sb(f"{name}{c}", shape, F32) for c in L]
        a2, gs, xs, v, x2d, h2d = (each(n, [P, T, D]) for n in ("a2", "gs", "xs", "v", "x2d", "h2d"))
        w3 = each("w3", [P, T, 3 * D])
        col, srcT = each("col", [P, CH]), each("srcT", [P, CH])
        ea, eaT = each("ea", [P, P]), each("eaT", [P, P])
        b = [Norm(sb, f"n{c}", k.ticks) for c in L]
        side_in = [sem(f"side_in{c}") for c in L]
        ea_in = [sem(f"ea_in{c}") for c in L]
        kept = [sem(f"kept{c}") for c in L]
        ea_zero = sem("ea_zero")
        p0 = banks("p", G)
        block = ctx.enter_context(nc.Block())
        order = (["turn_g", "gT", "mix_s", "plus_s", "x2s"] + ln("s_") + ["turn_s", "srcT"]
                 + ln("d_") + ["turn_d", "hT", "mix_d", "relu_d", "mix2_d", "plus_d", "x2d"] + ln("e_")
                 + ["turn_e", "dstT", "turn_ea", "eaT", "hidden", "relu_m", "message", "msg",
                    "match", "combine", "sumT", "apply", "keep"])
        at = counter(order)
        plan = stagger(order, G, beside={"e_stats": 8500, "keep": 4300})
        RD = NCH // G
        rows3 = tb.node3.rearrange("r k f -> (r k) f")
        whole = tb.node3.rearrange("r k f -> r (k f)")

        @block.sync
        def _(sp):
            def load_side(i, c):
                sp.dma_start(flat(gs[c][:, :, :]).unsqueeze(1), chunk_rows(tb.g1s, i, c)).then_inc(side_in[c], 16)
                sp.dma_start(flat(xs[c][:, :, :]).unsqueeze(1), chunk_rows(tb.x1s, i, c)).then_inc(side_in[c], 16)

            def load_ea(i, c):
                sp.dma_start(ea[c][:, 0:2 * T].unsqueeze(1),
                             chunk_rows(tb.ea.rearrange("(c p t) k -> c p (t k)", p=P, t=T), i, c)).then_inc(ea_in[c], 16)

            def step(name, i, c):
                if name == "s_stats" and not is_last(i):
                    sp.wait_ge(e.gathered[c], (i + 1) * 2 * T * 16)
                    load_gather_rows(sp, e, tb, i + 1, c)
                    sp.wait_ge(e.done[c], at(i, "s_stats"))
                    load_side(i + 1, c)
                if name == "turn_e":
                    sp.wait_ge(e.done[c], at(i, "turn_e"))
                    sp.dma_start(chunk_rows(tb.x2d, i, c), flat(x2d[c][:, :, :]).unsqueeze(1)).then_inc(kept[c], 16)
                    sp.dma_start(chunk_rows(tb.h2d, i, c), flat(h2d[c][:, :, :]).unsqueeze(1)).then_inc(kept[c], 16)
                if name == "combine" and not is_last(i):
                    sp.wait_ge(e.done[c], at(i, "combine"))
                    load_ea(i + 1, c)
                    load_records(sp, e, tb, tb.dst, i + 1, c)

            sp.wait_ge(ea_zero, 1)
            for c in L:
                load_gather_rows(sp, e, tb, 0, c)
                load_side(0, c)
            for c in L:
                load_ea(0, c)
                load_records(sp, e, tb, tb.dst, 0, c)
            rounds(sp, step, plan, RD)
            for c in L:
                sp.wait_ge(kept[c], RD * 32 + 1)

        @block.gpsimd
        def _(pool):
            for c in L:
                last = nc.gpsimd.memset(ea[c][:, :], 0.0)
            last.then_inc(ea_zero, 1)

            def gathers(c):
                for t in range(T):
                    gather(pool, a2[c][:, t, :], rows3, e.gidx[c], G_SRC3 * T + t, e.gathered[c], 2 * D)
                for t in range(T):
                    gather(pool, w3[c][:, t, :], whole, e.gidx[c], G_DST * T + t, e.gathered[c])

            def free(i, c):
                pool.wait_ge(e.done[c], at(i, "e_stats"))
            pool_program(pool, k.ticks, e, plan, at, gathers, "e_stats", free, tb.sum3, A_DST, 0)

        @block.vector
        def _(dve):
            def step(name, i, c):
                if name == "plus_s":
                    dve.wait_ge(e.gathered[c], (i + 1) * 2 * T * 16)
                    dve.wait_ge(e.done[c], at(i, "plus_s"))
                    nc.vector.tensor_tensor(flat(v[c][:, :, :]), p0[c][:, :], flat(a2[c][:, :, :]), ALU.add).then_inc(e.done[c], 1)
                if name == "x2s":
                    dve.wait_ge(e.done[c], at(i, "x2s"))
                    nc.vector.scalar_tensor_tensor(out=flat(v[c][:, :, :]), in0=flat(v[c][:, :, :]), scalar=0.0,
                                                   in1=flat(xs[c][:, :, :]), op0=ALU.max, op1=ALU.add).then_inc(e.done[c], 1)
                norm_vector(nc, dve, e.done[c], at, i, "s_", name, b[c], v[c])
                norm_vector(nc, dve, e.done[c], at, i, "d_", name, b[c], w3[c][:, :, 0:D])
                if name == "plus_d":
                    dve.wait_ge(kept[c], i * 32 + 1)
                    dve.wait_ge(e.done[c], at(i, "plus_d"))
                    nc.vector.tensor_tensor(x2d[c][:, :, :], p0[c][:, :].rearrange("p (t f) -> p t f", f=D),
                                            w3[c][:, :, 2 * D:3 * D], ALU.add).then_inc(e.done[c], 1)
                if name == "x2d":
                    dve.wait_ge(e.done[c], at(i, "x2d"))
                    nc.vector.scalar_tensor_tensor(out=x2d[c][:, :, :], in0=x2d[c][:, :, :], scalar=0.0,
                                                   in1=w3[c][:, :, 0:D], op0=ALU.max, op1=ALU.add).then_inc(e.done[c], 1)
                norm_vector(nc, dve, e.done[c], at, i, "e_", name, b[c], x2d[c])
                if name == "eaT":
                    dve.wait_ge(e.done[c], at(i, "eaT"))
                    nc.vector.tensor_copy(eaT[c][:, :], p0[c][:, 0:P]).then_inc(e.done[c], 1)
                if name == "msg":
                    dve.wait_ge(e.done[c], at(i, "msg"))
                    nc.vector.tensor_copy(flat(v[c][:, :, :]), p0[c][:, :]).then_inc(e.done[c], 1)
                if name == "match":
                    match_keys(nc, dve, e, at, i, c, F_KEYD, F_INVD)
                if name == "sumT":
                    dve.wait_ge(e.done[c], at(i, "sumT"))
                    nc.vector.tensor_copy(col[c][:, :], p0[c][:, :]).then_inc(e.done[c], 1)
            start_edge_side(dve, e, *kept)
            rounds(dve, step, plan, RD)

        @block.scalar
        def _(act):
            def step(name, i, c):
                copies = {"gT": (col[c], p0[c]), "srcT": (srcT[c], p0[c]), "hT": (col[c], p0[c]), "dstT": (col[c], p0[c])}
                if name in copies:
                    act.wait_ge(e.done[c], at(i, name))
                    nc.scalar.activation(copies[name][0][:, :], copies[name][1][:, :], ACT.Copy).then_inc(e.done[c], 1)
                if name == "relu_d":
                    act.wait_ge(e.done[c], at(i, "relu_d"))
                    nc.scalar.activation(col[c][:, :], p0[c][:, :], ACT.Relu).then_inc(e.done[c], 1)
                if name == "relu_m":
                    act.wait_ge(e.done[c], at(i, "relu_m"))
                    nc.scalar.activation(col[c][:, :], p0[c][:, :], ACT.Relu, bias=k.bcol[:, 0:1]).then_inc(e.done[c], 1)
                norm_scalar(nc, act, e.done[c], at, i, "s_", name, b[c], k.eps[:, :], v[c], v[c], ACT.Relu)
                norm_scalar(nc, act, e.done[c], at, i, "d_", name, b[c], k.eps[:, :], v[c], w3[c][:, :, 0:D], ACT.Relu)
                norm_scalar(nc, act, e.done[c], at, i, "e_", name, b[c], k.eps[:, :], h2d[c], x2d[c], ACT.Relu)
                if name == "keep":
                    keep_sums(nc, act, e, tb, at, i, c, p0[c])
            rounds(act, step, plan, RD)

        @block.tensor
        def _(pe):
            def step(name, i, c):
                if name == "turn_g":
                    pe.wait_ge(side_in[c], (i + 1) * 32)
                if name == "turn_ea":
                    pe.wait_ge(ea_in[c], (i + 1) * 16)
                turns = {"turn_g": (p0[c], gs[c]), "turn_s": (p0[c], v[c]), "turn_d": (p0[c], v[c]), "turn_e": (p0[c], h2d[c])}
                if name in turns:
                    pe.wait_ge(e.done[c], at(i, name))
                    transpose4(nc, turns[name][0], turns[name][1], k.ident[:, :]).then_inc(e.done[c], 1)
                if name == "mix_s":
                    pe.wait_ge(e.done[c], at(i, "mix_s"))
                    rows_matmul(nc, p0[c], [(col[c], k.wT[:, 3, :])]).then_inc(e.done[c], 1)
                if name == "mix_d":
                    pe.wait_ge(e.gathered[c], (i + 1) * 2 * T * 16)
                    pe.wait_ge(e.done[c], at(i, "mix_d"))
                    columns_plus(nc, p0[c], k.wT[:, 1, :], col[c], w3[c][:, :, D:2 * D], k.ident[:, :]).then_inc(e.done[c], 1)
                if name == "mix2_d":
                    pe.wait_ge(e.done[c], at(i, "mix2_d"))
                    rows_matmul(nc, p0[c], [(col[c], k.wT[:, 3, :])]).then_inc(e.done[c], 1)
                if name == "turn_ea":
                    pe.wait_ge(e.done[c], at(i, "turn_ea"))
                    nc.tensor.transpose(p0[c][:, 0:P], ea[c][:, :], k.ident[:, :]).then_inc(e.done[c], 1)
                if name == "hidden":
                    pe.wait_ge(e.done[c], at(i, "hidden"))
                    for t in range(T):
                        o = p0[c][:, t * P:(t + 1) * P]
                        nc.tensor.matmul(o, k.wD[:, 0, :], srcT[c][:, t * P:(t + 1) * P], start=True, stop=False)
                        nc.tensor.matmul(o, k.wD[:, 1, :], col[c][:, t * P:(t + 1) * P], start=False, stop=False)
                        last = nc.tensor.matmul(o, k.wC[:, t, :], eaT[c][:, :], start=False, stop=True)
                    last.then_inc(e.done[c], 1)
                if name == "message":
                    pe.wait_ge(e.done[c], at(i, "message"))
                    rows_matmul(nc, p0[c], [(col[c], k.wD[:, 2, :])],
                                (lambda t: k.ones[:, :], k.brow[:, 0, :])).then_inc(e.done[c], 1)
                if name == "combine":
                    pe.wait_ge(e.done[c], at(i, "combine"))
                    combine_columns(nc, p0[c], e.same[c], v[c]).then_inc(e.done[c], 1)
                if name == "apply":
                    pe.wait_ge(e.done[c], at(i, "apply"))
                    apply_columns(nc, p0[c], col[c], k.wD[:, 4, :]).then_inc(e.done[c], 1)
            rounds(pe, step, plan, RD)


def update_matmuls(nc, pe, k, done, at, i, name, h2, s3, hT, uT, pa, pb):
    if name == "turn_u":
        pe.wait_ge(done, at(i, "turn_u"))
        transpose4(nc, pa, h2, k.ident[:, :]).then_inc(done, 1)
    if name == "mix_u":
        pe.wait_ge(done, at(i, "mix_u"))
        columns_plus(nc, pb, k.wD[:, 3, :], hT, s3, k.ident[:, :]).then_inc(done, 1)
    if name == "mix_u2":
        pe.wait_ge(done, at(i, "mix_u2"))
        rows_matmul(nc, pa, [(uT, k.wD[:, 5, :])], (lambda t: k.ones[:, :], k.brow[:, 1, :])).then_inc(done, 1)


def update_scalar(nc, act, k, done, at, i, name, hT, uT, pa, pb):
    if name == "uhT":
        act.wait_ge(done, at(i, "uhT"))
        nc.scalar.activation(hT[:, :], pa[:, :], ACT.Copy).then_inc(done, 1)
    if name == "relu_u":
        act.wait_ge(done, at(i, "relu_u"))
        nc.scalar.activation(uT[:, :], pb[:, :], ACT.Relu, bias=k.bcol[:, 1:2]).then_inc(done, 1)


def update_vector(nc, dve, k, done, at, i, name, pa, h2, y, x2b):
    if name == "res":
        dve.wait_ge(done, at(i, "res"))
        nc.vector.tensor_tensor(flat(y[:, :, :]), pa[:, :], flat(h2[:, :, :]), ALU.add).then_inc(done, 1)
    if name == "gamma":
        dve.wait_ge(done, at(i, "gamma"))
        nc.vector.tensor_tensor(y[:, :, :], y[:, :, :], k.gamma[:, :].unsqueeze(1).to_broadcast([P, T, D]), ALU.mult).then_inc(done, 1)
    if name == "addx":
        dve.wait_ge(done, at(i, "addx"))
        nc.vector.tensor_tensor(flat(y[:, :, :]), flat(y[:, :, :]), flat(x2b[:, :, :]), ALU.add).then_inc(done, 1)


UPDATE = ["turn_u", "uhT", "mix_u", "relu_u", "mix_u2", "res"] + ln("t_") + ["gamma", "addx"]


def mean_phase(nc, k, tb):
    with ExitStack() as ctx:
        sb, sem, banks = phase_tools(ctx, nc, "mean")
        L = range(G)
        e = EdgeSide(sb, sem)

        def each(name, shape):
            return [sb(f"{name}{c}", shape, F32) for c in L]
        s3, x2, h2, y, h3 = (each(n, [P, T, D]) for n in ("s3", "x2", "h2", "y", "h3"))
        hT, uT = each("hT", [P, CH]), each("uT", [P, CH])
        b = [Norm(sb, f"n{c}", k.ticks) for c in L]
        side_in = [sem(f"side_in{c}") for c in L]
        p0 = banks("p", G)
        block = ctx.enter_context(nc.Block())
        order = ["beta"] + UPDATE + ln("h3_") + ["match", "combine", "sumT", "apply", "keep"]
        at = counter(order)
        plan = stagger(order, G, beside={"mix_u2": 4300, "keep": 4300})
        RD = NCH // G

        @block.sync
        def _(sp):
            def load_side(i, c):
                sp.dma_start(flat(x2[c][:, :, :]).unsqueeze(1), chunk_rows(tb.x2d, i, c)).then_inc(side_in[c], 16)
                sp.dma_start(flat(h2[c][:, :, :]).unsqueeze(1), chunk_rows(tb.h2d, i, c)).then_inc(side_in[c], 16)

            def step(name, i, c):
                if name == "t_stats" and not is_last(i):
                    sp.wait_ge(e.gathered[c], (i + 1) * T * 16)
                    load_gather_rows(sp, e, tb, i + 1, c)
                if name == "h3_stats" and not is_last(i):
                    sp.wait_ge(e.done[c], at(i, "h3_stats"))
                    load_side(i + 1, c)
                if name == "combine" and not is_last(i):
                    sp.wait_ge(e.done[c], at(i, "combine"))
                    load_records(sp, e, tb, tb.src, i + 1, c)

            for c in L:
                load_gather_rows(sp, e, tb, 0, c)
                load_side(0, c)
            for c in L:
                load_records(sp, e, tb, tb.src, 0, c)
            rounds(sp, step, plan, RD)

        @block.gpsimd
        def _(pool):
            def gathers(c):
                for t in range(T):
                    gather(pool, s3[c][:, t, :], tb.sum3, e.gidx[c], G_DST * T + t, e.gathered[c])

            def free(i, c):
                pool.wait_ge(e.done[c], at(i, "relu_u"))
            pool_program(pool, k.ticks, e, plan, at, gathers, "mix_u2", free, tb.sum4, A_SRC, 0)

        @block.vector
        def _(dve):
            def step(name, i, c):
                if name == "beta":
                    dve.wait_ge(side_in[c], (i + 1) * 32)
                    dve.wait_ge(e.done[c], at(i, "beta"))
                    nc.vector.tensor_tensor(x2[c][:, :, :], x2[c][:, :, :], k.beta[:, :].unsqueeze(1).to_broadcast([P, T, D]),
                                            ALU.add).then_inc(e.done[c], 1)
                update_vector(nc, dve, k, e.done[c], at, i, name, p0[c], h2[c], y[c], x2[c])
                norm_vector(nc, dve, e.done[c], at, i, "t_", name, b[c], y[c])
                norm_vector(nc, dve, e.done[c], at, i, "h3_", name, b[c], y[c])
                if name == "match":
                    match_keys(nc, dve, e, at, i, c, F_KEYS, F_INVS)
                if name == "sumT":
                    dve.wait_ge(e.done[c], at(i, "sumT"))
                    nc.vector.tensor_copy(hT[c][:, :], p0[c][:, :]).then_inc(e.done[c], 1)
            start_edge_side(dve, e)
            rounds(dve, step, plan, RD)

        @block.scalar
        def _(act):
            def step(name, i, c):
                update_scalar(nc, act, k, e.done[c], at, i, name, hT[c], uT[c], p0[c], p0[c])
                norm_scalar(nc, act, e.done[c], at, i, "t_", name, b[c], k.eps[:, :], y[c], y[c], ACT.Identity)
                norm_scalar(nc, act, e.done[c], at, i, "h3_", name, b[c], k.eps[:, :], h3[c], y[c], ACT.Relu)
                if name == "keep":
                    keep_sums(nc, act, e, tb, at, i, c, p0[c])
            rounds(act, step, plan, RD)

        @block.tensor
        def _(pe):
            def step(name, i, c):
                if name == "turn_u":
                    pe.wait_ge(side_in[c], (i + 1) * 32)
                if name == "mix_u":
                    pe.wait_ge(e.gathered[c], (i + 1) * T * 16)
                update_matmuls(nc, pe, k, e.done[c], at, i, name, h2[c], s3[c], hT[c], uT[c], p0[c], p0[c])
                if name == "combine":
                    pe.wait_ge(e.done[c], at(i, "combine"))
                    combine_columns(nc, p0[c], e.same[c], h3[c]).then_inc(e.done[c], 1)
                if name == "apply":
                    pe.wait_ge(e.done[c], at(i, "apply"))
                    apply_columns(nc, p0[c], hT[c], k.wT[:, 5, :]).then_inc(e.done[c], 1)
            rounds(pe, step, plan, RD)


def node_phase(nc, k, tb, out):
    with ExitStack() as ctx:
        sb, sem, banks = phase_tools(ctx, nc, "node")
        C = range(GD)
        NB = blocks(GD)

        def each(name, shape):
            return [sb(f"{name}{c}", shape, F32) for c in C]
        w3 = each("w3", [P, T, 3 * D])
        s3, s4, h, x2, x2b, y = (each(n, [P, T, D]) for n in ("s3", "s4", "h", "x2", "x2b", "y"))
        o = x2
        hT = each("hT", [P, CH])
        ind = [sb(f"ind{c}", [P, CH], BF16) for c in C]
        b = [Norm(sb, f"n{c}", k.ticks) for c in C]
        w3_in = [sem(f"w3_in{c}") for c in C]
        s3_in = [sem(f"s3_in{c}") for c in C]
        s4_in = [sem(f"s4_in{c}") for c in C]
        stored = [sem(f"stored{c}") for c in C]
        done = [sem(f"done{c}") for c in C]
        ind_set = sem("ind_set")
        pa = banks("pa", GD)
        block = ctx.enter_context(nc.Block())
        order = (ln("h1_") + ["turn", "hT", "mix", "relu", "mix2", "x2", "beta"] + ln("h2_") + UPDATE
                 + ln("h3_") + ["turn3", "h3T", "mix3", "plus4", "out"])
        at = counter(order)
        plan = stagger(order, GD, {"beta": (GPSIMD, 1230), "gamma": (GPSIMD, 1230),
                                   "addx": (GPSIMD, 1230)})

        @block.sync
        def _(sp):
            sp.wait_ge(ind_set, 2)

            def at_rows(i, c):
                return DynSlice(i * CH + stream_base(c), CH)

            def load_w3(i, c):
                sp.dma_start(w3[c][:, :, :], tb.node3[at_rows(i, c)].rearrange("(p t) k f -> p t (k f)", t=T)).then_inc(w3_in[c], 16)

            def load_s3(i, c):
                sp.dma_start(s3[c][:, :, :], tb.sum3[at_rows(i, c)].rearrange("(p t) f -> p t f", t=T)).then_inc(s3_in[c], 16)

            def load_s4(i, c):
                sp.dma_start(s4[c][:, :, :], tb.sum4[at_rows(i, c)].rearrange("(p t) f -> p t f", t=T)).then_inc(s4_in[c], 16)
                sp.dma_start(ind[c][3:6, :], tb.ind[at_rows(i, c)].partition_broadcast(3)).then_inc(s4_in[c], 16)

            def step(name, i, c):
                more = not (isinstance(i, int) and i == NB - 1)
                if name == "turn_u" and more:
                    sp.wait_ge(done[c], at(i, "beta"))
                    load_w3(i + 1, c)
                if name == "gamma" and more:
                    sp.wait_ge(done[c], at(i, "relu_u"))
                    load_s3(i + 1, c)
                if name == "out":
                    if more:
                        sp.wait_ge(done[c], at(i, "out"))
                        load_s4(i + 1, c)
                    sp.wait_ge(done[c], at(i, "end"))
                    sp.dma_start(out[at_rows(i, c)].rearrange("(p t) f -> p t f", t=T), o[c][:, :, :]).then_inc(stored[c], 16)

            for c in C:
                load_w3(0, c)
                load_s3(0, c)
                load_s4(0, c)
            rounds(sp, step, plan, NB)
            for c in C:
                sp.wait_ge(stored[c], NB * 16 + 1)

        @block.gpsimd
        def _(pool):
            for c in C:
                last = nc.gpsimd.memset(ind[c][:, :], 0.0)
            last.then_inc(ind_set, 1)
            pool.wait_ge(ind_set, 1)
            for c in C:
                last = nc.gpsimd.memset(ind[c][0:3, :], 1.0)
            last.then_inc(ind_set, 1)

            def step(name, i, c):
                if name == "beta":
                    pool.wait_ge(done[c], at(i, "beta"))
                    nc.gpsimd.tensor_tensor(x2b[c][:, :, :], x2[c][:, :, :], k.beta[:, :].unsqueeze(1).to_broadcast([P, T, D]),
                                            ALU.add).then_inc(done[c], 1)
                if name == "gamma":
                    pool.wait_ge(done[c], at(i, "gamma"))
                    nc.gpsimd.tensor_tensor(y[c][:, :, :], y[c][:, :, :], k.gamma[:, :].unsqueeze(1).to_broadcast([P, T, D]),
                                            ALU.mult).then_inc(done[c], 1)
                if name == "addx":
                    pool.wait_ge(done[c], at(i, "addx"))
                    nc.gpsimd.tensor_tensor(flat(y[c][:, :, :]), flat(y[c][:, :, :]), flat(x2b[c][:, :, :]),
                                            ALU.add).then_inc(done[c], 1)
            rounds(pool, step, plan, NB)

        @block.vector
        def _(dve):
            def step(name, i, c):
                if name == "h1_stats":
                    dve.wait_ge(w3_in[c], (i + 1) * 16)
                norm_vector(nc, dve, done[c], at, i, "h1_", name, b[c], w3[c][:, :, 0:D])
                if name == "h1_norm":
                    dve.wait_ge(done[c], at(i, "h1_norm"))
                    tiles(lambda t: nc.vector.tensor_scalar(h[c][:, t, :], w3[c][:, t, 0:D], b[c].rs[:, t:t + 1],
                                                            b[c].sh[:, t:t + 1], ALU.mult, ALU.add)).then_inc(done[c], 1)
                norm_vector(nc, dve, done[c], at, i, "h2_", name, b[c], x2[c])
                if name == "res":
                    update_vector(nc, dve, k, done[c], at, i, name, pa[c], h[c], y[c], x2b[c])
                norm_vector(nc, dve, done[c], at, i, "t_", name, b[c], y[c])
                norm_vector(nc, dve, done[c], at, i, "h3_", name, b[c], y[c])
                if name == "plus4":
                    dve.wait_ge(s4_in[c], (i + 1) * 32)
                    dve.wait_ge(done[c], at(i, "plus4"))
                    nc.vector.tensor_tensor(flat(o[c][:, :, :]), pa[c][:, :], flat(s4[c][:, :, :]), ALU.add).then_inc(done[c], 1)
                if name == "x2":
                    dve.wait_ge(stored[c], i * 16 + 1)
                    dve.wait_ge(done[c], at(i, "x2"))
                    nc.vector.scalar_tensor_tensor(out=x2[c][:, :, :], in0=pa[c][:, :].rearrange("p (t f) -> p t f", f=D), scalar=0.0,
                                                   in1=w3[c][:, :, 0:D], op0=ALU.max, op1=ALU.add).then_inc(done[c], 1)
                if name == "out":
                    dve.wait_ge(done[c], at(i, "out"))
                    nc.vector.scalar_tensor_tensor(out=flat(o[c][:, :, :]), in0=flat(o[c][:, :, :]), scalar=0.0,
                                                   in1=flat(y[c][:, :, :]), op0=ALU.max, op1=ALU.add).then_inc(done[c], 1)
            start(dve, *done, *stored)
            rounds(dve, step, plan, NB)

        @block.scalar
        def _(act):
            def step(name, i, c):
                if name != "h1_norm":
                    norm_scalar(nc, act, done[c], at, i, "h1_", name, b[c], k.eps[:, :], h[c], w3[c][:, :, 0:D], ACT.Relu)
                norm_scalar(nc, act, done[c], at, i, "h2_", name, b[c], k.eps[:, :], h[c], x2[c], ACT.Relu)
                norm_scalar(nc, act, done[c], at, i, "t_", name, b[c], k.eps[:, :], y[c], y[c], ACT.Identity)
                norm_scalar(nc, act, done[c], at, i, "h3_", name, b[c], k.eps[:, :], h[c], y[c], ACT.Relu)
                update_scalar(nc, act, k, done[c], at, i, name, hT[c], hT[c], pa[c], pa[c])
                if name in ("hT", "h3T"):
                    act.wait_ge(done[c], at(i, name))
                    nc.scalar.activation(hT[c][:, :], pa[c][:, :], ACT.Relu).then_inc(done[c], 1)
                if name == "relu":
                    act.wait_ge(done[c], at(i, "relu"))
                    nc.scalar.activation(hT[c][:, :], pa[c][:, :], ACT.Relu).then_inc(done[c], 1)
            rounds(act, step, plan, NB)

        @block.tensor
        def _(pe):
            def step(name, i, c):
                if name in ("turn", "turn3"):
                    pe.wait_ge(done[c], at(i, name))
                    transpose4(nc, pa[c], h[c], k.ident[:, :]).then_inc(done[c], 1)
                if name == "mix":
                    pe.wait_ge(w3_in[c], (i + 1) * 16)
                    pe.wait_ge(done[c], at(i, "mix"))
                    columns_plus(nc, pa[c], k.wT[:, 1, :], hT[c], w3[c][:, :, D:2 * D], k.ident[:, :]).then_inc(done[c], 1)
                if name == "mix2":
                    pe.wait_ge(done[c], at(i, "mix2"))
                    for t in range(T):
                        o = pa[c][:, t * P:(t + 1) * P]
                        nc.tensor.matmul(o, hT[c][:, t * P:(t + 1) * P], k.wT[:, 3, :], start=True, stop=False)
                        last = nc.tensor.matmul(o, k.ident[:, :], w3[c][:, t, 2 * D:3 * D], start=False, stop=True)
                    last.then_inc(done[c], 1)
                if name == "mix_u":
                    pe.wait_ge(s3_in[c], (i + 1) * 16)
                update_matmuls(nc, pe, k, done[c], at, i, name, h[c], s3[c], hT[c], hT[c], pa[c], pa[c])
                if name == "mix3":
                    pe.wait_ge(s4_in[c], (i + 1) * 32)
                    pe.wait_ge(done[c], at(i, "mix3"))
                    rows_matmul(nc, pa[c], [(hT[c], k.wT[:, 4, :])],
                                (lambda t: ind[c][:, t:CH:T], k.brow[:, 2, :])).then_inc(done[c], 1)
            rounds(pe, step, plan, NB)


def gnn_program(nc, inp, out):
    tb = Tables(nc)
    with ExitStack() as ctx:
        k = Consts(lambda name, shape, dt: ctx.enter_context(nc.sbuf_tensor(name, shape, dt)),
                   ctx.enter_context(nc.semaphore("ticks")))
        with nc.psum_tensor("hist", [P, 2, 1024], F32) as hist:
            setup_phase(nc, k, tb, inp, hist)
            small_table_phase(nc, tb, hist)
        first_rows_phase(nc, k, tb, inp)
        gcn_phase(nc, k, tb, inp, True)
        gcn_phase(nc, k, tb, inp, False)
        sage2_phase(nc, k, tb)
        edge_mlp_phase(nc, k, tb)
        mean_phase(nc, k, tb)
        node_phase(nc, k, tb, out)


_INS = ["x", "src", "dst", "edge_attr_2", "edge_weight", "L1_gnn_W1_l", "L1_gnn_W1_r", "L1_gnn_b1", "L1_gnn_W2_l",
        "L1_gnn_W2_r", "L1_gnn_b2", "L2_gnn_mW1", "L2_gnn_mb1", "L2_gnn_mW2", "L2_gnn_mb2", "L2_gnn_uW1", "L2_gnn_ub1",
        "L2_gnn_uW2", "L2_gnn_ub2", "L2_gnn_gamma", "L2_gnn_beta", "L3_gnn_W_self", "L3_gnn_b_self",
        "L3_gnn_W_neighbor", "L3_gnn_b_neighbor"]


def kernel(**inputs):
    import numpy as _np
    import concourse.bacc as _bacc
    from concourse import mybir as _mybir
    from concourse.bass_utils import run_bass_kernel_spmd as _run

    nc = _bacc.Bacc("TRN2", target_bir_lowering=False, num_devices=1)
    arrays, inp = {}, {}
    for name in _INS:
        a = _np.ascontiguousarray(inputs[name])
        arrays["in_" + name] = a
        inp[name] = nc.dram_tensor("in_" + name, a.shape, _mybir.dt.from_np(a.dtype), kind="ExternalInput").ap()
    out = nc.dram_tensor("out_0", (N, D), F32, kind="ExternalOutput").ap()
    gnn_program(nc, inp, out)
    r = _run(nc, [arrays], core_ids=[0])
    return r.results[0]["out_0"]
```
